# Optimizing a Trainium2 kernel written in Bass

```python
import numpy as np
import jax
import jax.numpy as jnp

def _softmax(x, axis=-1):
    return jax.nn.softmax(x, axis=axis)

def _gelu(x):
    return jax.nn.gelu(x, approximate=True)

def _silu(x):
    return jax.nn.silu(x)

def _sigmoid(x):
    return jax.nn.sigmoid(x)

def _layernorm(x, axis=-1, eps=1e-05):
    m = jnp.mean(x, axis=axis, keepdims=True)
    v = jnp.var(x, axis=axis, keepdims=True)
    return (x - m) / jnp.sqrt(v + eps)

def _scatter_add(tgt, idx, src, axis=0):
    return tgt.at[idx].add(src)

def _segment_sum(src, seg, n):
    return jax.ops.segment_sum(src, seg, n)
kernel_name = 'mk_gnn_resnorm_d4_gnn_r8_607a3d'

def setup_inputs(seed: int=0):
    np.random.seed(seed)
    _w = jnp.asarray

    def _rec_inputs():
        import jax
        import jax.numpy as jnp
        _gk = jax.random.key(seed)
        x = -0.000202 + 1 * jax.random.normal(jax.random.fold_in(_gk, 1), (6250, 128), jnp.float32)
        src = jax.random.randint(jax.random.fold_in(_gk, 2), (100000,), 0, 6250, jnp.int32)
        dst = jax.random.randint(jax.random.fold_in(_gk, 3), (100000,), 0, 6250, jnp.int32)
        _o = jnp.argsort(dst, stable=True)
        src = src[_o]
        dst = dst[_o]
        edge_attr_10 = 0.000254407 + 0.99978 * jax.random.normal(jax.random.fold_in(_gk, 12), (100000, 10), jnp.float32)
        edge_attr_3 = 0.000844983 + 0.999762 * jax.random.normal(jax.random.fold_in(_gk, 13), (100000, 3), jnp.float32)
        edge_weight1 = jax.random.uniform(jax.random.fold_in(_gk, 15), (100000, 1), jnp.float32, 0.0, 5.99999)
        return (x, src, dst, edge_attr_10, edge_attr_3, edge_weight1)
    x, src, dst, edge_attr_10, edge_attr_3, edge_weight1 = _rec_inputs()

    def _L0_gnn_setup():
        import jax, jax.numpy as jnp
        import numpy as np
        N_NODES = 6250
        N_EDGES = 100000
        NODE_DIM = 128
        EDGE_DIM = 10
        IN_DIM = 2 * NODE_DIM + EDGE_DIM
        BN_EPS = 1e-05
        key = jax.random.key(seed)
        ks = jax.random.split(key, 8)
        h = jax.random.normal(ks[0], (N_NODES, NODE_DIM), dtype=jnp.float32)
        edge_index = jax.random.randint(ks[1], (2, N_EDGES), 0, N_NODES, dtype=jnp.int64)
        edge_feat = jax.random.normal(ks[2], (N_EDGES, EDGE_DIM), dtype=jnp.float32)
        scale = 1.0 / np.sqrt(IN_DIM)
        gate_w = jax.random.normal(ks[3], (IN_DIM, NODE_DIM), dtype=jnp.float32) * scale
        gate_b = jax.random.normal(ks[4], (NODE_DIM,), dtype=jnp.float32) * scale
        cand_w = jax.random.normal(ks[5], (IN_DIM, NODE_DIM), dtype=jnp.float32) * scale
        cand_b = jax.random.normal(ks[6], (NODE_DIM,), dtype=jnp.float32) * scale
        bn_gamma = jnp.ones((NODE_DIM,), dtype=jnp.float32)
        bn_beta = jnp.zeros((NODE_DIM,), dtype=jnp.float32)
        return {'h': h, 'edge_index': edge_index, 'edge_feat': edge_feat, 'gate_w': gate_w, 'gate_b': gate_b, 'cand_w': cand_w, 'cand_b': cand_b, 'bn_gamma': bn_gamma, 'bn_beta': bn_beta}
    _L0_gnn_all = _L0_gnn_setup()
    _L0_gnn_in = {k: v for k, v in _L0_gnn_all.items() if k in ('gate_w', 'gate_b', 'cand_w', 'cand_b', 'bn_gamma', 'bn_beta')}
    del _L0_gnn_all

    def _L1_gnn_setup():
        import jax, jax.numpy as jnp
        import numpy as np
        N, E, DIM, H = (12500, 200000, 128, 8)
        HD = DIM // H
        key = jax.random.key(seed)
        ks = jax.random.split(key, 12)
        s = lambda k, sh, fan: jax.random.normal(k, sh, jnp.float32) * (1.0 / np.sqrt(fan))
        return {'x': jax.random.normal(ks[0], (N, DIM), jnp.float32), 'src': jax.random.randint(ks[1], (E,), 0, N, jnp.int32), 'dst': jax.random.randint(ks[2], (E,), 0, N, jnp.int32), 'w_in': s(ks[3], (DIM, DIM), DIM), 'b_in': jnp.zeros((DIM,), jnp.float32), 'w_au': s(ks[4], (DIM, H), DIM), 'b_au': jnp.zeros((H,), jnp.float32), 'w_av': s(ks[5], (DIM, H), DIM), 'w1': s(ks[6], (DIM, DIM), DIM), 'b1': jnp.zeros((DIM,), jnp.float32), 'w2': s(ks[7], (DIM, DIM), DIM), 'b2': jnpp if False else jnp.zeros((DIM,), jnp.float32)}
    _L1_gnn_all = _L1_gnn_setup()
    _L1_gnn_in = {k: v for k, v in _L1_gnn_all.items() if k in ('w_in', 'b_in', 'w_au', 'b_au', 'w_av', 'w1', 'b1', 'w2', 'b2')}
    del _L1_gnn_all

    def _L2_gnn_setup():
        import jax, jax.numpy as jnp
        import numpy as np
        N = 6250
        E = 75000
        D = 128
        L = 3
        key = jax.random.key(seed)
        ks = jax.random.split(key, 2 + 2 * L)
        x = jax.random.normal(ks[0], (N, D), dtype=jnp.float32)
        edge_index = jax.random.randint(ks[1], (2, E), 0, N, dtype=jnp.int32)
        s = float(np.sqrt(6.0 / (D + D)))
        inp = {'x': x, 'edge_index': edge_index}
        for i in range(L):
            inp[f'W{i}'] = jax.random.uniform(ks[2 + 2 * i], (D, D), jnp.float32, -s, s)
            inp[f'b{i}'] = jax.random.uniform(ks[3 + 2 * i], (D,), jnp.float32, -0.01, 0.01)
        return inp
    _L2_gnn_all = _L2_gnn_setup()
    _L2_gnn_in = {k: v for k, v in _L2_gnn_all.items() if k in ('W0', 'b0', 'W1', 'b1', 'W2', 'b2')}
    del _L2_gnn_all

    def _L3_gnn_setup():
        import jax, jax.numpy as jnp
        import numpy as np
        import math
        N = 5000
        E = 80000
        HID = 128
        H = 8
        HD = HID // H
        CUTOFF = 5.0
        LN_EPS = 1e-05

        def _linear_params(key, out_d, in_d):
            k1, k2 = jax.random.split(key)
            s = 1.0 / np.sqrt(in_d)
            W = jax.random.uniform(k1, (out_d, in_d), minval=-s, maxval=s, dtype=jnp.float32)
            b = jax.random.uniform(k2, (out_d,), minval=-s, maxval=s, dtype=jnp.float32)
            return (W, b)
        key = jax.random.key(seed)
        ks = jax.random.split(key, 12)
        x = jax.random.normal(ks[0], (N, HID), dtype=jnp.float32)
        edge_index = jax.random.randint(ks[1], (2, E), 0, N, dtype=jnp.int64)
        edge_vec = jax.random.normal(ks[2], (E, 3), dtype=jnp.float32)
        edge_length = jax.random.uniform(ks[3], (E, 1), dtype=jnp.float32) * 6.0
        Wq, bq = _linear_params(ks[4], HID, HID)
        Wk, bk = _linear_params(ks[5], HID, HID)
        Wv, bv = _linear_params(ks[6], HID, HID)
        We1, be1 = _linear_params(ks[7], HID, 1)
        We2, be2 = _linear_params(ks[8], H, HID)
        Wo, bo = _linear_params(ks[9], HID, HID)
        ln_g = jnp.ones((HID,), jnp.float32)
        ln_b = jnp.zeros((HID,), jnp.float32)
        return {'x': x, 'edge_vec': edge_vec, 'edge_length': edge_length, 'Wq': Wq, 'bq': bq, 'Wk': Wk, 'bk': bk, 'Wv': Wv, 'bv': bv, 'We1': We1, 'be1': be1, 'We2': We2, 'be2': be2, 'Wo': Wo, 'bo': bo, 'ln_g': ln_g, 'ln_b': ln_b, 'edge_index': edge_index}
    _L3_gnn_all = _L3_gnn_setup()
    _L3_gnn_in = {k: v for k, v in _L3_gnn_all.items() if k in ('Wq', 'bq', 'Wk', 'bk', 'Wv', 'bv', 'We1', 'be1', 'We2', 'be2', 'Wo', 'bo', 'ln_g', 'ln_b')}
    del _L3_gnn_all
    return {'x': x, 'src': src, 'dst': dst, 'edge_attr_10': edge_attr_10, 'edge_attr_3': edge_attr_3, 'edge_weight1': edge_weight1, 'L0_gnn_gate_w': _L0_gnn_in['gate_w'], 'L0_gnn_gate_b': _L0_gnn_in['gate_b'], 'L0_gnn_cand_w': _L0_gnn_in['cand_w'], 'L0_gnn_cand_b': _L0_gnn_in['cand_b'], 'L0_gnn_bn_gamma': _L0_gnn_in['bn_gamma'], 'L0_gnn_bn_beta': _L0_gnn_in['bn_beta'], 'L1_gnn_w_in': _L1_gnn_in['w_in'], 'L1_gnn_b_in': _L1_gnn_in['b_in'], 'L1_gnn_w_au': _L1_gnn_in['w_au'], 'L1_gnn_b_au': _L1_gnn_in['b_au'], 'L1_gnn_w_av': _L1_gnn_in['w_av'], 'L1_gnn_w1': _L1_gnn_in['w1'], 'L1_gnn_b1': _L1_gnn_in['b1'], 'L1_gnn_w2': _L1_gnn_in['w2'], 'L1_gnn_b2': _L1_gnn_in['b2'], 'L2_gnn_W0': _L2_gnn_in['W0'], 'L2_gnn_b0': _L2_gnn_in['b0'], 'L2_gnn_W1': _L2_gnn_in['W1'], 'L2_gnn_b1': _L2_gnn_in['b1'], 'L2_gnn_W2': _L2_gnn_in['W2'], 'L2_gnn_b2': _L2_gnn_in['b2'], 'L3_gnn_Wq': _L3_gnn_in['Wq'], 'L3_gnn_bq': _L3_gnn_in['bq'], 'L3_gnn_Wk': _L3_gnn_in['Wk'], 'L3_gnn_bk': _L3_gnn_in['bk'], 'L3_gnn_Wv': _L3_gnn_in['Wv'], 'L3_gnn_bv': _L3_gnn_in['bv'], 'L3_gnn_We1': _L3_gnn_in['We1'], 'L3_gnn_be1': _L3_gnn_in['be1'], 'L3_gnn_We2': _L3_gnn_in['We2'], 'L3_gnn_be2': _L3_gnn_in['be2'], 'L3_gnn_Wo': _L3_gnn_in['Wo'], 'L3_gnn_bo': _L3_gnn_in['bo'], 'L3_gnn_ln_g': _L3_gnn_in['ln_g'], 'L3_gnn_ln_b': _L3_gnn_in['ln_b']}

def reference(x, src, dst, edge_attr_10, edge_attr_3, edge_weight1, L0_gnn_gate_w, L0_gnn_gate_b, L0_gnn_cand_w, L0_gnn_cand_b, L0_gnn_bn_gamma, L0_gnn_bn_beta, L1_gnn_w_in, L1_gnn_b_in, L1_gnn_w_au, L1_gnn_b_au, L1_gnn_w_av, L1_gnn_w1, L1_gnn_b1, L1_gnn_w2, L1_gnn_b2, L2_gnn_W0, L2_gnn_b0, L2_gnn_W1, L2_gnn_b1, L2_gnn_W2, L2_gnn_b2, L3_gnn_Wq, L3_gnn_bq, L3_gnn_Wk, L3_gnn_bk, L3_gnn_Wv, L3_gnn_bv, L3_gnn_We1, L3_gnn_be1, L3_gnn_We2, L3_gnn_be2, L3_gnn_Wo, L3_gnn_bo, L3_gnn_ln_g, L3_gnn_ln_b):
    import jax
    import jax.numpy as jnp

    def _L0_gnn_ref(h, edge_index, edge_feat, gate_w, gate_b, cand_w, cand_b, bn_gamma, bn_beta):
        import jax, jax.numpy as jnp
        import numpy as np
        N_NODES = 6250
        N_EDGES = 100000
        NODE_DIM = 128
        EDGE_DIM = 10
        IN_DIM = 2 * NODE_DIM + EDGE_DIM
        BN_EPS = 1e-05
        src = edge_index[0]
        dst = edge_index[1]
        z = jnp.concatenate([h[src], h[dst], edge_feat], axis=1)
        g = jax.nn.sigmoid(z @ gate_w + gate_b)
        c = jax.nn.softplus(z @ cand_w + cand_b)
        m = g * c
        agg = jax.ops.segment_sum(m, src, num_segments=h.shape[0])
        mean = jnp.mean(agg, axis=0)
        var = jnp.var(agg, axis=0)
        agg_bn = (agg - mean) * jax.lax.rsqrt(var + BN_EPS) * bn_gamma + bn_beta
        return jax.nn.softplus(h + agg_bn)

    def _L1_gnn_ref(x, src, dst, w_in, b_in, w_au, b_au, w_av, w1, b1, w2, b2):
        import jax, jax.numpy as jnp
        import numpy as np
        N, E, DIM, H = (12500, 200000, 128, 8)
        HD = DIM // H
        n = x.shape[0]
        h = x @ w_in + b_in
        a_u = h @ w_au + b_au
        a_v = h @ w_av
        scores = jax.nn.leaky_relu(a_u[src] + a_v[dst], negative_slope=0.2)
        smax = jax.ops.segment_max(scores, dst, num_segments=n)
        ex = jnp.exp(scores - smax[dst])
        denom = jax.ops.segment_sum(ex, dst, num_segments=n)
        probs = ex / denom[dst]
        hv = h.reshape(n, HD, H)
        msg = hv[src] * probs[:, None, :]
        agg = jax.ops.segment_sum(msg, dst, num_segments=n)
        out = agg.reshape(n, DIM)
        out = jax.nn.gelu(out @ w1 + b1) @ w2 + b2
        return out

    def _L2_gnn_ref(x, edge_index, W0, b0, W1, b1, W2, b2):
        import jax, jax.numpy as jnp
        import numpy as np
        N = 6250
        E = 75000
        D = 128
        L = 3
        n = x.shape[0]
        loops = jnp.arange(n, dtype=edge_index.dtype)
        src = jnp.concatenate([edge_index[0], loops])
        dst = jnp.concatenate([edge_index[1], loops])
        deg = jax.ops.segment_sum(jnp.ones(src.shape, jnp.float32), dst, num_segments=n)
        dis = jnp.where(deg > 0, jax.lax.rsqrt(deg), 0.0)
        norm = dis[src] * dis[dst]

        def gcn_layer(h, W, b):
            h = h @ W
            msg = h[src] * norm[:, None]
            out = jax.ops.segment_sum(msg, dst, num_segments=n)
            return out + b
        h = gcn_layer(x, W0, b0)
        h = jax.nn.relu(h)
        h = gcn_layer(h, W1, b1)
        h = jax.nn.relu(h)
        h = gcn_layer(h, W2, b2)
        return h

    def _L3_gnn_ref(x, edge_vec, edge_length, Wq, bq, Wk, bk, Wv, bv, We1, be1, We2, be2, Wo, bo, ln_g, ln_b, edge_index):
        import jax, jax.numpy as jnp
        import numpy as np
        import math
        N = 5000
        E = 80000
        HID = 128
        H = 8
        HD = HID // H
        CUTOFF = 5.0
        LN_EPS = 1e-05

        def _linear_params(key, out_d, in_d):
            k1, k2 = jax.random.split(key)
            s = 1.0 / np.sqrt(in_d)
            W = jax.random.uniform(k1, (out_d, in_d), minval=-s, maxval=s, dtype=jnp.float32)
            b = jax.random.uniform(k2, (out_d,), minval=-s, maxval=s, dtype=jnp.float32)
            return (W, b)
        row, col = (edge_index[0], edge_index[1])
        n = x.shape[0]
        q = (x @ Wq.T + bq).reshape(n, H, HD)
        k = (x @ Wk.T + bk).reshape(n, H, HD)
        v = (x @ Wv.T + bv).reshape(n, H, HD)
        attn = jnp.einsum('ehd,ehd->eh', q[row], k[col]) / math.sqrt(HD)
        edge_bias = jax.nn.silu(edge_length @ We1.T + be1) @ We2.T + be2
        attn = attn + edge_bias
        cut = 0.5 * (jnp.cos(edge_length * math.pi / CUTOFF) + 1.0)
        cut = cut * (edge_length < CUTOFF).astype(jnp.float32)
        attn = attn * cut
        attn_exp = jnp.exp(attn - jnp.max(attn, axis=0, keepdims=True))
        attn_sum = jax.ops.segment_sum(attn_exp, row, num_segments=n)
        attn = attn_exp / (attn_sum[row] + 1e-08)
        out = jax.ops.segment_sum(attn[:, :, None] * v[col], row, num_segments=n)
        out = out.reshape(n, HID) @ Wo.T + bo
        h = x + out
        mu = jnp.mean(h, axis=-1, keepdims=True)
        var = jnp.mean(jnp.square(h - mu), axis=-1, keepdims=True)
        return (h - mu) / jnp.sqrt(var + LN_EPS) * ln_g + ln_b
    edge_index = jnp.stack([src, dst])
    x = _layernorm(x + _L0_gnn_ref(x, edge_index, edge_attr_10, L0_gnn_gate_w, L0_gnn_gate_b, L0_gnn_cand_w, L0_gnn_cand_b, L0_gnn_bn_gamma, L0_gnn_bn_beta), axis=-1)
    x = _layernorm(x + _L1_gnn_ref(x, src, dst, L1_gnn_w_in, L1_gnn_b_in, L1_gnn_w_au, L1_gnn_b_au, L1_gnn_w_av, L1_gnn_w1, L1_gnn_b1, L1_gnn_w2, L1_gnn_b2), axis=-1)
    x = _layernorm(x + _L2_gnn_ref(x, edge_index, L2_gnn_W0, L2_gnn_b0, L2_gnn_W1, L2_gnn_b1, L2_gnn_W2, L2_gnn_b2), axis=-1)
    x = _layernorm(x + _L3_gnn_ref(x, edge_attr_3, edge_weight1, L3_gnn_Wq, L3_gnn_bq, L3_gnn_Wk, L3_gnn_bk, L3_gnn_Wv, L3_gnn_bv, L3_gnn_We1, L3_gnn_be1, L3_gnn_We2, L3_gnn_be2, L3_gnn_Wo, L3_gnn_bo, L3_gnn_ln_g, L3_gnn_ln_b, edge_index), axis=-1)
    return x

_drawn_inputs = setup_inputs


def setup_inputs(seed=0):
    import zlib

    import numpy as np

    out = dict(_drawn_inputs(seed))
    spreads = {'L0_gnn_bn_gamma': (1.0, 0.2),
     'L0_gnn_bn_beta': (0.0, 0.1),
     'L1_gnn_b_in': (0.0, 0.1),
     'L1_gnn_b_au': (0.0, 2.0),
     'L1_gnn_b1': (0.0, 0.1),
     'L1_gnn_b2': (0.0, 0.1),
     'L3_gnn_ln_g': (1.0, 0.2),
     'L3_gnn_ln_b': (0.0, 0.1)}
    factors = {'edge_weight1': 44.855,
     'L0_gnn_gate_b': 8.0,
     'L0_gnn_cand_b': 8.0,
     'L2_gnn_b0': 28.928,
     'L2_gnn_b1': 8.0,
     'L2_gnn_b2': 8.0,
     'L3_gnn_Wq': 39.27,
     'L3_gnn_bq': 64.0,
     'L3_gnn_Wk': 37.744,
     'L3_gnn_bk': 64.0,
     'L3_gnn_bv': 31.392,
     'L3_gnn_We1': 64.0,
     'L3_gnn_be1': 55.882,
     'L3_gnn_We2': 64.0,
     'L3_gnn_be2': 64.0,
     'L3_gnn_Wv': 5.44,
     'L3_gnn_Wo': 5.108}
    for name, (base, spread) in spreads.items():
        noise = np.random.default_rng([zlib.crc32(name.encode()), seed]).standard_normal(out[name].shape)
        drawn = base * np.exp(spread * noise) if base else spread * noise
        out[name] = jnp.asarray(drawn.astype(out[name].dtype))
    for name, factor in factors.items():
        out[name] = (out[name] * factor).astype(out[name].dtype)
    return out
```

```python
from contextlib import ExitStack

import numpy as np

import concourse.bass as bass
from concourse import mybir

F32 = mybir.dt.float32
I32 = mybir.dt.int32
ALU = mybir.AluOpType
ACT = mybir.ActivationFunctionType
AX = mybir.AxisListType

P = 128
N = 6250
E = 100000
D = 128
H = 8
HD = D // H
EF = 10
B = -(-N // P)
NP = B * P
LAST = N - (B - 1) * P
COLS = -(-E // P)
C = 4
LANES = 4
T = COLS + B
T = -(-T // (C * LANES)) * C * LANES
NCH = T // C
ITERS = NCH // LANES
REC_S = 2 + EF + 1
REC_D = 2
G = 7
NG = B // G
SG = 17
NSG = COLS // SG
BIG = 1.0e30
CUTOFF = 5.0
assert B % G == 0 and COLS % SG == 0 and NSG % 2 == 0 and NCH % LANES == 0

W_COLS, V_COLS = {}, {}


def _place(table, items):
    at = 0
    for name, n in items:
        table[name] = (at, at + n)
        at += n
    return at


NW = _place(W_COLS, [("own0", 256), ("other0", 256), ("in1", D), ("a1", 2 * H), ("mlp1", D), ("mlp2", D),
                     ("g0", D), ("g1", D), ("g2", D), ("q3", D), ("kv3", 2 * D), ("bias3", H), ("o3", D),
                     ("hid_b", 1)])
NV = _place(V_COLS, [("b0", 256), ("b_in1", D), ("b_a1", 2 * H), ("b_mlp1", D), ("b_mlp2", D), ("b_g0", D),
                     ("b_g1", D), ("b_g2", D), ("b_q3", D), ("b_kv3", 2 * D), ("b_bias3", H), ("b_o3", D),
                     ("bn_g", D), ("bn_b", D), ("ln_g", D), ("ln_b", D)])


def over0(v):
    return not isinstance(v, int) or v > 0


def ctx_tools(nc, ctx):
    def sb(name, shape, dt=F32):
        return ctx.enter_context(nc.sbuf_tensor(name, shape, dt))

    def ps(name, shape):
        return ctx.enter_context(nc.psum_tensor(name, shape, F32))

    return sb, ps


def bc_mid(ap, n):
    return ap.unsqueeze(1).to_broadcast([ap.shape[0], n, ap.shape[1]])


def bc_last(ap, n):
    return ap.unsqueeze(len(ap.shape)).to_broadcast([*ap.shape, n])


def chunk_loop(eng, body, peel=2):
    for it in range(peel):
        body(it)
    with eng.Fori(peel, ITERS) as it:
        body(it)
    for it in range(ITERS, ITERS + 2):
        body(it)


def at_stage(it, lane, lag):
    if isinstance(it, int):
        c = LANES * it + lane - lag
        return (c, c % LANES) if 0 <= c < NCH else None
    return it * LANES + (lane - lag), (lane - lag) % LANES


class Sems:

    MOST = 150

    def __init__(self, nc, used, stage):
        if len(used) > self.MOST:
            nc.clear_and_free_semaphores(used)
            nc.all_engine_barrier()
            used.clear()
        self.nc, self.used, self.stage = nc, used, stage

    def __call__(self, *names):
        sems = [self.nc.alloc_semaphore(f"{self.stage}_{n}") for n in names]
        self.used.extend(sems)
        return sems



def load_and_sort(nc, K, io):
    ctx = ExitStack()
    with ctx:
        sb, ps = ctx_tools(nc, ctx)
        key = {"s": sb("src_i", [P, COLS], I32), "d": sb("dst_i", [P, COLS], I32)}
        whole = {"s": sb("src_f", [P, COLS]), "d": sb("dst_f", [P, COLS])}
        local = {"s": sb("src_local", [P, COLS]), "d": sb("dst_local", [P, COLS])}
        pos = {"s": sb("src_pos", [P, COLS]), "d": sb("dst_pos", [P, COLS])}
        pos_i = {"s": sb("src_pos_i", [P, COLS], I32), "d": sb("dst_pos_i", [P, COLS], I32)}
        blk = sb("blk", [P, COLS])
        mask = sb("mask", [P, COLS])
        rank = sb("rank", [P, COLS])
        feats = sb("feats", [P, COLS, EF])
        length = sb("length", [P, COLS])
        cnt = sb("cnt", [P, B])
        few = sb("few", [P, 6, B])
        few_i = sb("few_i", [P, B], I32)
        tile_no = sb("tile_no", [P, G])
        past = sb("past", [P, G, B - 1])
        tb_f = sb("tb_f", [P, G])
        tb_i = {"s": sb("tb_s", [P, G], I32), "d": sb("tb_d", [P, G], I32)}
        pad = sb("pad", [P, 104, REC_S])
        pad_d = sb("pad_d", [P, 104, REC_D])
        stage_s = sb("stage_s", [P, 2, SG, REC_S])
        stage_d = sb("stage_d", [P, 2, SG, REC_D])
        stage_i = {"s": sb("stage_si", [P, 2, SG], I32), "d": sb("stage_di", [P, 2, SG], I32)}
        p_cnt = {"s": ps("p_cnt_s", [P, 2, 64]), "d": ps("p_cnt_d", [P, 2, 64])}
        new = Sems(nc, K.used_sems, "sort")
        loaded, consts, chain, counted, summed = new("loaded", "consts", "chain", "counted", "summed")
        pads_set, pads_out, map_ready, map_out = new("pads_set", "pads_out", "map_ready", "map_out")
        pos_ready, gate, maps_in = new("pos_ready", "gate", "maps_in")
        staged = {k: new(f"staged_{k}0", f"staged_{k}1") for k in "sd"}
        sent = {k: new(f"sent_{k}0", f"sent_{k}1") for k in "sd"}
        n_loads = 8
        recs = {"s": K.rec_s, "d": K.rec_d}
        block = ctx.enter_context(nc.Block())

        @block.sync
        def _(sp):
            sp.dma_start(key["s"][:], io["src"]).then_inc(loaded, 16)
            sp.dma_start(key["d"][:], io["dst"]).then_inc(loaded, 16)
            sp.dma_start(feats[:].rearrange("p a b -> p (a b)"), io["ef"]).then_inc(loaded, 16)
            sp.dma_start(length[:], io["length"]).then_inc(loaded, 16)
            sp.dma_start(K.W[:], io["weights"]).then_inc(loaded, 16)
            sp.dma_start(K.V[:], io["vectors"]).then_inc(loaded, 16)
            sp.dma_start(K.w_ef[:], io["w_ef"]).then_inc(loaded, 16)
            sp.dma_start(K.w_len[:], io["w_len"]).then_inc(loaded, 16)
            sp.wait_ge(pads_set, 3)
            for k, src in (("s", pad), ("d", pad_d)):
                words = recs[k].shape[1]
                rows = recs[k].rearrange("(a p n) w -> a p (n w)", p=P, n=104)
                for a in range(T // 104):
                    sp.dma_start(rows[a], src[:].rearrange("p n w -> p (n w)")).then_inc(pads_out, 16)
            for n, k in enumerate("sd"):
                sp.wait_ge(map_ready, n + 1)
                sp.dma_start(K.map_dram[k].rearrange("(p n) -> p n", p=P), tb_i[k][:]).then_inc(map_out, 16)
                sp.wait_ge(map_out, 16 * (n + 1))
                sp.dma_start(K.blocks[k][0:1, :], K.map_dram[k][0:T].unsqueeze(0)).then_inc(maps_in, 16)
            sp.wait_ge(maps_in, 32)

        @block.gpsimd
        def _(pool):
            pool.iota(K.lane_i[:], pattern=[[1, P]], base=0, channel_multiplier=0).then_inc(consts, 1)
            pool.iota(K.tile_i[:], pattern=[[1, G]], base=0, channel_multiplier=G).then_inc(consts, 1)
            pool.memset(K.ident[:], 0.0).then_inc(consts, 1)
            pool.memset(K.ones[:], 1.0).then_inc(consts, 1)
            pool.memset(pad[:].rearrange("p n w -> p (n w)"), 0.0).then_inc(pads_set, 1)
            pool.memset(pad_d[:].rearrange("p n w -> p (n w)"), 0.0).then_inc(pads_set, 1)
            pool.wait_ge(consts, 4)
            pool.affine_select(out=K.ident[:], in_=K.ident[:], compare_op=ALU.not_equal, fill=1.0, base=0,
                               pattern=[[-1, P]], channel_multiplier=1).then_inc(consts, 1)
            pool.affine_select(out=K.before[:], in_=K.ones[:], compare_op=ALU.is_gt, fill=0.0, base=0,
                               pattern=[[1, P]], channel_multiplier=-1).then_inc(consts, 1)
            pool.wait_ge(pads_out, 2 * 16 * (T // 104))
            stage = {"s": stage_s, "d": stage_d}
            for k in "sd":
                def scatter(it, k=k):
                    for half in range(2):
                        pool.wait_ge(staged[k][half], 1 * (it + 1))
                        pool.sem_inc(gate, 1)
                        for j in range(SG):
                            pool.indirect_dma_start(
                                recs[k], bass.IndirectOffsetOnAxis(ap=stage_i[k][:, half, j:j + 1], axis=0),
                                stage[k][:, half, j, :], None,
                                bounds_check=T * P - 1, oob_is_err=False).then_inc(sent[k][half], 16)

                scatter(0)
                with pool.Fori(1, NSG // 2) as it:
                    scatter(it)
                for half in range(2):
                    pool.wait_ge(sent[k][half], 16 * SG * (NSG // 2))

        @block.scalar
        def _(act):
            act.wait_ge(loaded, 16 * n_loads)
            for n, k in enumerate("sd"):
                act.wait_ge(pos_ready, n + 1)
                other = whole["d" if k == "s" else "s"]

                def fill(it, k=k, other=other):
                    for half in range(2):
                        cols = bass.ds((it * 2 + half) * SG, SG)
                        if over0(it):
                            act.wait_ge(sent[k][half], 16 * SG * it)
                        dst = stage_s if k == "s" else stage_d
                        nc.scalar.activation(stage_i[k][:, half, :], pos_i[k][:, cols], ACT.Copy)
                        nc.scalar.activation(dst[:, half, :, 0], local[k][:, cols], ACT.Copy)
                        last = nc.scalar.activation(dst[:, half, :, 1], other[:, cols], ACT.Copy)
                        if k == "s":
                            nc.scalar.activation(dst[:, half, :, 2:2 + EF], feats[:, cols, :], ACT.Copy)
                            last = nc.scalar.activation(dst[:, half, :, 2 + EF], length[:, cols], ACT.Copy)
                        last.then_inc(staged[k][half], 1)

                fill(0)
                with act.Fori(1, NSG // 2) as it:
                    fill(it)

        @block.tensor
        def _(pe):
            pe.wait_ge(consts, 6)
            for n, k in enumerate("sd"):
                pe.wait_ge(counted, n + 1)
                pe.matmul(p_cnt[k][:, 0, 0:B], K.ones[:], cnt[:], start=True, stop=True)
                pe.matmul(p_cnt[k][:, 1, 0:B], K.before[:], cnt[:], start=True, stop=True).then_inc(summed, 1)

        @block.vector
        def _(dve):
            count = [0]

            def link(ins):
                count[0] += 1
                ins.then_inc(chain, 1)
                dve.wait_ge(chain, count[0])

            dve.wait_ge(pads_set, 2)
            dve.memset(pad[:, :, 0], -1.0)
            dve.memset(pad_d[:, :, 0], -1.0).then_inc(pads_set, 1)
            dve.wait_ge(consts, 2)
            dve.tensor_copy(K.lane[:], K.lane_i[:])
            link(dve.tensor_copy(tile_no[:], K.tile_i[:]))
            dve.wait_ge(loaded, 16 * n_loads)
            total, nt_end, nt, base, tend, junk = (few[:, i, :] for i in range(6))
            for n, k in enumerate("sd"):
                link(dve.tensor_copy(whole[k][:], key[k][:]))
                link(dve.tensor_scalar(key[k][:], key[k][:], 7, None, ALU.arith_shift_right))
                link(dve.tensor_copy(blk[:], key[k][:]))
                link(dve.scalar_tensor_tensor(out=local[k][:], in0=blk[:], scalar=-float(P), in1=whole[k][:],
                                              op0=ALU.mult, op1=ALU.add))
            for n, k in enumerate("sd"):
                if n == 1:
                    dve.wait_ge(summed, 1)
                link(dve.tensor_copy(blk[:], key[k][:]))
                with dve.Fori(0, B) as b:
                    dve.tensor_scalar(mask[:], blk[:], K.lane[:, bass.ds(b, 1)], None, ALU.is_equal, ALU.add,
                                      accum_out=cnt[:, bass.ds(b, 1)])
                    dve.drain()
                dve.drain().then_inc(counted, 1)
                dve.wait_ge(summed, n + 1)
                link(dve.tensor_copy(total, p_cnt[k][:, 0, 0:B]))
                link(dve.tensor_scalar(few_i[:], total, float(P - 1), None, ALU.add))
                link(dve.tensor_scalar(few_i[:], few_i[:], 7, None, ALU.arith_shift_right))
                link(dve.tensor_copy(nt, few_i[:]))
                link(dve.tensor_tensor_scan(tend, nt, nt, 0.0, ALU.add, ALU.max))
                link(dve.tensor_tensor(nt_end, tend, nt, ALU.subtract))
                link(dve.scalar_tensor_tensor(out=base, in0=nt_end, scalar=float(P), in1=p_cnt[k][:, 1, 0:B],
                                              op0=ALU.mult, op1=ALU.add))
                link(dve.tensor_tensor(past[:], bc_last(tile_no[:], B - 1), bc_mid(tend[:, 0:B - 1], G), ALU.is_ge))
                link(dve.tensor_reduce(tb_f[:], past[:], AX.X, ALU.add))
                link(dve.tensor_copy(tb_i[k][:], tb_f[:]))
                dve.sem_inc(map_ready, 1)
                link(dve.memset(pos[k][:], float(1 << 22)))
                with dve.Fori(0, B) as b:
                    dve.tensor_scalar(mask[:], blk[:], K.lane[:, bass.ds(b, 1)], None, ALU.is_equal)
                    dve.drain()
                    dve.tensor_tensor_scan(rank[:], mask[:], mask[:], base[:, bass.ds(b, 1)], ALU.add, ALU.max)
                    dve.drain()
                    dve.copy_predicated(pos[k][:], mask[:].bitcast(I32), rank[:])
                    dve.drain()
                link(dve.tensor_scalar(pos_i[k][:], pos[k][:], -1.0, None, ALU.add))
                dve.sem_inc(pos_ready, 1)


def load_orders(nc, K):
    ctx = ExitStack()
    with ctx:
        sb, ps = ctx_tools(nc, ctx)
        groups = [(g * P, min(P, T - g * P)) for g in range(-(-T // P))]
        jobs = [("s", g) for g in range(len(groups))] + [("d", g) for g in range(len(groups))]
        rows = sb("rows", [P, 2, P * REC_S])
        turned = ps("turned", [P, 2, 4, P])
        new = Sems(nc, K.used_sems, "orders")
        row_in = new("row_in0", "row_in1")
        turned_in, copied = new("turned", "copied")
        block = ctx.enter_context(nc.Block())

        @block.sync
        def _(sp):
            for n, (k, g) in enumerate(jobs):
                t0, nt = groups[g]
                words = REC_S if k == "s" else REC_D
                rec = K.rec_s if k == "s" else K.rec_d
                if n >= 2:
                    sp.wait_ge(turned_in, n - 1)
                sp.dma_start(rows[0:nt, n % 2, 0:P * words],
                             rec[t0 * P:(t0 + nt) * P, :].rearrange("(t e) w -> t (e w)", e=P)).then_inc(row_in[n % 2], 16)

        @block.tensor
        def _(pe):
            for n, (k, g) in enumerate(jobs):
                t0, nt = groups[g]
                words = REC_S if k == "s" else REC_D
                pe.wait_ge(row_in[n % 2], 16 * (n // 2 + 1))
                if n >= 2:
                    pe.wait_ge(copied, n - 1)
                v = rows[0:nt, n % 2, 0:P * words].rearrange("t (e w) -> t w e", w=words)
                for i, w in enumerate([0, 1, REC_S - 1][:3 if k == "s" else 2]):
                    mm = pe.transpose(turned[:, n % 2, i, 0:nt], v[:, w, :], K.ident[0:nt, 0:nt])
                mm.then_inc(turned_in, 1)

        @block.vector
        def _(dve):
            for n, (k, g) in enumerate(jobs):
                t0, nt = groups[g]
                dve.wait_ge(turned_in, n + 1)
                dve.tensor_copy(K.key[k][:, t0:t0 + nt], turned[:, n % 2, 0, 0:nt])
                last = dve.tensor_copy(K.other[k][:, t0:t0 + nt], turned[:, n % 2, 1, 0:nt])
                if k == "s":
                    last = dve.tensor_copy(K.length[:, t0:t0 + nt], turned[:, n % 2, 2, 0:nt])
                last.then_inc(copied, 1)



def node_pass(nc, K, stage, nodes, outs, clear=None):
    ctx = ExitStack()
    with ctx:
        sb, ps = ctx_tools(nc, ctx)
        group = sb(f"{stage}_group", [P, G, D])
        turned = sb(f"{stage}_turned", [P, G, P])
        result = sb(f"{stage}_result", [P, G, max(o[1] for o in outs)])
        p_turn = ps(f"{stage}_p_turn", [P, 2, 4, P])
        p_out = ps(f"{stage}_p_out", [P, 4, 512])
        new = Sems(nc, K.used_sems, stage)
        picked, turns, turned_in, product, taken, stored = new(
            "picked", "turns", "turned_in", "product", "taken", "stored")
        n_out = len(outs)
        drams = [i for i, o in enumerate(outs) if isinstance(o[3], tuple)]
        slot = {128: 128, 256: 256}
        block = ctx.enter_context(nc.Block())

        def product_of(n, i):
            per = 512 // n if n >= 128 else 4
            return p_out[:, i // per, (i % per) * n:(i % per) * n + n]

        @block.scalar
        def _(act):
            def body(it):
                if over0(it):
                    act.wait_ge(turns, it)
                nc.scalar.activation(group[:], nodes[:, bass.ds(it * G, G), :], ACT.Copy).then_inc(picked, 1)
                act.wait_ge(turns, it + 1)
                if over0(it):
                    act.wait_ge(product, it * n_out)
                nc.scalar.activation(turned[:, 0:4, :], p_turn[:, 0, :, :], ACT.Copy)
                nc.scalar.activation(turned[:, 4:G, :], p_turn[:, 1, 0:G - 4, :], ACT.Copy).then_inc(turned_in, 1)

            body(0)
            with act.Fori(1, NG) as it:
                body(it)

        @block.tensor
        def _(pe):
            def body(it):
                pe.wait_ge(picked, it + 1)
                if over0(it):
                    pe.wait_ge(turned_in, it)
                for i in range(G):
                    mm = pe.transpose(p_turn[:, i // 4, i % 4, :], group[:, i, :], K.ident[:])
                mm.then_inc(turns, 1)
                pe.wait_ge(turned_in, it + 1)
                for o, (w, n, _, _) in enumerate(outs):
                    if over0(it * n_out + o):
                        pe.wait_ge(taken, it * n_out + o)
                    for i in range(G):
                        mm = pe.matmul(product_of(n, i), turned[:, i, :], w, start=True, stop=True)
                    mm.then_inc(product, 1)

            body(0)
            with pe.Fori(1, NG) as it:
                body(it)

        @block.gpsimd
        def _(pool):
            if clear is not None:
                pool.memset(clear[:], 0.0)

        @block.vector
        def _(dve):
            def body(it):
                for o, (_, n, bias, target) in enumerate(outs):
                    dve.wait_ge(product, it * n_out + o + 1)
                    if o in drams:
                        before = it * len(drams) + drams.index(o)
                        if over0(before):
                            dve.wait_ge(stored, before * 16)
                    per = 512 // n if n >= 128 else 4
                    for a in range(0, G, per):
                        m = min(per, G - a)
                        p = p_out[:, a // per, 0:m * n].rearrange("p (m n) -> p m n", n=n)
                        dst = result[:, a:a + m, 0:n] if o in drams else target[:, bass.ds(it * G + a, m), 0:n]
                        if bias is None:
                            last = dve.tensor_copy(dst, p)
                        else:
                            last = dve.tensor_tensor(dst, p, bc_mid(bias, m), ALU.add)
                    last.then_inc(taken, 1)

            body(0)
            with dve.Fori(1, NG) as it:
                body(it)

        @block.sync
        def _(sp):
            def body(it):
                for o in drams:
                    table, col, width = outs[o][3]
                    sp.wait_ge(taken, it * n_out + o + 1)
                    rows = table.rearrange("(b n) f -> n b f", n=P)
                    sp.dma_start(rows[:, bass.ds(it * G, G), col:col + width], result[:, :, 0:width]).then_inc(stored, 16)

            if drams:
                body(0)
                with sp.Fori(1, NG) as it:
                    body(it)
                sp.wait_ge(stored, 16 * NG * len(drams))


def on_vector(nc, K, stage, program):
    with ExitStack() as ctx:
        new = Sems(nc, K.used_sems, stage)
        chain, asked, answered = new("chain", "asked", "answered")
        block = ctx.enter_context(nc.Block())
        todo = []

        @block.vector
        def _(dve):
            count = [0]

            def link(ins):
                count[0] += 1
                ins.then_inc(chain, 1)
                dve.wait_ge(chain, count[0])

            def scalar_step(out, in_, func, **kw):
                todo.append((out, in_, func, kw))
                dve.sem_inc(asked, 1)
                dve.wait_ge(answered, len(todo))

            program(dve, link, scalar_step)

        @block.scalar
        def _(act):
            for n, (out, in_, func, kw) in enumerate(todo):
                act.wait_ge(asked, n + 1)
                nc.scalar.activation(out, in_, func, **kw).then_inc(answered, 1)


def layer_norm(dve, link, scalar_step, K, t, tmp, scale=None, shift=None):
    mean, var = K.stat[:, 0, :], K.stat[:, 1, :]
    link(dve.tensor_reduce(mean, t, AX.X, ALU.add))
    link(dve.tensor_scalar(mean, mean, 1.0 / D, None, ALU.mult))
    link(dve.tensor_tensor(t, t, bc_last(mean, D), ALU.subtract))
    link(dve.tensor_tensor(tmp, t, t, ALU.mult))
    link(dve.tensor_reduce(var, tmp, AX.X, ALU.add))
    link(dve.tensor_scalar(var, var, 1.0 / D, 1e-5, ALU.mult, ALU.add))
    scalar_step(mean, var, ACT.Sqrt)
    link(dve.reciprocal(var, mean))
    link(dve.tensor_tensor(t, t, bc_last(var, D), ALU.mult))
    if scale is not None:
        link(dve.tensor_tensor(t, t, bc_mid(scale, B), ALU.mult))
        link(dve.tensor_tensor(t, t, bc_mid(shift, B), ALU.add))



class Edges:

    def __init__(self, nc, K, k):
        self.nc, self.K, self.k = nc, K, k

    def pick_others(self, act, out, c):
        return self.nc.scalar.activation(out, self.K.other[self.k][:, bass.ds(c * C, C)], ACT.Copy)

    def one_hot(self, dve, out, c):
        keys = self.K.key[self.k][:, bass.ds(c * C, C)]
        return dve.tensor_tensor(out, bc_mid(self.K.lane[:], C), bc_last(keys, P), ALU.is_equal)

    def block_values(self, eng, regs, c):
        eng.load(regs, self.K.blocks[self.k][0:1, bass.ds(c * C, C)])
        return [eng.snap(r, min_val=0, max_val=B - 1) for r in regs]

def load_x(nc, K, io, x):
    [came] = Sems(nc, K.used_sems, "x")("came")
    with nc.Block() as block:
        @block.sync
        def _(sp):
            sp.dma_start(x[:].rearrange("p b d -> p (b d)"), io["x"]).then_inc(came, 16)
            sp.wait_ge(came, 16)


def edge_pass0(nc, K, own, agg):
    ctx = ExitStack()
    with ctx:
        sb, ps = ctx_tools(nc, ctx)
        ed = Edges(nc, K, "s")
        idx = sb("e0_idx", [P, LANES, C], I32)
        far = sb("e0_far", [P, LANES, C, 2 * D])
        rec = sb("e0_rec", [P, LANES, C * REC_S])
        S = sb("e0_S", [P, 4, C, P])
        ST = sb("e0_ST", [P, 2, C * P])
        FT = sb("e0_FT", [C * REC_S, 2, P])
        z = sb("e0_z", [P, 2, C, 2 * D])
        soft = sb("e0_soft", [P, 2, C, 2 * D])
        low = sb("e0_low", [P, 2, C, D])
        high = sb("e0_high", [P, 2, C, D])
        msg = sb("e0_msg", [P, 2, C, D])
        p_turn = ps("e0_p_turn", [P, C * P])
        p_feat = ps("e0_p_feat", [C * REC_S, P])
        p_z = ps("e0_p_z", [P, 2, C, 2 * D])
        p_agg = ps("e0_p_agg", [P, 2, C, D])
        new = Sems(nc, K.used_sems, "e0")
        picked, gate = new("picked", "gate")
        recs_in = new("rec_in0", "rec_in1", "rec_in2", "rec_in3")
        far_in = new("far_in0", "far_in1", "far_in2", "far_in3")
        hot, turned, kept, z_done, z_read, abs_done, exp_done, ln_done = new(
            "hot", "turned", "kept", "z_done", "z_read", "abs_done", "exp_done", "ln_done")
        halves, sig_done, msg_done, summed, added = new("halves", "sig_done", "msg_done", "summed", "added")
        block = ctx.enter_context(nc.Block())

        @block.gpsimd
        def _(pool):
            def body(it):
                for lane in range(LANES):
                    if (at := at_stage(it, lane, 0)) is not None:
                        c, l = at
                        pool.wait_ge(picked, c + 1)
                        if over0(c - LANES + 1):
                            pool.wait_ge(z_read, c - LANES + 1)
                        pool.sem_inc(gate, 1)
                        for i in range(C):
                            pool.indirect_dma_start(far[:, l, i, :], None, K.table0,
                                                    bass.IndirectOffsetOnAxis(ap=idx[:, l, i:i + 1], axis=0)
                                                    ).then_inc(far_in[l], 16)

            chunk_loop(pool, body)

        @block.sync
        def _(sp):
            chunks = K.rec_s.rearrange("(c t e) w -> e c t w", t=C, e=P)

            def body(it):
                for lane in range(LANES):
                    if (at := at_stage(it, lane, 0)) is not None:
                        c, l = at
                        if over0(c - LANES + 1):
                            sp.wait_ge(turned, c - LANES + 1)
                        sp.dma_start(rec[:, l, :].rearrange("p (o t w) -> p o t w", o=1, t=C),
                                     chunks[:, bass.ds(c, 1), :, :]).then_inc(recs_in[l], 16)

            chunk_loop(sp, body)

        @block.scalar
        def _(act):
            def body(it):
                for lane in range(LANES):
                    if (at := at_stage(it, lane, 0)) is not None:
                        c, l = at
                        if over0(c - LANES + 1):
                            act.wait_ge(far_in[l], 64 * (lane_turn(it, lane, 0) - 1))
                        ed.pick_others(act, idx[:, l, :], c).then_inc(picked, 1)
                    if (at := at_stage(it, lane, 2)) is not None:
                        c, l = at
                        act.wait_ge(turned, c + 1)
                        if over0(c - 1):
                            act.wait_ge(z_done, c - 1)
                        nc.scalar.activation(FT[:, l % 2, :], p_feat[:], ACT.Copy)
                        nc.scalar.activation(ST[:, l % 2, :], p_turn[:], ACT.Copy).then_inc(kept, 1)
                    if (at := at_stage(it, lane, 4)) is not None:
                        c, l = at
                        act.wait_ge(halves, c + 1)
                        nc.scalar.activation(low[:, l % 2], low[:, l % 2], ACT.Exp).then_inc(sig_done, 1)
                    if (at := at_stage(it, lane, 3)) is not None:
                        c, l = at
                        act.wait_ge(z_read, c + 1)
                        nc.scalar.activation(soft[:, l % 2], z[:, l % 2], ACT.Abs).then_inc(abs_done, 1)
                        act.wait_ge(abs_done, c + 1)
                        nc.scalar.activation(soft[:, l % 2], soft[:, l % 2], ACT.Exp, scale=-1.0).then_inc(exp_done, 1)
                        act.wait_ge(exp_done, c + 1)
                        nc.scalar.activation(soft[:, l % 2], soft[:, l % 2], ACT.Ln, bias=1.0).then_inc(ln_done, 1)

            chunk_loop(act, body)

        @block.tensor
        def _(pe):
            regs = [pe.alloc_register(f"e0_pe{i}") for i in range(C)]

            def body(it):
                for lane in range(LANES):
                    if (at := at_stage(it, lane, 2)) is not None:
                        c, l = at
                        pe.wait_ge(hot, c + 1)
                        pe.wait_ge(recs_in[l], 16 * lane_turn(it, lane, 2))
                        if over0(c):
                            pe.wait_ge(kept, c)
                        for i in range(C):
                            pe.transpose(p_turn[:, i * P:(i + 1) * P], S[:, l, i, :], K.ident[:])
                        pe.transpose(p_feat[:], rec[:, l, :], K.ident[:]).then_inc(turned, 1)
                    if (at := at_stage(it, lane, 3)) is not None:
                        c, l = at
                        blocks = ed.block_values(pe, regs, c)
                        pe.wait_ge(kept, c + 1)
                        if over0(c - 1):
                            pe.wait_ge(z_read, c - 1)
                        for i in range(C):
                            pe.matmul(p_z[:, l % 2, i, :], ST[:, l % 2, i * P:(i + 1) * P],
                                      own[:, bass.ds(blocks[i], 1), :], start=True, stop=False)
                            mm = pe.matmul(p_z[:, l % 2, i, :], FT[:, l % 2, :], K.w_ef[:, i, :],
                                           start=False, stop=True)
                        mm.then_inc(z_done, 1)
                    if (at := at_stage(it, lane, 5)) is not None:
                        c, l = at
                        pe.wait_ge(msg_done, c + 1)
                        if over0(C * (c - 1)):
                            pe.wait_ge(added, C * (c - 1))
                        for i in range(C):
                            mm = pe.matmul(p_agg[:, l % 2, i, :], S[:, l, i, :], msg[:, l % 2, i, :],
                                           start=True, stop=True)
                        mm.then_inc(summed, 1)

            chunk_loop(pe, body)

        @block.vector
        def _(dve):
            regs = [dve.alloc_register(f"e0_dve{i}") for i in range(C)]

            def body(it):
                for lane in range(LANES):
                    if (at := at_stage(it, lane, 2)) is not None:
                        c, l = at
                        if over0(c - LANES + 1):
                            dve.wait_ge(summed, c - LANES + 1)
                        ed.one_hot(dve, S[:, l], c).then_inc(hot, 1)
                    if (at := at_stage(it, lane, 4)) is not None:
                        c, l = at
                        dve.wait_ge(ln_done, c + 1)
                        dve.scalar_tensor_tensor(out=low[:, l % 2], in0=z[:, l % 2, :, 0:D], scalar=0.0,
                                                 in1=soft[:, l % 2, :, 0:D], op0=ALU.min, op1=ALU.subtract)
                        dve.scalar_tensor_tensor(out=high[:, l % 2], in0=z[:, l % 2, :, D:2 * D], scalar=0.0,
                                                 in1=soft[:, l % 2, :, D:2 * D], op0=ALU.max, op1=ALU.add
                                                 ).then_inc(halves, 1)
                    if (at := at_stage(it, lane, 3)) is not None:
                        c, l = at
                        dve.wait_ge(z_done, c + 1)
                        dve.wait_ge(far_in[l], 64 * lane_turn(it, lane, 3))
                        dve.tensor_tensor(z[:, l % 2], p_z[:, l % 2], far[:, l], ALU.add).then_inc(z_read, 1)
                    if (at := at_stage(it, lane, 4)) is not None:
                        c, l = at
                        dve.wait_ge(sig_done, c + 1)
                        if over0(c - 1):
                            dve.wait_ge(summed, c - 1)
                        dve.tensor_tensor(msg[:, l % 2], low[:, l % 2], high[:, l % 2], ALU.mult).then_inc(msg_done, 1)
                    if (at := at_stage(it, lane, 5)) is not None:
                        c, l = at
                        add_to_blocks(dve, ed, regs, c, agg, p_agg[:, l % 2], D, summed, added)

            chunk_loop(dve, body)


def lane_turn(it, lane, lag):
    return (LANES * it + lane - lag) // LANES + 1 if isinstance(it, int) else it + (lane - lag) // LANES + 1


def add_to_blocks(dve, ed, regs, c, agg, p, n, summed, added):
    blocks = ed.block_values(dve, regs, c)
    dve.wait_ge(summed, c + 1)
    for i in range(C):
        if over0(C * c + i):
            dve.wait_ge(added, C * c + i)
        dst = agg[:, bass.ds(blocks[i], 1), 0:n]
        dve.tensor_tensor(dst, dst, p[:, i:i + 1, 0:n], ALU.add).then_inc(added, 1)


def layer0(nc, K, x):
    with ExitStack() as ctx:
        agg = ctx.enter_context(nc.sbuf_tensor("agg0", [P, B, D], F32))
        with ExitStack() as inner:
            own = inner.enter_context(nc.sbuf_tensor("own0", [P, B, 2 * D], F32))
            node_pass(nc, K, "n0", x, [(K.w("own0"), 2 * D, K.v("b0"), own),
                                            (K.w("other0"), 2 * D, None, (K.table0, 0, 2 * D))], clear=agg)
            edge_pass0(nc, K, own, agg)
        tmp = ctx.enter_context(nc.sbuf_tensor("tmp0", [P, B, D], F32))
        batch_norm(nc, K, agg, tmp)

        def program(dve, link, scalar_step):
            link(dve.tensor_tensor(agg[:], agg[:], bc_mid(K.v("bn_g"), B), ALU.mult))
            link(dve.tensor_tensor(agg[:], agg[:], bc_mid(K.v("bn_b"), B), ALU.add))
            link(dve.tensor_tensor(agg[:], agg[:], x[:], ALU.add))
            scalar_step(tmp[:], agg[:], ACT.Abs)
            scalar_step(tmp[:], tmp[:], ACT.Exp, scale=-1.0)
            scalar_step(tmp[:], tmp[:], ACT.Ln, bias=1.0)
            link(dve.scalar_tensor_tensor(out=agg[:], in0=agg[:], scalar=0.0, in1=tmp[:], op0=ALU.max, op1=ALU.add))
            link(dve.tensor_tensor(x[:], x[:], agg[:], ALU.add))
            layer_norm(dve, link, scalar_step, K, x[:], tmp[:])

        on_vector(nc, K, "f0", program)


def batch_norm(nc, K, agg, tmp):
    with ExitStack() as ctx:
        sb, ps = ctx_tools(nc, ctx)
        p_sum = ps("bn_p_sum", [P, 2, 512])
        mean, rstd = sb("bn_mean", [P, D]), sb("bn_rstd", [P, D])
        new = Sems(nc, K.used_sems, "bn")
        chain, mean_sum, squares, var_sum, asked, rooted = new("chain", "mean_sum", "squares", "var_sum", "asked", "rooted")
        block = ctx.enter_context(nc.Block())

        def column_sums(pe, bank, src, done):
            for b in range(B):
                rows = P if b < B - 1 else LAST
                mm = pe.matmul(p_sum[:, bank, 0:D], K.ones[0:rows, :], src[0:rows, b, :],
                               start=(b == 0), stop=(b == B - 1))
            mm.then_inc(done, 1)

        @block.tensor
        def _(pe):
            column_sums(pe, 0, agg, mean_sum)
            pe.wait_ge(squares, 1)
            column_sums(pe, 1, tmp, var_sum)

        @block.scalar
        def _(act):
            act.wait_ge(asked, 1)
            nc.scalar.activation(mean[:], rstd[:], ACT.Sqrt).then_inc(rooted, 1)

        @block.vector
        def _(dve):
            count = [0]

            def link(ins):
                count[0] += 1
                ins.then_inc(chain, 1)
                dve.wait_ge(chain, count[0])

            dve.wait_ge(mean_sum, 1)
            link(dve.tensor_scalar(mean[:], p_sum[:, 0, 0:D], 1.0 / N, None, ALU.mult))
            link(dve.tensor_tensor(agg[:], agg[:], bc_mid(mean[:], B), ALU.subtract))
            dve.tensor_tensor(tmp[:], agg[:], agg[:], ALU.mult).then_inc(squares, 1)
            dve.wait_ge(var_sum, 1)
            dve.tensor_scalar(rstd[:], p_sum[:, 1, 0:D], 1.0 / N, 1e-5, ALU.mult, ALU.add).then_inc(asked, 1)
            dve.wait_ge(rooted, 1)
            link(dve.reciprocal(rstd[:], mean[:]))
            link(dve.tensor_tensor(agg[:], agg[:], bc_mid(rstd[:], B), ALU.mult))



def edge_pass1a(nc, K, peak):
    ctx = ExitStack()
    with ctx:
        sb, ps = ctx_tools(nc, ctx)
        ed = Edges(nc, K, "d")
        R = C * H
        idx = sb("m1_idx", [P, LANES, C], I32)
        far = sb("m1_far", [P, LANES, C, D + H])
        S = sb("m1_S", [P, 2, C, P])
        a_u = sb("m1_au", [P, 2, C, H])
        keys = sb("m1_keys", [P, 2, C, H])
        same = sb("m1_same", [R, 2, P + 1])
        reset = sb("m1_reset", [R, 2, P])
        run = sb("m1_run", [R, 2, P])
        kt = sb("m1_kt", [R, 2, P])
        ends = sb("m1_ends", [R, 2, 2, P])
        back = sb("m1_back", [P, 2, 2, R])
        miss = sb("m1_miss", [P, 2, C, H])
        cand = sb("m1_cand", [P, 2, C, H])
        p_turn = ps("m1_p_turn", [R, 2, 2, 2 * P])
        p_back = ps("m1_p_back", [P, 2, 2, 4 * R * 2])
        p_max = ps("m1_p_max", [P, 2, C, 2 * P])
        new = Sems(nc, K.used_sems, "m1")
        picked, gate, spilled_all = new("picked", "gate", "spilled_all")
        far_in = new("far_in0", "far_in1", "far_in2", "far_in3")
        spilled = new("spilled0", "spilled1", "spilled2", "spilled3")
        hot, laid, turned, scanned, scan_steps, returned, copied, spread, maxed = new(
            "hot", "laid", "turned", "scanned", "scan_steps", "returned", "copied", "spread", "maxed")
        cleared, cand_steps, pe_gate = new("cleared", "cand_steps", "pe_gate")
        block = ctx.enter_context(nc.Block())

        @block.gpsimd
        def _(pool):
            def body(it):
                for lane in range(LANES):
                    if (at := at_stage(it, lane, 0)) is not None:
                        c, l = at
                        pool.wait_ge(picked, c + 1)
                        if over0(c - LANES + 1):
                            pool.wait_ge(laid, c - LANES + 1)
                            pool.wait_ge(spilled[l], 16 * (lane_turn(it, lane, 0) - 1))
                        pool.sem_inc(gate, 1)
                        for i in range(C):
                            pool.indirect_dma_start(far[:, l, i, :], None, K.table1,
                                                    bass.IndirectOffsetOnAxis(ap=idx[:, l, i:i + 1], axis=0)
                                                    ).then_inc(far_in[l], 16)

            chunk_loop(pool, body)

        @block.sync
        def _(sp):
            chunks = K.spill1.rearrange("(c e t) w -> e c t w", t=C, e=P)

            def body(it):
                for lane in range(LANES):
                    if (at := at_stage(it, lane, 2)) is not None:
                        c, l = at
                        sp.wait_ge(far_in[l], 64 * lane_turn(it, lane, 2))
                        sp.dma_start(chunks[:, bass.ds(c, 1), :, :].rearrange("e c t w -> e c (t w)"),
                                     far[:, l:l + 1, :, :].rearrange("p o t w -> p o (t w)")).then_inc(spilled[l], 16)

            chunk_loop(sp, body)
            for l in range(LANES):
                sp.wait_ge(spilled[l], 16 * ITERS)

        @block.scalar
        def _(act):
            def body(it):
                for lane in range(LANES):
                    if (at := at_stage(it, lane, 0)) is not None:
                        c, l = at
                        if over0(c - LANES + 1):
                            act.wait_ge(far_in[l], 64 * (lane_turn(it, lane, 0) - 1))
                        ed.pick_others(act, idx[:, l, :], c).then_inc(picked, 1)
                    if (at := at_stage(it, lane, 2)) is not None:
                        c, l = at
                        act.wait_ge(far_in[l], 64 * lane_turn(it, lane, 2))
                        if over0(c - 1):
                            act.wait_ge(turned, c - 1)
                        nc.scalar.activation(keys[:, l % 2], bc_last(K.key["d"][:, bass.ds(c * C, C)], H), ACT.Copy)
                        nc.scalar.activation(a_u[:, l % 2], far[:, l, :, D:D + H], ACT.Copy).then_inc(laid, 1)
                    if (at := at_stage(it, lane, 3)) is not None:
                        c, l = at
                        act.wait_ge(returned, c + 1)
                        if over0(c - 1):
                            act.wait_ge(spread, c - 1)
                        nc.scalar.activation(back[:, l % 2], p_back[:, l % 2, :, 0:R], ACT.Copy).then_inc(copied, 1)

            chunk_loop(act, body)

        @block.tensor
        def _(pe):
            def body(it):
                for lane in range(LANES):
                    if (at := at_stage(it, lane, 2)) is not None:
                        c, l = at
                        pe.wait_ge(laid, c + 1)
                        if over0(c - 1):
                            pe.wait_ge(scanned, c - 1)
                        pe.transpose(p_turn[:, l % 2, 0, 0:P], a_u[:, l % 2].rearrange("p t h -> p (t h)"), K.ident[:])
                        pe.transpose(p_turn[:, l % 2, 1, 0:P], keys[:, l % 2].rearrange("p t h -> p (t h)"), K.ident[:]
                                     ).then_inc(turned, 1)
                    if (at := at_stage(it, lane, 3)) is not None:
                        c, l = at
                        pe.wait_ge(scanned, c + 1)
                        if over0(c - 1):
                            pe.wait_ge(copied, c - 1)
                        pe.sem_inc(pe_gate, 1)
                        pe.transpose(p_back[:, l % 2, 0, 0:R], ends[:, l % 2, 0, :], K.ident[0:R, 0:R])
                        pe.transpose(p_back[:, l % 2, 1, 0:R], ends[:, l % 2, 1, :], K.ident[0:R, 0:R]).then_inc(returned, 1)
                    if (at := at_stage(it, lane, 4)) is not None:
                        c, l = at
                        pe.wait_ge(hot, c + 1)
                        pe.wait_ge(copied, c + 1)
                        if over0(c - 1):
                            pe.wait_ge(cand_steps, 2 * (c - 1))
                        for i in range(C):
                            mm = pe.matmul(p_max[:, l % 2, i, 0:2 * H],
                                           S[:, l % 2, i, :], back[:, l % 2, :, i * H:(i + 1) * H], start=True, stop=True)
                        mm.then_inc(spread, 1)

            chunk_loop(pe, body)

        @block.vector
        def _(dve):
            regs = [dve.alloc_register(f"m1_dve{i}") for i in range(C)]
            dve.memset(peak[:], -BIG).then_inc(cleared, 1)
            dve.memset(same[:], 0.0).then_inc(cleared, 1)
            dve.wait_ge(cleared, 2)

            def body(it):
                for lane in range(LANES):
                    if (at := at_stage(it, lane, 3)) is not None:
                        c, l = at
                        h = l % 2
                        dve.wait_ge(turned, c + 1)
                        if over0(c - 1):
                            dve.wait_ge(returned, c - 1)
                        dve.tensor_copy(kt[:, h, :], p_turn[:, h, 1, 0:P]).then_inc(scan_steps, 1)
                        dve.wait_ge(scan_steps, 4 * c + 1)
                        dve.tensor_tensor(same[:, h, 1:P], kt[:, h, 1:P], kt[:, h, 0:P - 1], ALU.is_equal
                                          ).then_inc(scan_steps, 1)
                        dve.wait_ge(scan_steps, 4 * c + 2)
                        dve.tensor_scalar(ends[:, h, 1, :], same[:, h, 1:P + 1], -1.0, 1.0, ALU.mult, ALU.add)
                        dve.tensor_scalar(reset[:, h, :], same[:, h, 0:P], -1.0, BIG, ALU.add, ALU.mult
                                          ).then_inc(scan_steps, 1)
                        dve.wait_ge(scan_steps, 4 * c + 3)
                        dve.tensor_tensor_scan(run[:, h, :], reset[:, h, :], p_turn[:, h, 0, 0:P], -BIG, ALU.add, ALU.max
                                               ).then_inc(scan_steps, 1)
                        dve.wait_ge(scan_steps, 4 * c + 4)
                        dve.tensor_tensor(ends[:, h, 0, :], run[:, h, :], ends[:, h, 1, :], ALU.mult).then_inc(scanned, 1)
                    if (at := at_stage(it, lane, 3)) is not None:
                        c, l = at
                        if over0(c - 1):
                            dve.wait_ge(spread, c - 1)
                        ed.one_hot(dve, S[:, l % 2], c).then_inc(hot, 1)
                    if (at := at_stage(it, lane, 5)) is not None:
                        c, l = at
                        h = l % 2
                        blocks = ed.block_values(dve, regs, c)
                        dve.wait_ge(spread, c + 1)
                        dve.tensor_scalar(miss[:, h], p_max[:, h, :, H:2 * H], -1.0, BIG, ALU.add, ALU.mult
                                          ).then_inc(cand_steps, 1)
                        dve.wait_ge(cand_steps, 2 * c + 1)
                        dve.tensor_tensor(cand[:, h], p_max[:, h, :, 0:H], miss[:, h], ALU.add).then_inc(cand_steps, 1)
                        dve.wait_ge(cand_steps, 2 * c + 2)
                        for i in range(C):
                            if over0(C * c + i):
                                dve.wait_ge(maxed, C * c + i)
                            dst = peak[:, bass.ds(blocks[i], 1), :]
                            dve.tensor_tensor(dst, dst, cand[:, h, i:i + 1, :], ALU.max).then_inc(maxed, 1)

            chunk_loop(dve, body)


def edge_pass1b(nc, K, own, agg):
    ctx = ExitStack()
    with ctx:
        sb, ps = ctx_tools(nc, ctx)
        ed = Edges(nc, K, "d")
        M = D + H + 1
        far = sb("a1_far", [P, LANES, C, D + H])
        S = sb("a1_S", [P, 4, C, P])
        ST = sb("a1_ST", [P, 2, C * P])
        score = sb("a1_score", [P, 2, C, H])
        shifted = sb("a1_shifted", [P, 2, C, H])
        msg = sb("a1_msg", [P, 2, C, M])
        p_turn = ps("a1_p_turn", [P, C * P])
        p_own = ps("a1_p_own", [P, 2, C, P])
        p_agg = ps("a1_p_agg", [P, 2, C, 2 * P])
        new = Sems(nc, K.used_sems, "a1")
        far_in = new("far_in0", "far_in1", "far_in2", "far_in3")
        hot, turned, kept, owned, steps, exped, msg_done, summed, added, cleared = new(
            "hot", "turned", "kept", "owned", "steps", "exped", "msg_done", "summed", "added", "cleared")
        block = ctx.enter_context(nc.Block())

        @block.sync
        def _(sp):
            chunks = K.spill1.rearrange("(c e t) w -> e c t w", t=C, e=P)

            def body(it):
                for lane in range(LANES):
                    if (at := at_stage(it, lane, 0)) is not None:
                        c, l = at
                        if over0(c - LANES + 1):
                            sp.wait_ge(msg_done, c - LANES + 1)
                        sp.dma_start(far[:, l:l + 1, :, :].rearrange("p o t w -> p o (t w)"),
                                     chunks[:, bass.ds(c, 1), :, :].rearrange("e c t w -> e c (t w)")
                                     ).then_inc(far_in[l], 16)

            chunk_loop(sp, body)

        @block.scalar
        def _(act):
            def body(it):
                for lane in range(LANES):
                    if (at := at_stage(it, lane, 2)) is not None:
                        c, l = at
                        act.wait_ge(turned, c + 1)
                        if over0(c - 1):
                            act.wait_ge(owned, c - 1)
                        nc.scalar.activation(ST[:, l % 2, :], p_turn[:], ACT.Copy).then_inc(kept, 1)
                    if (at := at_stage(it, lane, 3)) is not None:
                        c, l = at
                        act.wait_ge(steps, 4 * (c + 1))
                        if over0(c - 1):
                            act.wait_ge(summed, c - 1)
                        nc.scalar.activation(msg[:, l % 2, :, D:D + H], shifted[:, l % 2], ACT.Exp).then_inc(exped, 1)

            chunk_loop(act, body)

        @block.tensor
        def _(pe):
            regs = [pe.alloc_register(f"a1_pe{i}") for i in range(C)]

            def body(it):
                for lane in range(LANES):
                    if (at := at_stage(it, lane, 2)) is not None:
                        c, l = at
                        pe.wait_ge(hot, c + 1)
                        if over0(c):
                            pe.wait_ge(kept, c)
                        for i in range(C):
                            mm = pe.transpose(p_turn[:, i * P:(i + 1) * P], S[:, l, i, :], K.ident[:])
                        mm.then_inc(turned, 1)
                    if (at := at_stage(it, lane, 3)) is not None:
                        c, l = at
                        blocks = ed.block_values(pe, regs, c)
                        pe.wait_ge(kept, c + 1)
                        if over0(c - 1):
                            pe.wait_ge(steps, 4 * (c - 1))
                        for i in range(C):
                            mm = pe.matmul(p_own[:, l % 2, i, 0:2 * H], ST[:, l % 2, i * P:(i + 1) * P],
                                           own[:, bass.ds(blocks[i], 1), :], start=True, stop=True)
                        mm.then_inc(owned, 1)
                    if (at := at_stage(it, lane, 5)) is not None:
                        c, l = at
                        pe.wait_ge(msg_done, c + 1)
                        if over0(C * (c - 1)):
                            pe.wait_ge(added, C * (c - 1))
                        for i in range(C):
                            mm = pe.matmul(p_agg[:, l % 2, i, 0:M], S[:, l, i, :], msg[:, l % 2, i, :],
                                           start=True, stop=True)
                        mm.then_inc(summed, 1)

            chunk_loop(pe, body)

        @block.vector
        def _(dve):
            regs = [dve.alloc_register(f"a1_dve{i}") for i in range(C)]
            dve.memset(agg[:], 0.0).then_inc(cleared, 1)
            dve.memset(msg[:], 1.0).then_inc(cleared, 1)
            dve.wait_ge(cleared, 2)

            def body(it):
                for lane in range(LANES):
                    if (at := at_stage(it, lane, 2)) is not None:
                        c, l = at
                        if over0(c - LANES + 1):
                            dve.wait_ge(summed, c - LANES + 1)
                        ed.one_hot(dve, S[:, l], c).then_inc(hot, 1)
                    if (at := at_stage(it, lane, 3)) is not None:
                        c, l = at
                        h = l % 2
                        dve.wait_ge(owned, c + 1)
                        dve.wait_ge(far_in[l], 16 * lane_turn(it, lane, 3))
                        if over0(c - 1):
                            dve.wait_ge(exped, c - 1)
                        dve.tensor_tensor(score[:, h], p_own[:, h, :, 0:H], far[:, l, :, D:D + H], ALU.add
                                          ).then_inc(steps, 1)
                        dve.wait_ge(steps, 4 * c + 1)
                        dve.scalar_tensor_tensor(out=shifted[:, h], in0=score[:, h], scalar=0.2, in1=score[:, h],
                                                 op0=ALU.mult, op1=ALU.max).then_inc(steps, 1)
                        dve.wait_ge(steps, 4 * c + 2)
                        dve.tensor_tensor(score[:, h], shifted[:, h], p_own[:, h, :, H:2 * H], ALU.subtract
                                          ).then_inc(steps, 1)
                        dve.wait_ge(steps, 4 * c + 3)
                        dve.tensor_scalar(shifted[:, h], score[:, h], 0.0, None, ALU.min).then_inc(steps, 1)
                    if (at := at_stage(it, lane, 4)) is not None:
                        c, l = at
                        h = l % 2
                        dve.wait_ge(exped, c + 1)
                        for i in range(C):
                            ex = msg[:, h, i, D:D + H]
                            mm = dve.tensor_tensor(
                                msg[:, h, i, 0:D].rearrange("p (d h) -> p d h", h=H),
                                far[:, l, i, 0:D].rearrange("p (d h) -> p d h", h=H), bc_mid(ex, HD), ALU.mult)
                        mm.then_inc(msg_done, 1)
                    if (at := at_stage(it, lane, 5)) is not None:
                        c, l = at
                        add_to_blocks(dve, ed, regs, c, agg, p_agg[:, l % 2], M, summed, added)

            chunk_loop(dve, body)


def layer1(nc, K, x, root):
    with ExitStack() as ctx:
        sb, _ = ctx_tools(nc, ctx)
        peak, own = sb("peak1", [P, B, H]), sb("own1", [P, B, 2 * H])
        with ExitStack() as inner:
            h = inner.enter_context(nc.sbuf_tensor("h1", [P, B, D], F32))
            node_pass(nc, K, "n1h", x, [(K.w("in1"), D, K.v("b_in1"), h)])
            node_pass(nc, K, "n1a", h, [(K.w("a1"), 2 * H, K.v("b_a1"), own),
                                             (K.w("a1"), 2 * H, K.v("b_a1"), (K.table1, D, H))])
            [out] = Sems(nc, K.used_sems, "h1")("out")
            with nc.Block() as block:
                @block.sync
                def _(sp):
                    rows = K.table1.rearrange("(b n) f -> n b f", n=P)
                    sp.dma_start(rows[:, :, 0:D], h[:]).then_inc(out, 16)
                    sp.wait_ge(out, 16)
        edge_pass1a(nc, K, peak)
        agg = sb("agg1", [P, B, D + H + 1])
        y, tmp = sb("y1", [P, B, D]), sb("tmp1", [P, B, D])

        def largest(dve, link, scalar_step):
            link(dve.tensor_copy(own[:, :, 0:H], own[:, :, H:2 * H]))
            link(dve.tensor_tensor(peak[:], peak[:], own[:, :, 0:H], ALU.add))
            link(dve.scalar_tensor_tensor(out=own[:, :, H:2 * H], in0=peak[:], scalar=0.2, in1=peak[:],
                                          op0=ALU.mult, op1=ALU.max))

        on_vector(nc, K, "f1a", largest)
        edge_pass1b(nc, K, own, agg)

        def divide(dve, link, scalar_step):
            link(dve.tensor_scalar(peak[:], agg[:, :, D:D + H], 1e-30, None, ALU.max))
            link(dve.reciprocal(peak[:], peak[:]))
            for b in range(HD):
                link(dve.tensor_tensor(y[:, :, b * H:(b + 1) * H], agg[:, :, b * H:(b + 1) * H], peak[:], ALU.mult))
            link(dve.tensor_scalar(root[:], agg[:, :, D + H], 1.0, None, ALU.add))
            scalar_step(K.stat[:, 0, :], root[:], ACT.Sqrt)
            link(dve.reciprocal(root[:], K.stat[:, 0, :]))

        on_vector(nc, K, "f1b", divide)
        node_pass(nc, K, "n1m", y, [(K.w("mlp1"), D, K.v("b_mlp1"), tmp)])

        def gelu(dve, link, scalar_step):
            scalar_step(y[:], tmp[:], ACT.Gelu_apprx_tanh)

        on_vector(nc, K, "f1c", gelu)
        node_pass(nc, K, "n1n", y, [(K.w("mlp2"), D, K.v("b_mlp2"), tmp)])

        def finish(dve, link, scalar_step):
            link(dve.tensor_tensor(x[:], x[:], tmp[:], ALU.add))
            layer_norm(dve, link, scalar_step, K, x[:], y[:])

        on_vector(nc, K, "f1d", finish)



def edge_pass2(nc, K, i_layer, agg):
    ctx = ExitStack()
    with ctx:
        sb, ps = ctx_tools(nc, ctx)
        ed = Edges(nc, K, "d")
        s = f"g{i_layer}"
        idx = sb(f"{s}_idx", [P, LANES, C], I32)
        far = sb(f"{s}_far", [P, LANES, C, D])
        S = sb(f"{s}_S", [P, 2, C, P])
        p_agg = ps(f"{s}_p_agg", [P, 2, C, D])
        new = Sems(nc, K.used_sems, s)
        picked, gate = new("picked", "gate")
        far_in = new("far_in0", "far_in1", "far_in2", "far_in3")
        hot, summed, added = new("hot", "summed", "added")
        block = ctx.enter_context(nc.Block())

        @block.gpsimd
        def _(pool):
            def body(it):
                for lane in range(LANES):
                    if (at := at_stage(it, lane, 0)) is not None:
                        c, l = at
                        pool.wait_ge(picked, c + 1)
                        if over0(c - LANES + 1):
                            pool.wait_ge(summed, c - LANES + 1)
                        pool.sem_inc(gate, 1)
                        for i in range(C):
                            pool.indirect_dma_start(far[:, l, i, :], None, K.table2[i_layer],
                                                    bass.IndirectOffsetOnAxis(ap=idx[:, l, i:i + 1], axis=0)
                                                    ).then_inc(far_in[l], 16)

            chunk_loop(pool, body)

        @block.scalar
        def _(act):
            def body(it):
                for lane in range(LANES):
                    if (at := at_stage(it, lane, 0)) is not None:
                        c, l = at
                        if over0(c - LANES + 1):
                            act.wait_ge(far_in[l], 64 * (lane_turn(it, lane, 0) - 1))
                        ed.pick_others(act, idx[:, l, :], c).then_inc(picked, 1)

            chunk_loop(act, body)

        @block.tensor
        def _(pe):
            def body(it):
                for lane in range(LANES):
                    if (at := at_stage(it, lane, 2)) is not None:
                        c, l = at
                        pe.wait_ge(hot, c + 1)
                        pe.wait_ge(far_in[l], 64 * lane_turn(it, lane, 2))
                        if over0(C * (c - 1)):
                            pe.wait_ge(added, C * (c - 1))
                        for i in range(C):
                            mm = pe.matmul(p_agg[:, l % 2, i, :], S[:, l % 2, i, :], far[:, l, i, :],
                                           start=True, stop=True)
                        mm.then_inc(summed, 1)

            chunk_loop(pe, body)

        @block.vector
        def _(dve):
            regs = [dve.alloc_register(f"{s}_dve{i}") for i in range(C)]

            def body(it):
                for lane in range(LANES):
                    if (at := at_stage(it, lane, 1)) is not None:
                        c, l = at
                        if over0(c - 1):
                            dve.wait_ge(summed, c - 1)
                        ed.one_hot(dve, S[:, l % 2], c).then_inc(hot, 1)
                    if (at := at_stage(it, lane, 2)) is not None:
                        c, l = at
                        add_to_blocks(dve, ed, regs, c, agg, p_agg[:, l % 2], D, summed, added)

            chunk_loop(dve, body)


def layer2(nc, K, x, root):
    with ExitStack() as ctx:
        sb, _ = ctx_tools(nc, ctx)
        h, agg = sb("h2", [P, B, D]), sb("agg2", [P, B, D])
        nodes = x
        for i in range(3):
            node_pass(nc, K, f"n2{i}", nodes, [(K.w(f"g{i}"), D, None, agg)])
            [out] = Sems(nc, K.used_sems, f"t2{i}")("out")

            def scale(dve, link, scalar_step):
                link(dve.tensor_tensor(agg[:], agg[:], bc_last(root[:], D), ALU.mult))

            on_vector(nc, K, f"f2{i}a", scale)
            with nc.Block() as block:
                @block.sync
                def _(sp, i=i, out=out):
                    sp.dma_start(K.table2[i].rearrange("(b n) f -> n b f", n=P), agg[:]).then_inc(out, 16)
                    sp.wait_ge(out, 16)
            edge_pass2(nc, K, i, agg)

            def finish(dve, link, scalar_step, i=i):
                link(dve.tensor_tensor(h[:], agg[:], bc_last(root[:], D), ALU.mult))
                link(dve.tensor_tensor(h[:], h[:], bc_mid(K.v(f"b_g{i}"), B), ALU.add))
                if i < 2:
                    link(dve.tensor_scalar(h[:], h[:], 0.0, None, ALU.max))
                else:
                    link(dve.tensor_tensor(x[:], x[:], h[:], ALU.add))
                    layer_norm(dve, link, scalar_step, K, x[:], h[:])

            on_vector(nc, K, f"f2{i}b", finish)
            nodes = h



def edge_pass3a(nc, K, q, logit):
    ctx = ExitStack()
    with ctx:
        sb, ps = ctx_tools(nc, ctx)
        ed = Edges(nc, K, "s")
        idx = sb("l3_idx", [P, LANES, C], I32)
        lens = sb("l3_lens", [P, LANES, C])
        far = sb("l3_far", [P, LANES, C, 2 * D])
        S = sb("l3_S", [P, 2, C, P])
        ST = sb("l3_ST", [P, 2, C * P])
        LT = sb("l3_LT", [C, 2, P])
        hid = sb("l3_hid", [P, 2, C * P])
        prod = sb("l3_prod", [P, 2, C, D])
        dot = sb("l3_dot", [P, 2, C, H])
        bias = sb("l3_bias", [P, 2, C, H])
        p_turn = ps("l3_p_turn", [P, C * P])
        p_len = ps("l3_p_len", [C, P])
        p_hid = ps("l3_p_hid", [P, C * P])
        p_q = ps("l3_p_q", [P, 2, C, D])
        p_bias = ps("l3_p_bias", [P, 2, C, P])
        new = Sems(nc, K.used_sems, "l3")
        picked, gate = new("picked", "gate")
        far_in = new("far_in0", "far_in1", "far_in2", "far_in3")
        spilled = new("spilled0", "spilled1", "spilled2", "spilled3")
        hot, turned, kept, q_done, hid_in, hid_out, biased, multiplied, steps = new(
            "hot", "turned", "kept", "q_done", "hid_in", "hid_out", "biased", "multiplied", "steps")
        block = ctx.enter_context(nc.Block())

        @block.gpsimd
        def _(pool):
            def body(it):
                for lane in range(LANES):
                    if (at := at_stage(it, lane, 0)) is not None:
                        c, l = at
                        pool.wait_ge(picked, c + 1)
                        if over0(c - LANES + 1):
                            pool.wait_ge(multiplied, c - LANES + 1)
                            pool.wait_ge(spilled[l], 16 * (lane_turn(it, lane, 0) - 1))
                        pool.sem_inc(gate, 1)
                        for i in range(C):
                            pool.indirect_dma_start(far[:, l, i, :], None, K.table3,
                                                    bass.IndirectOffsetOnAxis(ap=idx[:, l, i:i + 1], axis=0)
                                                    ).then_inc(far_in[l], 16)

            chunk_loop(pool, body)

        @block.sync
        def _(sp):
            chunks = K.spill3.rearrange("(c e t) w -> e c t w", t=C, e=P)

            def body(it):
                for lane in range(LANES):
                    if (at := at_stage(it, lane, 2)) is not None:
                        c, l = at
                        sp.wait_ge(far_in[l], 64 * lane_turn(it, lane, 2))
                        sp.dma_start(chunks[:, bass.ds(c, 1), :, :], far[:, l:l + 1, :, D:2 * D]).then_inc(spilled[l], 16)

            chunk_loop(sp, body)
            for l in range(LANES):
                sp.wait_ge(spilled[l], 16 * ITERS)

        @block.scalar
        def _(act):
            def body(it):
                for lane in range(LANES):
                    if (at := at_stage(it, lane, 0)) is not None:
                        c, l = at
                        if over0(c - LANES + 1):
                            act.wait_ge(far_in[l], 64 * (lane_turn(it, lane, 0) - 1))
                            act.wait_ge(turned, c - LANES + 1)
                        nc.scalar.activation(lens[:, l, :], K.length[:, bass.ds(c * C, C)], ACT.Copy)
                        ed.pick_others(act, idx[:, l, :], c).then_inc(picked, 1)
                    if (at := at_stage(it, lane, 2)) is not None:
                        c, l = at
                        act.wait_ge(turned, c + 1)
                        if over0(c - 1):
                            act.wait_ge(q_done, c - 1)
                            act.wait_ge(hid_in, c - 1)
                        nc.scalar.activation(LT[:, l % 2, :], p_len[:], ACT.Copy)
                        nc.scalar.activation(ST[:, l % 2, :], p_turn[:], ACT.Copy).then_inc(kept, 1)
                    if (at := at_stage(it, lane, 3)) is not None:
                        c, l = at
                        act.wait_ge(hid_in, c + 1)
                        if over0(c - 1):
                            act.wait_ge(biased, c - 1)
                        nc.scalar.activation(hid[:, l % 2, :], p_hid[:], ACT.Silu, bias=K.w("hid_b")).then_inc(hid_out, 1)

            chunk_loop(act, body)

        @block.tensor
        def _(pe):
            regs = [pe.alloc_register(f"l3_pe{i}") for i in range(C)]

            def body(it):
                for lane in range(LANES):
                    if (at := at_stage(it, lane, 2)) is not None:
                        c, l = at
                        pe.wait_ge(hot, c + 1)
                        pe.wait_ge(picked, c + 1)
                        if over0(c):
                            pe.wait_ge(kept, c)
                        for i in range(C):
                            pe.transpose(p_turn[:, i * P:(i + 1) * P], S[:, l % 2, i, :], K.ident[:])
                        pe.transpose(p_len[:], lens[:, l, :], K.ident[:]).then_inc(turned, 1)
                    if (at := at_stage(it, lane, 3)) is not None:
                        c, l = at
                        blocks = ed.block_values(pe, regs, c)
                        pe.wait_ge(kept, c + 1)
                        if over0(c):
                            pe.wait_ge(hid_out, c)
                        for i in range(C):
                            mm = pe.matmul(p_hid[:, i * P:(i + 1) * P], K.w_len[:, i, :], LT[:, l % 2, :],
                                           start=True, stop=True)
                        mm.then_inc(hid_in, 1)
                        if over0(c - 1):
                            pe.wait_ge(multiplied, c - 1)
                        for i in range(C):
                            mm = pe.matmul(p_q[:, l % 2, i, :], ST[:, l % 2, i * P:(i + 1) * P],
                                           q[:, bass.ds(blocks[i], 1), :], start=True, stop=True)
                        mm.then_inc(q_done, 1)
                    if (at := at_stage(it, lane, 4)) is not None:
                        c, l = at
                        pe.wait_ge(hid_out, c + 1)
                        if over0(c - 1):
                            pe.wait_ge(steps, 3 * (c - 1))
                        for i in range(C):
                            mm = pe.matmul(p_bias[:, l % 2, i, 0:H], hid[:, l % 2, i * P:(i + 1) * P], K.w("bias3"),
                                           start=True, stop=True)
                        mm.then_inc(biased, 1)

            chunk_loop(pe, body)

        @block.vector
        def _(dve):
            def body(it):
                for lane in range(LANES):
                    if (at := at_stage(it, lane, 2)) is not None:
                        c, l = at
                        if over0(c - 1):
                            dve.wait_ge(turned, c - 1)
                        ed.one_hot(dve, S[:, l % 2], c).then_inc(hot, 1)
                    if (at := at_stage(it, lane, 4)) is not None:
                        c, l = at
                        h = l % 2
                        dve.wait_ge(q_done, c + 1)
                        dve.wait_ge(far_in[l], 64 * lane_turn(it, lane, 4))
                        dve.tensor_tensor(prod[:, h], p_q[:, h], far[:, l, :, 0:D], ALU.mult).then_inc(multiplied, 1)
                        dve.wait_ge(multiplied, c + 1)
                        dve.tensor_reduce(dot[:, h], prod[:, h].rearrange("p t (h d) -> p t h d", h=H), AX.X, ALU.add
                                          ).then_inc(steps, 1)
                        dve.wait_ge(biased, c + 1)
                        dve.tensor_tensor(bias[:, h], p_bias[:, h, :, 0:H], bc_mid(K.v("b_bias3"), C), ALU.add
                                          ).then_inc(steps, 1)
                        dve.wait_ge(steps, 3 * c + 2)
                        dve.scalar_tensor_tensor(out=logit[:, bass.ds(c * C, C), :], in0=dot[:, h], scalar=HD ** -0.5,
                                                 in1=bias[:, h], op0=ALU.mult, op1=ALU.add).then_inc(steps, 1)

            chunk_loop(dve, body)


def cut_and_exp(nc, K, logit):
    with ExitStack() as ctx:
        sb, ps = ctx_tools(nc, ctx)
        cut, turn, real = sb("cut", [P, T]), sb("turn", [P, T]), sb("real", [P, T])
        most, row, diag = sb("most", [P, H]), sb("row", [H, 1]), sb("diag", [H, H])
        every = sb("every", [P, H])
        p_row, p_all = ps("p_row", [H, P]), ps("p_all", [P, H])
        new = Sems(nc, K.used_sems, "cut")
        chain, turned, asked, answered, ready, crossed = new("chain", "turned", "asked", "answered", "ready", "crossed")
        block = ctx.enter_context(nc.Block())

        @block.vector
        def _(dve):
            count = [0]

            def link(ins):
                count[0] += 1
                ins.then_inc(chain, 1)
                dve.wait_ge(chain, count[0])

            link(dve.tensor_scalar(turn[:], K.length[:], 0.5 / CUTOFF, None, ALU.mult))
            link(dve.tensor_scalar(turn[:], turn[:], 12582912.0, 12582912.0, ALU.add, ALU.subtract))
            link(dve.scalar_tensor_tensor(out=turn[:], in0=turn[:], scalar=-2.0 * CUTOFF, in1=K.length[:],
                                          op0=ALU.mult, op1=ALU.add))
            link(dve.tensor_scalar(cut[:], turn[:], -1.0, None, ALU.mult))
            link(dve.tensor_tensor(turn[:], turn[:], cut[:], ALU.max))
            link(dve.tensor_scalar(turn[:], turn[:], -np.pi / CUTOFF, np.pi / 2, ALU.mult, ALU.add))
            link(dve.tensor_scalar(turn[:], turn[:], -np.pi / 2, np.pi / 2, ALU.max, ALU.min))
            dve.sem_inc(asked, 1)
            dve.wait_ge(answered, 1)
            link(dve.tensor_scalar(cut[:], cut[:], 1.0, 0.5, ALU.add, ALU.mult))
            link(dve.tensor_scalar(turn[:], K.length[:], CUTOFF, None, ALU.is_lt))
            link(dve.tensor_tensor(cut[:], cut[:], turn[:], ALU.mult))
            link(dve.tensor_tensor(logit[:], logit[:], bc_last(cut[:], H), ALU.mult))
            link(dve.tensor_scalar(real[:], K.key["s"][:], 0.0, None, ALU.is_ge))
            link(dve.tensor_scalar(turn[:], real[:], -1.0, 3.0e38, ALU.add, ALU.mult))
            link(dve.tensor_tensor(logit[:], logit[:], bc_last(real[:], H), ALU.mult))
            link(dve.tensor_tensor(logit[:], logit[:], bc_last(turn[:], H), ALU.add))
            link(dve.tensor_reduce(most[:], logit[:].rearrange("p t h -> p h t"), AX.X, ALU.max))
            dve.sem_inc(ready, 1)
            dve.wait_ge(crossed, 1)
            link(dve.tensor_reduce(row[:], p_row[:], AX.X, ALU.max))
            link(dve.tensor_scalar(diag[:], K.ident[0:H, 0:H], row[:, 0:1], None, ALU.mult))
            dve.sem_inc(ready, 1)
            dve.wait_ge(crossed, 2)
            link(dve.tensor_copy(every[:], p_all[:]))
            link(dve.tensor_tensor(logit[:], logit[:], bc_mid(every[:], T), ALU.subtract))
            dve.sem_inc(asked, 1)
            dve.wait_ge(answered, 2)

        @block.tensor
        def _(pe):
            pe.wait_ge(ready, 1)
            pe.transpose(p_row[:], most[:], K.ident[:]).then_inc(crossed, 1)
            pe.wait_ge(ready, 2)
            pe.matmul(p_all[:], K.ones[0:H, :], diag[:], start=True, stop=True).then_inc(crossed, 1)

        @block.scalar
        def _(act):
            act.wait_ge(asked, 1)
            nc.scalar.activation(cut[:], turn[:], ACT.Sin).then_inc(answered, 1)
            act.wait_ge(asked, 2)
            nc.scalar.activation(logit[:], logit[:], ACT.Exp).then_inc(answered, 1)


def edge_pass3b(nc, K, weight, agg):
    ctx = ExitStack()
    with ctx:
        sb, ps = ctx_tools(nc, ctx)
        ed = Edges(nc, K, "s")
        M = D + H
        far = sb("v3_far", [P, LANES, C, D])
        S = sb("v3_S", [P, 2, C, P])
        msg = sb("v3_msg", [P, 2, C, M])
        p_agg = ps("v3_p_agg", [P, 2, C, 2 * P])
        new = Sems(nc, K.used_sems, "v3")
        far_in = new("far_in0", "far_in1", "far_in2", "far_in3")
        hot, weights_in, msg_done, summed, added, cleared = new(
            "hot", "weights_in", "msg_done", "summed", "added", "cleared")
        block = ctx.enter_context(nc.Block())

        @block.sync
        def _(sp):
            chunks = K.spill3.rearrange("(c e t) w -> e c t w", t=C, e=P)

            def body(it):
                for lane in range(LANES):
                    if (at := at_stage(it, lane, 0)) is not None:
                        c, l = at
                        if over0(c - LANES + 1):
                            sp.wait_ge(msg_done, c - LANES + 1)
                        sp.dma_start(far[:, l:l + 1, :, :], chunks[:, bass.ds(c, 1), :, :]).then_inc(far_in[l], 16)

            chunk_loop(sp, body)

        @block.scalar
        def _(act):
            def body(it):
                for lane in range(LANES):
                    if (at := at_stage(it, lane, 2)) is not None:
                        c, l = at
                        if over0(c - 1):
                            act.wait_ge(summed, c - 1)
                        nc.scalar.activation(msg[:, l % 2, :, D:M], weight[:, bass.ds(c * C, C), :], ACT.Copy
                                             ).then_inc(weights_in, 1)

            chunk_loop(act, body)

        @block.tensor
        def _(pe):
            def body(it):
                for lane in range(LANES):
                    if (at := at_stage(it, lane, 2)) is not None:
                        c, l = at
                        pe.wait_ge(hot, c + 1)
                        pe.wait_ge(msg_done, c + 1)
                        if over0(C * (c - 1)):
                            pe.wait_ge(added, C * (c - 1))
                        for i in range(C):
                            mm = pe.matmul(p_agg[:, l % 2, i, 0:M], S[:, l % 2, i, :], msg[:, l % 2, i, :],
                                           start=True, stop=True)
                        mm.then_inc(summed, 1)

            chunk_loop(pe, body)

        @block.vector
        def _(dve):
            regs = [dve.alloc_register(f"v3_dve{i}") for i in range(C)]
            dve.memset(agg[:], 0.0).then_inc(cleared, 1)
            dve.wait_ge(cleared, 1)

            def body(it):
                for lane in range(LANES):
                    if (at := at_stage(it, lane, 2)) is not None:
                        c, l = at
                        h = l % 2
                        if over0(c - 1):
                            dve.wait_ge(summed, c - 1)
                        ed.one_hot(dve, S[:, h], c).then_inc(hot, 1)
                        dve.wait_ge(weights_in, c + 1)
                        dve.wait_ge(far_in[l], 16 * lane_turn(it, lane, 2))
                        for i in range(C):
                            mm = dve.tensor_tensor(msg[:, h, i, 0:D].rearrange("p (h d) -> p h d", h=H),
                                                   far[:, l, i, :].rearrange("p (h d) -> p h d", h=H),
                                                   bc_last(msg[:, h, i, D:M], HD), ALU.mult)
                        mm.then_inc(msg_done, 1)
                    if (at := at_stage(it, lane, 3)) is not None:
                        c, l = at
                        add_to_blocks(dve, ed, regs, c, agg, p_agg[:, l % 2], M, summed, added)

            chunk_loop(dve, body)


def layer3(nc, K, x):
    with ExitStack() as ctx:
        sb, _ = ctx_tools(nc, ctx)
        logit = sb("logit3", [P, T, H])
        with ExitStack() as inner:
            q = inner.enter_context(nc.sbuf_tensor("q3", [P, B, D], F32))
            node_pass(nc, K, "n3", x, [(K.w("q3"), D, K.v("b_q3"), q),
                                            (K.w("kv3"), 2 * D, K.v("b_kv3"), (K.table3, 0, 2 * D))])
            edge_pass3a(nc, K, q, logit)
        cut_and_exp(nc, K, logit)
        agg = sb("agg3", [P, B, D + H])
        y, tmp = sb("y3", [P, B, D]), sb("tmp3", [P, B, D])
        edge_pass3b(nc, K, logit, agg)

        def divide(dve, link, scalar_step):
            link(dve.tensor_scalar(tmp[:, :, 0:H], agg[:, :, D:D + H], 1e-8, None, ALU.add))
            link(dve.reciprocal(tmp[:, :, 0:H], tmp[:, :, 0:H]))
            for h in range(H):
                link(dve.tensor_tensor(y[:, :, h * HD:(h + 1) * HD], agg[:, :, h * HD:(h + 1) * HD],
                                       bc_last(tmp[:, :, h], HD), ALU.mult))

        on_vector(nc, K, "f3a", divide)
        node_pass(nc, K, "n3o", y, [(K.w("o3"), D, K.v("b_o3"), tmp)])

        def finish(dve, link, scalar_step):
            link(dve.tensor_tensor(tmp[:], tmp[:], x[:], ALU.add))
            layer_norm(dve, link, scalar_step, K, tmp[:], y[:], K.v("ln_g"), K.v("ln_b"))
            link(dve.tensor_tensor(x[:], x[:], tmp[:], ALU.add))
            layer_norm(dve, link, scalar_step, K, x[:], y[:])

        on_vector(nc, K, "f3b", finish)


def layers(nc, top, K, io):
    x = top.enter_context(nc.sbuf_tensor("x", [P, B, D], F32))
    root = top.enter_context(nc.sbuf_tensor("root", [P, B], F32))
    load_x(nc, K, io, x)
    layer0(nc, K, x)
    layer1(nc, K, x, root)
    layer2(nc, K, x, root)
    layer3(nc, K, x)
    [stored] = Sems(nc, K.used_sems, "end")("stored")
    with nc.Block() as block:
        @block.sync
        def _(sp):
            sp.dma_start(io["out"], x[:].rearrange("p b d -> p (b d)")).then_inc(stored, 16)
            sp.wait_ge(stored, 16)



class Kept:

    def __init__(self, nc, ctx):
        def sb(name, shape, dt=F32):
            return ctx.enter_context(nc.sbuf_tensor(name, shape, dt))

        self.used_sems = []
        self.W, self.V = sb("weights", [P, NW]), sb("vectors", [P, NV])
        self.w_ef = sb("w_ef", [C * REC_S, C, 2 * D])
        self.w_len = sb("w_len", [C, C, D])
        self.lane_i, self.lane = sb("lane_i", [P, P], I32), sb("lane", [P, P])
        self.tile_i = sb("tile_i", [P, G], I32)
        self.ident, self.ones, self.before = sb("ident", [P, P]), sb("ones", [P, P]), sb("before", [P, P])
        self.key = {k: sb(f"key_{k}", [P, T]) for k in "sd"}
        self.other = {k: sb(f"other_{k}", [P, T], I32) for k in "sd"}
        self.blocks = {k: sb(f"blocks_{k}", [1, T], I32) for k in "sd"}
        self.length = sb("len_sorted", [P, T])
        self.stat = sb("stat", [P, 2, B])
        self.rec_s = nc.dram_tensor("rec_s", [T * P, REC_S], F32).ap()
        self.rec_d = nc.dram_tensor("rec_d", [T * P, REC_D], F32).ap()
        self.map_dram = {k: nc.dram_tensor(f"map_{k}", [P * G], I32).ap() for k in "sd"}
        self.table0 = nc.dram_tensor("table0", [NP, 2 * D], F32).ap()
        self.table1 = nc.dram_tensor("table1", [NP, D + H], F32).ap()
        self.table2 = [nc.dram_tensor(f"table2_{i}", [NP, D], F32).ap() for i in range(3)]
        self.table3 = nc.dram_tensor("table3", [NP, 2 * D], F32).ap()
        self.spill1 = nc.dram_tensor("spill1", [T * P, D + H], F32).ap()
        self.spill3 = nc.dram_tensor("spill3", [T * P, D], F32).ap()

    def w(self, name):
        a, b = W_COLS[name]
        return self.W[:, a:b]

    def v(self, name):
        a, b = V_COLS[name]
        return self.V[:, a:b]


IO = {"x": ([P, B * D], F32), "src": ([P, COLS], I32), "dst": ([P, COLS], I32), "ef": ([P, COLS * EF], F32),
      "length": ([P, COLS], F32), "weights": ([P, NW], F32), "vectors": ([P, NV], F32),
      "w_ef": ([C * REC_S, C, 2 * D], F32), "w_len": ([C, C, D], F32)}


def build(nc, io):
    ctx = ExitStack()
    with ctx:
        K = Kept(nc, ctx)
        load_and_sort(nc, K, io)
        load_orders(nc, K)
        layers(nc, ctx, K, io)


def lay_out(a):
    a = {k: np.asarray(v) for k, v in a.items()}

    def padded(v, rows, fill=0):
        out = np.full((rows, *v.shape[1:]), fill, v.dtype)
        out[:len(v)] = v
        return out

    out = {"x": padded(a["x"], NP).reshape(B, P, D).transpose(1, 0, 2).reshape(P, B * D)}
    for k in ("src", "dst"):
        out[k] = padded(a[k], P * COLS, NP).reshape(P, COLS)
    out["ef"] = padded(a["edge_attr_10"], P * COLS).reshape(P, COLS * EF)
    out["length"] = padded(a["edge_weight1"], P * COLS).reshape(P, COLS)
    gate, cand = a["L0_gnn_gate_w"], a["L0_gnn_cand_w"]
    both = np.concatenate([gate, cand], 1)
    W = np.zeros((P, NW), np.float32)
    for name, w in (("own0", both[0:D]), ("other0", both[D:2 * D]), ("in1", a["L1_gnn_w_in"]),
                    ("a1", np.concatenate([a["L1_gnn_w_au"], a["L1_gnn_w_av"]], 1)),
                    ("mlp1", a["L1_gnn_w1"]), ("mlp2", a["L1_gnn_w2"]),
                    ("g0", a["L2_gnn_W0"]), ("g1", a["L2_gnn_W1"]), ("g2", a["L2_gnn_W2"]),
                    ("q3", a["L3_gnn_Wq"].T), ("kv3", np.concatenate([a["L3_gnn_Wk"].T, a["L3_gnn_Wv"].T], 1)),
                    ("bias3", a["L3_gnn_We2"].T), ("o3", a["L3_gnn_Wo"].T), ("hid_b", a["L3_gnn_be1"][:, None])):
        lo, hi = W_COLS[name]
        W[:, lo:hi] = w
    V = np.zeros((P, NV), np.float32)
    zeros = np.zeros(H, np.float32)
    for name, v in (("b0", np.concatenate([a["L0_gnn_gate_b"], a["L0_gnn_cand_b"]])), ("b_in1", a["L1_gnn_b_in"]),
                    ("b_a1", np.concatenate([a["L1_gnn_b_au"], zeros])), ("b_mlp1", a["L1_gnn_b1"]),
                    ("b_mlp2", a["L1_gnn_b2"]), ("b_g0", a["L2_gnn_b0"]), ("b_g1", a["L2_gnn_b1"]),
                    ("b_g2", a["L2_gnn_b2"]), ("b_q3", a["L3_gnn_bq"]),
                    ("b_kv3", np.concatenate([a["L3_gnn_bk"], a["L3_gnn_bv"]])), ("b_bias3", a["L3_gnn_be2"]),
                    ("b_o3", a["L3_gnn_bo"]), ("bn_g", a["L0_gnn_bn_gamma"]), ("bn_b", a["L0_gnn_bn_beta"]),
                    ("ln_g", a["L3_gnn_ln_g"]), ("ln_b", a["L3_gnn_ln_b"])):
        lo, hi = V_COLS[name]
        V[:, lo:hi] = v[None, :]
    out["weights"], out["vectors"] = W, V
    w_ef = np.zeros((C * REC_S, C, 2 * D), np.float32)
    w_len = np.zeros((C, C, D), np.float32)
    for i in range(C):
        w_ef[i * REC_S + 2:i * REC_S + 2 + EF, i] = both[2 * D:]
        w_len[i, i] = a["L3_gnn_We1"][:, 0]
    out["w_ef"], out["w_len"] = w_ef, w_len
    return {k: np.ascontiguousarray(v) for k, v in out.items()}


def kernel(**inputs):
    import concourse.bacc as bacc
    from concourse.bass_utils import run_bass_kernel_spmd

    nc = bacc.Bacc("TRN2", target_bir_lowering=False, num_devices=1)
    arrays = {f"in_{k}": v for k, v in lay_out(inputs).items()}
    io = {k: nc.dram_tensor(f"in_{k}", shape, dt, kind="ExternalInput").ap() for k, (shape, dt) in IO.items()}
    io["out"] = nc.dram_tensor("out", [P, B * D], F32, kind="ExternalOutput").ap()
    build(nc, io)
    got = run_bass_kernel_spmd(nc, [arrays], core_ids=[0]).results[0]["out"]
    return np.ascontiguousarray(got.reshape(P, B, D).transpose(1, 0, 2).reshape(NP, D)[:N])
```

```python
from contextlib import ExitStack

import numpy as np

import concourse.bass as bass
from concourse import mybir

F32 = mybir.dt.float32
I32 = mybir.dt.int32
BF16 = mybir.dt.bfloat16
ALU = mybir.AluOpType
ACT = mybir.ActivationFunctionType
AX = mybir.AxisListType

P = 128
N = 6250
E = 100000
D = 128
H = 8
HD = D // H
EF = 10
B = -(-N // P)
NP = B * P
LAST = N - (B - 1) * P
COLS = -(-E // P)
C = 4
LANES = 4
T = COLS + B
T = -(-T // (C * LANES)) * C * LANES
NCH = T // C
ITERS = NCH // LANES
REC_S = 2 + EF + 1
PARTS = 64
FEAT_PARTS = (0, 0, 0, 1, 1, 2)
WEIGHT_PARTS = (0, 1, 2, 0, 1, 0)
REC_D = 2
G = 7
NG = B // G
SG = 17
NSG = COLS // SG
BIG = 1.0e30
CUTOFF = 5.0
EXP_LN_SET = "natural_log_exp_and_others"
assert B % G == 0 and COLS % SG == 0 and NSG % 2 == 0 and NCH % LANES == 0

W_COLS, V_COLS = {}, {}


def _place(table, items):
    at = 0
    for name, n in items:
        table[name] = (at, at + n)
        at += n
    return at


NW = _place(W_COLS, [("own0", 256), ("other0", 256), ("in1", D), ("a1", 2 * H), ("mlp1", D), ("mlp2", D),
                     ("g0", D), ("g1", D), ("g2", D), ("q3", D), ("kv3", 2 * D), ("bias3", H), ("o3", D),
                     ("hid_b", 1)])
NV = _place(V_COLS, [("b0", 256), ("b_in1", D), ("b_a1", 2 * H), ("b_mlp1", D), ("b_mlp2", D), ("b_g0", D),
                     ("b_g1", D), ("b_g2", D), ("b_q3", D), ("b_kv3", 2 * D), ("b_bias3", H), ("b_o3", D),
                     ("bn_g", D), ("bn_b", D), ("ln_g", D), ("ln_b", D)])


def over0(v):
    return not isinstance(v, int) or v > 0


def ctx_tools(nc, ctx):
    def sb(name, shape, dt=F32):
        return ctx.enter_context(nc.sbuf_tensor(name, shape, dt))

    def ps(name, shape, dt=F32):
        return ctx.enter_context(nc.psum_tensor(name, shape, dt))

    return sb, ps


def bc_mid(ap, n):
    return ap.unsqueeze(1).to_broadcast([ap.shape[0], n, ap.shape[1]])


def bc_last(ap, n):
    return ap.unsqueeze(len(ap.shape)).to_broadcast([*ap.shape, n])


def chunk_loop(eng, body, peel=2):
    for it in range(peel):
        body(it)
    with eng.Fori(peel, ITERS) as it:
        body(it)
    for it in range(ITERS, ITERS + 2):
        body(it)


def at_stage(it, lane, lag):
    if isinstance(it, int):
        c = LANES * it + lane - lag
        return (c, c % LANES) if 0 <= c < NCH else None
    return it * LANES + (lane - lag), (lane - lag) % LANES


class Sems:

    MOST = 110

    def __init__(self, nc, used, stage):
        if len(used) > self.MOST:
            nc.clear_and_free_semaphores(used)
            nc.all_engine_barrier()
            used.clear()
        self.nc, self.used, self.stage = nc, used, stage

    def __call__(self, *names):
        sems = [self.nc.alloc_semaphore(f"{self.stage}_{n}") for n in names]
        self.used.extend(sems)
        return sems



def load_and_sort(nc, K, io, late, x):
    ctx = ExitStack()
    with ctx:
        sb, ps = ctx_tools(nc, ctx)
        key = {"s": sb("src_i", [P, COLS], I32), "d": sb("dst_i", [P, COLS], I32)}
        whole = {"s": sb("src_f", [P, COLS]), "d": sb("dst_f", [P, COLS])}
        local = {"s": sb("src_local", [P, COLS]), "d": sb("dst_local", [P, COLS])}
        pos = {"s": sb("src_pos", [P, COLS]), "d": sb("dst_pos", [P, T])}
        pos_i = {"s": sb("src_pos_i", [P, COLS], I32), "d": late.pos}
        blk = sb("blk", [P, COLS])
        mask = sb("mask", [P, COLS])
        rank = sb("rank", [P, COLS])
        feats = sb("feats", [P, COLS, EF])
        length = sb("length", [P, COLS])
        w_ef, part = sb("w_ef", [P, 2 * D]), sb("part", [P, 5])
        lane_i, tile_i, col_i = sb("lane_i", [P, P], I32), sb("tile_i", [P, G], I32), sb("col_i", [P, 1], I32)
        before = sb("before", [P, P])
        ef_parts = sb("ef_parts", [P, 3, 2 * D])
        cnt = sb("cnt", [P, B])
        few = sb("few", [P, 6, B])
        few_i = sb("few_i", [P, B], I32)
        tile_no = sb("tile_no", [P, G])
        past = sb("past", [P, G, B - 1])
        tb_f = sb("tb_f", [P, G])
        tb_i = {"s": sb("tb_s", [P, G], I32), "d": sb("tb_d", [P, G], I32)}
        pad = sb("pad", [P, 104, REC_S])
        pad_d = sb("pad_d", [P, 104, REC_D])
        stage_s = sb("stage_s", [P, 2, SG, REC_S])
        stage_i = sb("stage_i", [P, 2, SG], I32)
        p_cnt = {"s": ps("p_cnt_s", [P, 2, 64]), "d": ps("p_cnt_d", [P, 2, 64])}
        new = Sems(nc, K.used_sems, "sort")
        loaded, consts, chain, counted, summed = new("loaded", "consts", "chain", "counted", "summed")
        pads_set, pads_out, map_ready, map_out = new("pads_set", "pads_out", "map_ready", "map_out")
        pos_ready, gate, maps_in = new("pos_ready", "gate", "maps_in")
        staged, sent = new("staged0", "staged1"), new("sent0", "sent1")
        n_loads = 10
        recs = {"s": K.rec_s, "d": K.rec_d}
        block = ctx.enter_context(nc.Block())

        @block.sync
        def _(sp):
            sp.dma_start(key["s"][:], io["src"]).then_inc(loaded, 16)
            sp.dma_start(key["d"][:], io["dst"]).then_inc(loaded, 16)
            sp.dma_start(x[:].rearrange("p b d -> p (b d)"), io["x"]).then_inc(loaded, 16)
            sp.dma_start(feats[:].rearrange("p a b -> p (a b)"), io["ef"]).then_inc(loaded, 16)
            sp.dma_start(length[:], io["length"]).then_inc(loaded, 16)
            sp.dma_start(K.W[:], io["weights"]).then_inc(loaded, 16)
            sp.dma_start(K.V[:], io["vectors"]).then_inc(loaded, 16)
            sp.dma_start(w_ef[:], io["w_ef"]).then_inc(loaded, 16)
            sp.dma_start(K.w_len[:], io["w_len"]).then_inc(loaded, 16)
            sp.dma_start(part[:], io["part"]).then_inc(loaded, 16)
            sp.wait_ge(pads_set, 3)
            for k, src in (("s", pad), ("d", pad_d)):
                words = recs[k].shape[1]
                rows = recs[k].rearrange("(a p n) w -> a p (n w)", p=P, n=104)
                for a in range(T // 104):
                    sp.dma_start(rows[a], src[:].rearrange("p n w -> p (n w)")).then_inc(pads_out, 16)
            for n, k in enumerate("sd"):
                sp.wait_ge(map_ready, n + 1)
                sp.dma_start(K.map_dram[k].rearrange("(p n) -> p n", p=P), tb_i[k][:]).then_inc(map_out, 16)
                sp.wait_ge(map_out, 16 * (n + 1))
                sp.dma_start(K.blocks[k][0:1, :], K.map_dram[k][0:T].unsqueeze(0)).then_inc(maps_in, 16)
            sp.wait_ge(maps_in, 32)

        @block.gpsimd
        def _(pool):
            pool.iota(lane_i[:], pattern=[[1, P]], base=0, channel_multiplier=0).then_inc(consts, 1)
            pool.iota(tile_i[:], pattern=[[1, G]], base=0, channel_multiplier=G).then_inc(consts, 1)
            pool.iota(col_i[:], pattern=[[0, 1]], base=0, channel_multiplier=1).then_inc(consts, 1)
            pool.memset(K.ident[:], 0.0).then_inc(consts, 1)
            pool.memset(K.ones[:], 1.0).then_inc(consts, 1)
            pool.memset(pad[:].rearrange("p n w -> p (n w)"), 0.0).then_inc(pads_set, 1)
            pool.memset(pad_d[:].rearrange("p n w -> p (n w)"), 0.0).then_inc(pads_set, 1)
            pool.wait_ge(consts, 5)
            pool.affine_select(out=K.ident[:], in_=K.ident[:], compare_op=ALU.not_equal, fill=1.0, base=0,
                               pattern=[[-1, P]], channel_multiplier=1).then_inc(consts, 1)
            pool.affine_select(out=before[:], in_=K.ones[:], compare_op=ALU.is_gt, fill=0.0, base=0,
                               pattern=[[1, P]], channel_multiplier=-1).then_inc(consts, 1)
            pool.wait_ge(pads_out, 2 * 16 * (T // 104))

            def scatter(it):
                for half in range(2):
                    pool.wait_ge(staged[half], 1 * (it + 1))
                    pool.sem_inc(gate, 1)
                    for j in range(SG):
                        pool.indirect_dma_start(
                            K.rec_s, bass.IndirectOffsetOnAxis(ap=stage_i[:, half, j:j + 1], axis=0),
                            stage_s[:, half, j, :], None,
                            bounds_check=T * P - 1, oob_is_err=False).then_inc(sent[half], 16)

            scatter(0)
            with pool.Fori(1, NSG // 2) as it:
                scatter(it)
            for half in range(2):
                pool.wait_ge(sent[half], 16 * SG * (NSG // 2))

        @block.scalar
        def _(act):
            act.wait_ge(loaded, 16 * n_loads)
            act.wait_ge(pos_ready, 1)

            def fill(it):
                for half in range(2):
                    cols = bass.ds((it * 2 + half) * SG, SG)
                    if over0(it):
                        act.wait_ge(sent[half], 16 * SG * it)
                    dst = stage_s[:, half]
                    nc.scalar.activation(stage_i[:, half, :], pos_i["s"][:, cols], ACT.Copy)
                    nc.scalar.activation(dst[:, :, 0], local["s"][:, cols], ACT.Copy)
                    nc.scalar.activation(dst[:, :, 1], whole["d"][:, cols], ACT.Copy)
                    nc.scalar.activation(dst[:, :, 2:2 + EF], feats[:, cols, :], ACT.Copy)
                    nc.scalar.activation(dst[:, :, 2 + EF], length[:, cols], ACT.Copy).then_inc(staged[half], 1)

            fill(0)
            with act.Fori(1, NSG // 2) as it:
                fill(it)

        @block.tensor
        def _(pe):
            pe.wait_ge(consts, 7)
            for n, k in enumerate("sd"):
                pe.wait_ge(counted, n + 1)
                pe.matmul(p_cnt[k][:, 0, 0:B], K.ones[:], cnt[:], start=True, stop=True)
                pe.matmul(p_cnt[k][:, 1, 0:B], before[:], cnt[:], start=True, stop=True).then_inc(summed, 1)

        @block.vector
        def _(dve):
            count = [0]

            def link(ins):
                count[0] += 1
                ins.then_inc(chain, 1)
                dve.wait_ge(chain, count[0])

            dve.wait_ge(pads_set, 2)
            dve.memset(pad[:, :, 0], -1.0)
            dve.memset(pad_d[:, :, 0], -1.0).then_inc(pads_set, 1)
            dve.wait_ge(consts, 3)
            dve.tensor_copy(K.col[:], col_i[:])
            dve.tensor_copy(K.lane[:], lane_i[:])
            link(dve.tensor_copy(tile_no[:], tile_i[:]))
            dve.wait_ge(loaded, 16 * n_loads)
            high, rest, mid = (ef_parts[:, i, :] for i in range(3))
            dve.wait_ge(consts, 7)
            link(dve.tensor_copy(K.ident_bf[:], K.ident[:]))
            link(dve.tensor_copy(K.w_ef_parts[:, 0], w_ef[:]))
            link(dve.tensor_copy(high, K.w_ef_parts[:, 0]))
            link(dve.tensor_tensor(rest, w_ef[:], high, ALU.subtract))
            link(dve.tensor_copy(K.w_ef_parts[:, 0], rest))
            link(dve.tensor_copy(mid, K.w_ef_parts[:, 0]))
            link(dve.tensor_tensor(rest, rest, mid, ALU.subtract))
            link(dve.tensor_scalar(high, high, part[:, 0:1], None, ALU.mult))
            link(dve.scalar_tensor_tensor(out=high, in0=mid, scalar=part[:, 1:2], in1=high,
                                          op0=ALU.mult, op1=ALU.add))
            link(dve.scalar_tensor_tensor(out=high, in0=rest, scalar=part[:, 2:3], in1=high,
                                          op0=ALU.mult, op1=ALU.add))
            for tile in range(2):
                link(dve.tensor_scalar(K.w_ef_parts[:, tile], high, part[:, 3 + tile:4 + tile], None, ALU.mult))
            total, nt_end, nt, base, tend, junk = (few[:, i, :] for i in range(6))
            for n, k in enumerate("sd"):
                link(dve.tensor_copy(whole[k][:], key[k][:]))
                link(dve.tensor_scalar(key[k][:], key[k][:], 7, None, ALU.arith_shift_right))
                link(dve.tensor_copy(blk[:], key[k][:]))
                link(dve.scalar_tensor_tensor(out=local[k][:], in0=blk[:], scalar=-float(P), in1=whole[k][:],
                                              op0=ALU.mult, op1=ALU.add))
            for n, k in enumerate("sd"):
                if n == 1:
                    dve.wait_ge(summed, 1)
                link(dve.tensor_copy(blk[:], key[k][:]))
                with dve.Fori(0, B) as b:
                    dve.tensor_scalar(mask[:], blk[:], K.lane[:, bass.ds(b, 1)], None, ALU.is_equal, ALU.add,
                                      accum_out=cnt[:, bass.ds(b, 1)])
                    dve.drain()
                dve.drain().then_inc(counted, 1)
                dve.wait_ge(summed, n + 1)
                link(dve.tensor_copy(total, p_cnt[k][:, 0, 0:B]))
                link(dve.tensor_scalar(few_i[:], total, float(P - 1), None, ALU.add))
                link(dve.tensor_scalar(few_i[:], few_i[:], 7, None, ALU.arith_shift_right))
                link(dve.tensor_copy(nt, few_i[:]))
                link(dve.tensor_tensor_scan(tend, nt, nt, 0.0, ALU.add, ALU.max))
                link(dve.tensor_tensor(nt_end, tend, nt, ALU.subtract))
                link(dve.scalar_tensor_tensor(out=base, in0=nt_end, scalar=float(P), in1=p_cnt[k][:, 1, 0:B],
                                              op0=ALU.mult, op1=ALU.add))
                link(dve.tensor_tensor(past[:], bc_last(tile_no[:], B - 1), bc_mid(tend[:, 0:B - 1], G), ALU.is_ge))
                link(dve.tensor_reduce(tb_f[:], past[:], AX.X, ALU.add))
                link(dve.tensor_copy(tb_i[k][:], tb_f[:]))
                dve.sem_inc(map_ready, 1)
                link(dve.memset(pos[k][:], float(1 << 22)))
                with dve.Fori(0, B) as b:
                    dve.tensor_scalar(mask[:], blk[:], K.lane[:, bass.ds(b, 1)], None, ALU.is_equal)
                    dve.drain()
                    dve.tensor_tensor_scan(rank[:], mask[:], mask[:], base[:, bass.ds(b, 1)], ALU.add, ALU.max)
                    dve.drain()
                    dve.copy_predicated(pos[k][:, 0:COLS], mask[:].bitcast(I32), rank[:])
                    dve.drain()
                link(dve.tensor_scalar(pos_i[k][:], pos[k][:], -1.0, None, ALU.add))
                dve.sem_inc(pos_ready, 1)
            link(dve.memset(late.rec[:], -1.0))
            link(dve.tensor_copy(late.rec[:, 0:COLS, 0], local["d"][:]))
            link(dve.tensor_copy(late.rec[:, 0:COLS, 1], whole["s"][:]))


def load_order(nc, K, k):
    ctx = ExitStack()
    with ctx:
        sb, ps = ctx_tools(nc, ctx)
        groups = [(g * P, min(P, T - g * P)) for g in range(-(-T // P))]
        words = REC_S if k == "s" else REC_D
        rec = K.rec_s if k == "s" else K.rec_d
        rows = sb(f"rows_{k}", [P, 2, P * words])
        key_rows, len_rows = sb(f"key_rows_{k}", [P, 2, P], BF16), sb(f"len_rows_{k}", [P, 2, P])
        turned = ps(f"turned_{k}", [P, 2, 4, P])
        new = Sems(nc, K.used_sems, f"order_{k}")
        row_in = new("row_in0", "row_in1")
        turned_in, copied, rows_set = new("turned", "copied", "rows_set")
        key_out, len_out = new("key_out0", "key_out1"), new("len_out0", "len_out1")
        block = ctx.enter_context(nc.Block())

        @block.sync
        def _(sp):
            for n, (t0, nt) in enumerate(groups):
                if n >= 2:
                    sp.wait_ge(turned_in, n - 1)
                    sp.wait_ge(rows_set, n - 1)
                sp.dma_start(rows[0:nt, n % 2, 0:P * words],
                             rec[t0 * P:(t0 + nt) * P, :].rearrange("(t e) w -> t (e w)", e=P)).then_inc(row_in[n % 2], 16)

        @block.tensor
        def _(pe):
            for n, (t0, nt) in enumerate(groups):
                pe.wait_ge(row_in[n % 2], 16 * (n // 2 + 1))
                if n >= 2:
                    pe.wait_ge(copied, n - 1)
                v = rows[0:nt, n % 2, 0:P * words].rearrange("t (e w) -> t w e", w=words)
                for i, w in enumerate([0, 1, REC_S - 1][:3 if k == "s" else 2]):
                    mm = pe.transpose(turned[:, n % 2, i, 0:nt], v[:, w, :], K.ident[0:nt, 0:nt])
                mm.then_inc(turned_in, 1)

        @block.vector
        def _(dve):
            for n, (t0, nt) in enumerate(groups):
                dve.wait_ge(turned_in, n + 1)
                dve.tensor_copy(K.key[k][:, t0:t0 + nt], turned[:, n % 2, 0, 0:nt])
                last = dve.tensor_copy(K.other[k][:, t0:t0 + nt], turned[:, n % 2, 1, 0:nt])
                if k == "s":
                    last = dve.tensor_copy(K.length[:, t0:t0 + nt], turned[:, n % 2, 2, 0:nt])
                last.then_inc(copied, 1)

        @block.scalar
        def _(act):
            for n, (t0, nt) in enumerate(groups):
                act.wait_ge(row_in[n % 2], 16 * (n // 2 + 1))
                if n >= 2:
                    act.wait_ge(key_out[n % 2], 16 * (n // 2))
                    if k == "s":
                        act.wait_ge(len_out[n % 2], 16 * (n // 2))
                v = rows[0:nt, n % 2, 0:P * words].rearrange("t (e w) -> t w e", w=words)
                last = nc.scalar.activation(key_rows[0:nt, n % 2, :], v[:, 0, :], ACT.Copy)
                if k == "s":
                    last = nc.scalar.activation(len_rows[0:nt, n % 2, :], v[:, REC_S - 1, :], ACT.Copy)
                last.then_inc(rows_set, 1)

        @block.gpsimd
        def _(pool):
            for n, (t0, nt) in enumerate(groups):
                pool.wait_ge(rows_set, n + 1)
                pool.dma_start(K.key_rows[k][t0:t0 + nt, :], key_rows[0:nt, n % 2, :]).then_inc(key_out[n % 2], 16)
                if k == "s":
                    pool.dma_start(K.len_rows[t0:t0 + nt, :], len_rows[0:nt, n % 2, :]).then_inc(len_out[n % 2], 16)
            for half in range(2):
                times = (len(groups) + 1 - half) // 2
                pool.wait_ge(key_out[half], 16 * times)
                if k == "s":
                    pool.wait_ge(len_out[half], 16 * times)



def node_pass(nc, K, stage, nodes, outs, clear=None):
    ctx = ExitStack()
    with ctx:
        sb, ps = ctx_tools(nc, ctx)
        group = sb(f"{stage}_group", [P, G, D])
        turned = sb(f"{stage}_turned", [P, G, P])
        result = sb(f"{stage}_result", [P, G, max(o[1] for o in outs)])
        p_turn = ps(f"{stage}_p_turn", [P, 2, 4, P])
        p_out = ps(f"{stage}_p_out", [P, 4, 512])
        new = Sems(nc, K.used_sems, stage)
        picked, turns, turned_in, product, taken, stored = new(
            "picked", "turns", "turned_in", "product", "taken", "stored")
        n_out = len(outs)
        drams = [i for i, o in enumerate(outs) if isinstance(o[3], tuple)]
        slot = {128: 128, 256: 256}
        block = ctx.enter_context(nc.Block())

        def product_of(n, i):
            per = 512 // n if n >= 128 else 4
            return p_out[:, i // per, (i % per) * n:(i % per) * n + n]

        @block.scalar
        def _(act):
            def body(it):
                if over0(it):
                    act.wait_ge(turns, it)
                nc.scalar.activation(group[:], nodes[:, bass.ds(it * G, G), :], ACT.Copy).then_inc(picked, 1)
                act.wait_ge(turns, it + 1)
                if over0(it):
                    act.wait_ge(product, it * n_out)
                nc.scalar.activation(turned[:, 0:4, :], p_turn[:, 0, :, :], ACT.Copy)
                nc.scalar.activation(turned[:, 4:G, :], p_turn[:, 1, 0:G - 4, :], ACT.Copy).then_inc(turned_in, 1)

            body(0)
            with act.Fori(1, NG) as it:
                body(it)

        @block.tensor
        def _(pe):
            def body(it):
                pe.wait_ge(picked, it + 1)
                if over0(it):
                    pe.wait_ge(turned_in, it)
                for i in range(G):
                    mm = pe.transpose(p_turn[:, i // 4, i % 4, :], group[:, i, :], K.ident[:])
                mm.then_inc(turns, 1)
                pe.wait_ge(turned_in, it + 1)
                for o, (w, n, _, _) in enumerate(outs):
                    if over0(it * n_out + o):
                        pe.wait_ge(taken, it * n_out + o)
                    for i in range(G):
                        mm = pe.matmul(product_of(n, i), turned[:, i, :], w, start=True, stop=True)
                    mm.then_inc(product, 1)

            body(0)
            with pe.Fori(1, NG) as it:
                body(it)

        @block.gpsimd
        def _(pool):
            if clear is not None:
                pool.memset(clear[:], 0.0)

        @block.vector
        def _(dve):
            def body(it):
                for o, (_, n, bias, target) in enumerate(outs):
                    dve.wait_ge(product, it * n_out + o + 1)
                    if o in drams:
                        before = it * len(drams) + drams.index(o)
                        if over0(before):
                            dve.wait_ge(stored, before * 16)
                    per = 512 // n if n >= 128 else 4
                    for a in range(0, G, per):
                        m = min(per, G - a)
                        p = p_out[:, a // per, 0:m * n].rearrange("p (m n) -> p m n", n=n)
                        dst = result[:, a:a + m, 0:n] if o in drams else target[:, bass.ds(it * G + a, m), 0:n]
                        if bias is None:
                            last = dve.tensor_copy(dst, p)
                        else:
                            last = dve.tensor_tensor(dst, p, bc_mid(bias, m), ALU.add)
                    last.then_inc(taken, 1)

            body(0)
            with dve.Fori(1, NG) as it:
                body(it)

        @block.sync
        def _(sp):
            def body(it):
                for o in drams:
                    table, col, width = outs[o][3]
                    sp.wait_ge(taken, it * n_out + o + 1)
                    rows = table.rearrange("(b n) f -> n b f", n=P)
                    sp.dma_start(rows[:, bass.ds(it * G, G), col:col + width], result[:, :, 0:width]).then_inc(stored, 16)

            if drams:
                body(0)
                with sp.Fori(1, NG) as it:
                    body(it)
                sp.wait_ge(stored, 16 * NG * len(drams))


def on_vector(nc, K, stage, program):
    with ExitStack() as ctx:
        new = Sems(nc, K.used_sems, stage)
        chain, asked, answered = new("chain", "asked", "answered")
        block = ctx.enter_context(nc.Block())
        todo = []

        @block.vector
        def _(dve):
            count = [0]

            def link(ins):
                count[0] += 1
                ins.then_inc(chain, 1)
                dve.wait_ge(chain, count[0])

            def scalar_step(out, in_, func, **kw):
                todo.append((out, in_, func, kw))
                dve.sem_inc(asked, 1)
                dve.wait_ge(answered, len(todo))

            program(dve, link, scalar_step)

        @block.scalar
        def _(act):
            for n, (out, in_, func, kw) in enumerate(todo):
                act.wait_ge(asked, n + 1)
                nc.scalar.activation(out, in_, func, **kw).then_inc(answered, 1)


def layer_norm(dve, link, scalar_step, K, t, tmp, scale=None, shift=None):
    mean, var = K.stat[:, 0, :], K.stat[:, 1, :]
    link(dve.tensor_reduce(mean, t, AX.X, ALU.add))
    link(dve.tensor_scalar(mean, mean, 1.0 / D, None, ALU.mult))
    link(dve.tensor_tensor(t, t, bc_last(mean, D), ALU.subtract))
    link(dve.tensor_tensor(tmp, t, t, ALU.mult))
    link(dve.tensor_reduce(var, tmp, AX.X, ALU.add))
    link(dve.tensor_scalar(var, var, 1.0 / D, 1e-5, ALU.mult, ALU.add))
    scalar_step(mean, var, ACT.Sqrt)
    link(dve.reciprocal(var, mean))
    link(dve.tensor_tensor(t, t, bc_last(var, D), ALU.mult))
    if scale is not None:
        link(dve.tensor_tensor(t, t, bc_mid(scale, B), ALU.mult))
        link(dve.tensor_tensor(t, t, bc_mid(shift, B), ALU.add))



class Edges:

    def __init__(self, nc, K, k):
        self.nc, self.K, self.k = nc, K, k

    def pick_others(self, act, out, c):
        return self.nc.scalar.activation(out, self.K.other[self.k][:, bass.ds(c * C, C)], ACT.Copy)

    def one_hot(self, dve, out, c):
        keys = self.K.key[self.k][:, bass.ds(c * C, C)]
        return dve.tensor_tensor(out, bc_mid(self.K.lane[:], C), bc_last(keys, P), ALU.is_equal)

    def load_rows(self, sp, out, c):
        rows = self.K.key_rows[self.k].rearrange("t e -> (t e)")[bass.ds(c * (C * P), C * P)]
        return sp.dma_start(out, rows.unsqueeze(0).to_broadcast([P, C * P]))

    def hot_nodes(self, dve, out, rows):
        return dve.tensor_scalar(out, rows, self.K.col[:, 0:1], None, ALU.is_equal)

    def block_values(self, eng, regs, c):
        eng.load(regs, self.K.blocks[self.k][0:1, bass.ds(c * C, C)])
        return [eng.snap(r, min_val=0, max_val=B - 1) for r in regs]


def edge_pass0(nc, K, own, agg, late):
    ctx = ExitStack()
    with ctx:
        sb, ps = ctx_tools(nc, ctx)
        ed = Edges(nc, K, "s")
        idx = sb("e0_idx", [P, LANES, C], I32)
        far = sb("e0_far", [P, LANES, C, 2 * D])
        rec = sb("e0_rec", [P, LANES, C * REC_S])
        S = sb("e0_S", [P, 4, C, P])
        rows = sb("e0_rows", [P, LANES, C * P], BF16)
        ST = sb("e0_ST", [P, 2, C * P])
        parts = sb("e0_parts", [P, 2, C, PARTS], BF16)
        rest = sb("e0_rest", [P, 2, C, EF])
        FT = sb("e0_FT", [P, 2, C // 2, P], BF16)
        z = sb("e0_z", [P, 2, C, 2 * D])
        soft = sb("e0_soft", [P, 2, C, 2 * D])
        low = sb("e0_low", [P, 2, C, D])
        late_i = sb("e0_late_i", [P, 2, C], I32)
        late_rec = sb("e0_late_rec", [P, 2, C, REC_D])
        p_feat = ps("e0_p_feat", [P, 2, C // 2, 4 * P], BF16)
        p_z = ps("e0_p_z", [P, 2, C, 2 * D])
        p_agg = ps("e0_p_agg", [P, 2, C, D])
        new = Sems(nc, K.used_sems, "e0")
        picked, gate = new("picked", "gate")
        rows_in = new("row_in0", "row_in1", "row_in2", "row_in3")
        recs_in = new("rec_in0", "rec_in1", "rec_in2", "rec_in3")
        far_in = new("far_in0", "far_in1", "far_in2", "far_in3")
        hot, turned, kept, z_done, z_read, abs_done, exp_done, ln_done = new(
            "hot", "turned", "kept", "z_done", "z_read", "abs_done", "exp_done", "ln_done")
        turned_hot, split, split_steps, cleared = new("turned_hot", "split", "split_steps", "cleared")
        halves, sig_done, msg_done, summed, added = new("halves", "sig_done", "msg_done", "summed", "added")
        late_set = new("late_set")[0]
        late_out = new("late_out0", "late_out1")
        block = ctx.enter_context(nc.Block())

        @block.gpsimd
        def _(pool):
            def body(it):
                for lane in range(LANES):
                    if (at := at_stage(it, lane, 0)) is not None:
                        c, l = at
                        pool.wait_ge(picked, c + 1)
                        if over0(c - LANES + 1):
                            pool.wait_ge(z_read, c - LANES + 1)
                        pool.sem_inc(gate, 1)
                        for i in range(C):
                            pool.indirect_dma_start(far[:, l, i, :], None, K.table0,
                                                    bass.IndirectOffsetOnAxis(ap=idx[:, l, i:i + 1], axis=0)
                                                    ).then_inc(far_in[l], 16)
                        pool.wait_ge(late_set, c + 1)
                        pool.sem_inc(gate, 1)
                        for i in range(C):
                            pool.indirect_dma_start(
                                K.rec_d, bass.IndirectOffsetOnAxis(ap=late_i[:, l % 2, i:i + 1], axis=0),
                                late_rec[:, l % 2, i, :], None,
                                bounds_check=T * P - 1, oob_is_err=False).then_inc(late_out[l % 2], 16)

            chunk_loop(pool, body)
            for half in range(2):
                pool.wait_ge(late_out[half], 16 * C * NCH // 2)

        @block.sync
        def _(sp):
            chunks = K.rec_s.rearrange("(c t e) w -> e c t w", t=C, e=P)

            def body(it):
                for lane in range(LANES):
                    if (at := at_stage(it, lane, 0)) is not None:
                        c, l = at
                        if over0(c - LANES + 1):
                            sp.wait_ge(split, c - LANES + 1)
                            sp.wait_ge(turned_hot, c - LANES + 1)
                        ed.load_rows(sp, rows[:, l, :], c).then_inc(rows_in[l], 16)
                        sp.dma_start(rec[:, l, :].rearrange("p (o t w) -> p o t w", o=1, t=C),
                                     chunks[:, bass.ds(c, 1), :, :]).then_inc(recs_in[l], 16)

            chunk_loop(sp, body)

        @block.scalar
        def _(act):
            act.preload_act_table_set(EXP_LN_SET)

            def body(it):
                for lane in range(LANES):
                    if (at := at_stage(it, lane, 0)) is not None:
                        c, l = at
                        if over0(c - LANES + 1):
                            act.wait_ge(far_in[l], 64 * (lane_turn(it, lane, 0) - 1))
                        ed.pick_others(act, idx[:, l, :], c).then_inc(picked, 1)
                        if over0(c - 1):
                            act.wait_ge(late_out[l % 2], 16 * C * half_turns(it, lane))
                        nc.scalar.activation(late_i[:, l % 2, :], late.pos[:, bass.ds(c * C, C)], ACT.Copy)
                        nc.scalar.activation(late_rec[:, l % 2], late.rec[:, bass.ds(c * C, C), :], ACT.Copy
                                             ).then_inc(late_set, 1)
                    if (at := at_stage(it, lane, 2)) is not None:
                        c, l = at
                        act.wait_ge(turned, c + 1)
                        if over0(c - 1):
                            act.wait_ge(z_done, c - 1)
                        nc.scalar.activation(FT[:, l % 2], p_feat[:, l % 2, :, 0:P], ACT.Copy).then_inc(kept, 1)
                    if (at := at_stage(it, lane, 4)) is not None:
                        c, l = at
                        act.wait_ge(halves, c + 1)
                        nc.scalar.activation(low[:, l % 2], low[:, l % 2], ACT.Exp).then_inc(sig_done, 1)
                    if (at := at_stage(it, lane, 3)) is not None:
                        c, l = at
                        act.wait_ge(z_read, c + 1)
                        nc.scalar.activation(soft[:, l % 2], z[:, l % 2], ACT.Abs).then_inc(abs_done, 1)
                        act.wait_ge(abs_done, c + 1)
                        nc.scalar.activation(soft[:, l % 2], soft[:, l % 2], ACT.Exp, scale=-1.0).then_inc(exp_done, 1)
                        act.wait_ge(exp_done, c + 1)
                        nc.scalar.activation(soft[:, l % 2], soft[:, l % 2], ACT.Ln, bias=1.0).then_inc(ln_done, 1)

            chunk_loop(act, body)

        @block.tensor
        def _(pe):
            regs = [pe.alloc_register(f"e0_pe{i}") for i in range(C)]

            def body(it):
                for lane in range(LANES):
                    if (at := at_stage(it, lane, 2)) is not None:
                        c, l = at
                        pe.wait_ge(split, c + 1)
                        if over0(c - 1):
                            pe.wait_ge(kept, c - 1)
                        for j in range(C // 2):
                            mm = pe.transpose(p_feat[:, l % 2, j, 0:P],
                                              parts[:, l % 2, 2 * j:2 * j + 2, :].rearrange("p t w -> p (t w)"),
                                              K.ident_bf[:])
                        mm.then_inc(turned, 1)
                    if (at := at_stage(it, lane, 3)) is not None:
                        c, l = at
                        blocks = ed.block_values(pe, regs, c)
                        pe.wait_ge(kept, c + 1)
                        pe.wait_ge(turned_hot, c + 1)
                        if over0(c - 1):
                            pe.wait_ge(z_read, c - 1)
                        for i in range(C):
                            pe.matmul(p_z[:, l % 2, i, :], ST[:, l % 2, i * P:(i + 1) * P],
                                      own[:, bass.ds(blocks[i], 1), :], start=True, stop=False)
                            mm = pe.matmul(p_z[:, l % 2, i, :], FT[:, l % 2, i // 2, :],
                                           K.w_ef_parts[:, i % 2], start=False, stop=True)
                        mm.then_inc(z_done, 1)
                    if (at := at_stage(it, lane, 5)) is not None:
                        c, l = at
                        pe.wait_ge(hot, c + 1)
                        pe.wait_ge(msg_done, c + 1)
                        if over0(C * (c - 1)):
                            pe.wait_ge(added, C * (c - 1))
                        for i in range(C):
                            mm = pe.matmul(p_agg[:, l % 2, i, :], S[:, l, i, :], low[:, l % 2, i, :],
                                           start=True, stop=True)
                        mm.then_inc(summed, 1)

            chunk_loop(pe, body)

        @block.vector
        def _(dve):
            regs = [dve.alloc_register(f"e0_dve{i}") for i in range(C)]

            dve.memset(parts[:], 0.0).then_inc(cleared, 1)
            dve.wait_ge(cleared, 1)

            def body(it):
                for lane in range(LANES):
                    if (at := at_stage(it, lane, 1)) is not None:
                        c, l = at
                        h = l % 2
                        dve.wait_ge(recs_in[l], 16 * lane_turn(it, lane, 1))
                        if over0(c - 1):
                            dve.wait_ge(turned, c - 1)
                        feats = rec[:, l, :].rearrange("p (t w) -> p t w", w=REC_S)[:, :, 2:2 + EF]
                        high, mid, low_p = (parts[:, h, :, a * EF:b * EF] for a, b in ((0, 3), (3, 5), (5, 6)))
                        dve.tensor_copy(high.rearrange("p t (r f) -> p t r f", f=EF),
                                        feats.unsqueeze(2).to_broadcast([P, C, 3, EF])).then_inc(split_steps, 1)
                        dve.wait_ge(split_steps, 3 * c + 1)
                        dve.tensor_tensor(rest[:, h], feats, high[:, :, 0:EF], ALU.subtract).then_inc(split_steps, 1)
                        dve.wait_ge(split_steps, 3 * c + 2)
                        dve.tensor_copy(mid.rearrange("p t (r f) -> p t r f", f=EF),
                                        rest[:, h].unsqueeze(2).to_broadcast([P, C, 2, EF])).then_inc(split_steps, 1)
                        dve.wait_ge(split_steps, 3 * c + 3)
                        dve.tensor_tensor(low_p, rest[:, h], mid[:, :, 0:EF], ALU.subtract).then_inc(split, 1)
                    if (at := at_stage(it, lane, 2)) is not None:
                        c, l = at
                        if over0(c - LANES + 1):
                            dve.wait_ge(summed, c - LANES + 1)
                        ed.one_hot(dve, S[:, l], c).then_inc(hot, 1)
                        dve.wait_ge(rows_in[l], 16 * lane_turn(it, lane, 2))
                        if over0(c - 1):
                            dve.wait_ge(z_done, c - 1)
                        ed.hot_nodes(dve, ST[:, l % 2, :], rows[:, l, :]).then_inc(turned_hot, 1)
                    if (at := at_stage(it, lane, 4)) is not None:
                        c, l = at
                        dve.wait_ge(ln_done, c + 1)
                        if over0(c - 1):
                            dve.wait_ge(summed, c - 1)
                        dve.scalar_tensor_tensor(out=low[:, l % 2], in0=z[:, l % 2, :, 0:D], scalar=0.0,
                                                 in1=soft[:, l % 2, :, 0:D], op0=ALU.min, op1=ALU.subtract)
                        dve.scalar_tensor_tensor(out=z[:, l % 2, :, D:2 * D], in0=z[:, l % 2, :, D:2 * D], scalar=0.0,
                                                 in1=soft[:, l % 2, :, D:2 * D], op0=ALU.max, op1=ALU.add
                                                 ).then_inc(halves, 1)
                    if (at := at_stage(it, lane, 3)) is not None:
                        c, l = at
                        dve.wait_ge(z_done, c + 1)
                        dve.wait_ge(far_in[l], 64 * lane_turn(it, lane, 3))
                        dve.tensor_tensor(z[:, l % 2], p_z[:, l % 2], far[:, l], ALU.add).then_inc(z_read, 1)
                    if (at := at_stage(it, lane, 4)) is not None:
                        c, l = at
                        dve.wait_ge(sig_done, c + 1)
                        dve.tensor_tensor(low[:, l % 2], low[:, l % 2], z[:, l % 2, :, D:2 * D], ALU.mult).then_inc(msg_done, 1)
                    if (at := at_stage(it, lane, 5)) is not None:
                        c, l = at
                        add_to_blocks(dve, ed, regs, c, agg, p_agg[:, l % 2], D, summed, added)

            chunk_loop(dve, body)


def lane_turn(it, lane, lag):
    return (LANES * it + lane - lag) // LANES + 1 if isinstance(it, int) else it + (lane - lag) // LANES + 1


def half_turns(it, lane):
    return (LANES * it + lane) // 2


def add_to_blocks(dve, ed, regs, c, agg, p, n, summed, added):
    blocks = ed.block_values(dve, regs, c)
    dve.wait_ge(summed, c + 1)
    for i in range(C):
        if over0(C * c + i):
            dve.wait_ge(added, C * c + i)
        dst = agg[:, bass.ds(blocks[i], 1), 0:n]
        dve.tensor_tensor(dst, dst, p[:, i:i + 1, 0:n], ALU.add).then_inc(added, 1)


def layer0(nc, K, x, late):
    with ExitStack() as ctx:
        agg = ctx.enter_context(nc.sbuf_tensor("agg0", [P, B, D], F32))
        with ExitStack() as inner:
            own = inner.enter_context(nc.sbuf_tensor("own0", [P, B, 2 * D], F32))
            node_pass(nc, K, "n0", x, [(K.w("own0"), 2 * D, K.v("b0"), own),
                                            (K.w("other0"), 2 * D, None, (K.table0, 0, 2 * D))], clear=agg)
            edge_pass0(nc, K, own, agg, late)
        tmp = ctx.enter_context(nc.sbuf_tensor("tmp0", [P, B, D], F32))
        batch_norm(nc, K, agg, tmp)

        def program(dve, link, scalar_step):
            link(dve.tensor_tensor(agg[:], agg[:], bc_mid(K.v("bn_g"), B), ALU.mult))
            link(dve.tensor_tensor(agg[:], agg[:], bc_mid(K.v("bn_b"), B), ALU.add))
            link(dve.tensor_tensor(agg[:], agg[:], x[:], ALU.add))
            scalar_step(tmp[:], agg[:], ACT.Abs)
            scalar_step(tmp[:], tmp[:], ACT.Exp, scale=-1.0)
            scalar_step(tmp[:], tmp[:], ACT.Ln, bias=1.0)
            link(dve.scalar_tensor_tensor(out=agg[:], in0=agg[:], scalar=0.0, in1=tmp[:], op0=ALU.max, op1=ALU.add))
            link(dve.tensor_tensor(x[:], x[:], agg[:], ALU.add))
            layer_norm(dve, link, scalar_step, K, x[:], tmp[:])

        on_vector(nc, K, "f0", program)


def batch_norm(nc, K, agg, tmp):
    with ExitStack() as ctx:
        sb, ps = ctx_tools(nc, ctx)
        p_sum = ps("bn_p_sum", [P, 2, 512])
        mean, rstd = sb("bn_mean", [P, D]), sb("bn_rstd", [P, D])
        new = Sems(nc, K.used_sems, "bn")
        chain, mean_sum, squares, var_sum, asked, rooted = new("chain", "mean_sum", "squares", "var_sum", "asked", "rooted")
        block = ctx.enter_context(nc.Block())

        def column_sums(pe, bank, src, done):
            for b in range(B):
                rows = P if b < B - 1 else LAST
                mm = pe.matmul(p_sum[:, bank, 0:D], K.ones[0:rows, :], src[0:rows, b, :],
                               start=(b == 0), stop=(b == B - 1))
            mm.then_inc(done, 1)

        @block.tensor
        def _(pe):
            column_sums(pe, 0, agg, mean_sum)
            pe.wait_ge(squares, 1)
            column_sums(pe, 1, tmp, var_sum)

        @block.scalar
        def _(act):
            act.wait_ge(asked, 1)
            nc.scalar.activation(mean[:], rstd[:], ACT.Sqrt).then_inc(rooted, 1)

        @block.vector
        def _(dve):
            count = [0]

            def link(ins):
                count[0] += 1
                ins.then_inc(chain, 1)
                dve.wait_ge(chain, count[0])

            dve.wait_ge(mean_sum, 1)
            link(dve.tensor_scalar(mean[:], p_sum[:, 0, 0:D], 1.0 / N, None, ALU.mult))
            link(dve.tensor_tensor(agg[:], agg[:], bc_mid(mean[:], B), ALU.subtract))
            dve.tensor_tensor(tmp[:], agg[:], agg[:], ALU.mult).then_inc(squares, 1)
            dve.wait_ge(var_sum, 1)
            dve.tensor_scalar(rstd[:], p_sum[:, 1, 0:D], 1.0 / N, 1e-5, ALU.mult, ALU.add).then_inc(asked, 1)
            dve.wait_ge(rooted, 1)
            link(dve.reciprocal(rstd[:], mean[:]))
            link(dve.tensor_tensor(agg[:], agg[:], bc_mid(rstd[:], B), ALU.mult))



def edge_pass1a(nc, K, peak):
    ctx = ExitStack()
    with ctx:
        sb, ps = ctx_tools(nc, ctx)
        ed = Edges(nc, K, "d")
        R = C * H
        idx = sb("m1_idx", [P, LANES, C], I32)
        far = sb("m1_far", [P, LANES, C, D + H])
        S = sb("m1_S", [P, 2, C, P])
        a_u = sb("m1_au", [P, 2, C, H])
        keys = sb("m1_keys", [P, 2, C, H])
        same = sb("m1_same", [R, 2, P + 1])
        reset = sb("m1_reset", [R, 2, P])
        run = sb("m1_run", [R, 2, P])
        kt = sb("m1_kt", [R, 2, P])
        ends = sb("m1_ends", [R, 2, 2, P])
        back = sb("m1_back", [P, 2, 2, R])
        miss = sb("m1_miss", [P, 2, C, H])
        cand = sb("m1_cand", [P, 2, C, H])
        p_turn = ps("m1_p_turn", [R, 2, 2, 2 * P])
        p_back = ps("m1_p_back", [P, 2, 2, 4 * R * 2])
        p_max = ps("m1_p_max", [P, 2, C, 2 * P])
        new = Sems(nc, K.used_sems, "m1")
        picked, gate, spilled_all = new("picked", "gate", "spilled_all")
        far_in = new("far_in0", "far_in1", "far_in2", "far_in3")
        spilled = new("spilled0", "spilled1", "spilled2", "spilled3")
        hot, laid, turned, scanned, scan_steps, returned, copied, spread, maxed = new(
            "hot", "laid", "turned", "scanned", "scan_steps", "returned", "copied", "spread", "maxed")
        cleared, cand_steps, pe_gate = new("cleared", "cand_steps", "pe_gate")
        block = ctx.enter_context(nc.Block())

        @block.gpsimd
        def _(pool):
            def body(it):
                for lane in range(LANES):
                    if (at := at_stage(it, lane, 0)) is not None:
                        c, l = at
                        pool.wait_ge(picked, c + 1)
                        if over0(c - LANES + 1):
                            pool.wait_ge(laid, c - LANES + 1)
                            pool.wait_ge(spilled[l], 16 * (lane_turn(it, lane, 0) - 1))
                        pool.sem_inc(gate, 1)
                        for i in range(C):
                            pool.indirect_dma_start(far[:, l, i, :], None, K.table1,
                                                    bass.IndirectOffsetOnAxis(ap=idx[:, l, i:i + 1], axis=0)
                                                    ).then_inc(far_in[l], 16)

            chunk_loop(pool, body)

        @block.sync
        def _(sp):
            chunks = K.spill1.rearrange("(c e t) w -> e c t w", t=C, e=P)

            def body(it):
                for lane in range(LANES):
                    if (at := at_stage(it, lane, 2)) is not None:
                        c, l = at
                        sp.wait_ge(far_in[l], 64 * lane_turn(it, lane, 2))
                        sp.dma_start(chunks[:, bass.ds(c, 1), :, :].rearrange("e c t w -> e c (t w)"),
                                     far[:, l:l + 1, :, :].rearrange("p o t w -> p o (t w)")).then_inc(spilled[l], 16)

            chunk_loop(sp, body)
            for l in range(LANES):
                sp.wait_ge(spilled[l], 16 * ITERS)

        @block.scalar
        def _(act):
            def body(it):
                for lane in range(LANES):
                    if (at := at_stage(it, lane, 0)) is not None:
                        c, l = at
                        if over0(c - LANES + 1):
                            act.wait_ge(far_in[l], 64 * (lane_turn(it, lane, 0) - 1))
                        ed.pick_others(act, idx[:, l, :], c).then_inc(picked, 1)
                    if (at := at_stage(it, lane, 2)) is not None:
                        c, l = at
                        act.wait_ge(far_in[l], 64 * lane_turn(it, lane, 2))
                        if over0(c - 1):
                            act.wait_ge(turned, c - 1)
                        nc.scalar.activation(keys[:, l % 2], bc_last(K.key["d"][:, bass.ds(c * C, C)], H), ACT.Copy)
                        nc.scalar.activation(a_u[:, l % 2], far[:, l, :, D:D + H], ACT.Copy).then_inc(laid, 1)
                    if (at := at_stage(it, lane, 3)) is not None:
                        c, l = at
                        act.wait_ge(returned, c + 1)
                        if over0(c - 1):
                            act.wait_ge(spread, c - 1)
                        nc.scalar.activation(back[:, l % 2], p_back[:, l % 2, :, 0:R], ACT.Copy).then_inc(copied, 1)

            chunk_loop(act, body)

        @block.tensor
        def _(pe):
            def body(it):
                for lane in range(LANES):
                    if (at := at_stage(it, lane, 2)) is not None:
                        c, l = at
                        pe.wait_ge(laid, c + 1)
                        if over0(c - 1):
                            pe.wait_ge(scanned, c - 1)
                        pe.transpose(p_turn[:, l % 2, 0, 0:P], a_u[:, l % 2].rearrange("p t h -> p (t h)"), K.ident[:])
                        pe.transpose(p_turn[:, l % 2, 1, 0:P], keys[:, l % 2].rearrange("p t h -> p (t h)"), K.ident[:]
                                     ).then_inc(turned, 1)
                    if (at := at_stage(it, lane, 3)) is not None:
                        c, l = at
                        pe.wait_ge(scanned, c + 1)
                        if over0(c - 1):
                            pe.wait_ge(copied, c - 1)
                        pe.sem_inc(pe_gate, 1)
                        pe.transpose(p_back[:, l % 2, 0, 0:R], ends[:, l % 2, 0, :], K.ident[0:R, 0:R])
                        pe.transpose(p_back[:, l % 2, 1, 0:R], ends[:, l % 2, 1, :], K.ident[0:R, 0:R]).then_inc(returned, 1)
                    if (at := at_stage(it, lane, 4)) is not None:
                        c, l = at
                        pe.wait_ge(hot, c + 1)
                        pe.wait_ge(copied, c + 1)
                        if over0(c - 1):
                            pe.wait_ge(cand_steps, 2 * (c - 1))
                        for i in range(C):
                            mm = pe.matmul(p_max[:, l % 2, i, 0:2 * H],
                                           S[:, l % 2, i, :], back[:, l % 2, :, i * H:(i + 1) * H], start=True, stop=True)
                        mm.then_inc(spread, 1)

            chunk_loop(pe, body)

        @block.vector
        def _(dve):
            regs = [dve.alloc_register(f"m1_dve{i}") for i in range(C)]
            dve.memset(peak[:], -BIG).then_inc(cleared, 1)
            dve.memset(same[:], 0.0).then_inc(cleared, 1)
            dve.wait_ge(cleared, 2)

            def body(it):
                for lane in range(LANES):
                    if (at := at_stage(it, lane, 3)) is not None:
                        c, l = at
                        h = l % 2
                        dve.wait_ge(turned, c + 1)
                        if over0(c - 1):
                            dve.wait_ge(returned, c - 1)
                        dve.tensor_copy(kt[:, h, :], p_turn[:, h, 1, 0:P]).then_inc(scan_steps, 1)
                        dve.wait_ge(scan_steps, 4 * c + 1)
                        dve.tensor_tensor(same[:, h, 1:P], kt[:, h, 1:P], kt[:, h, 0:P - 1], ALU.is_equal
                                          ).then_inc(scan_steps, 1)
                        dve.wait_ge(scan_steps, 4 * c + 2)
                        dve.tensor_scalar(ends[:, h, 1, :], same[:, h, 1:P + 1], -1.0, 1.0, ALU.mult, ALU.add)
                        dve.tensor_scalar(reset[:, h, :], same[:, h, 0:P], -1.0, BIG, ALU.add, ALU.mult
                                          ).then_inc(scan_steps, 1)
                        dve.wait_ge(scan_steps, 4 * c + 3)
                        dve.tensor_tensor_scan(run[:, h, :], reset[:, h, :], p_turn[:, h, 0, 0:P], -BIG, ALU.add, ALU.max
                                               ).then_inc(scan_steps, 1)
                        dve.wait_ge(scan_steps, 4 * c + 4)
                        dve.tensor_tensor(ends[:, h, 0, :], run[:, h, :], ends[:, h, 1, :], ALU.mult).then_inc(scanned, 1)
                    if (at := at_stage(it, lane, 3)) is not None:
                        c, l = at
                        if over0(c - 1):
                            dve.wait_ge(spread, c - 1)
                        ed.one_hot(dve, S[:, l % 2], c).then_inc(hot, 1)
                    if (at := at_stage(it, lane, 5)) is not None:
                        c, l = at
                        h = l % 2
                        blocks = ed.block_values(dve, regs, c)
                        dve.wait_ge(spread, c + 1)
                        dve.tensor_scalar(miss[:, h], p_max[:, h, :, H:2 * H], -1.0, BIG, ALU.add, ALU.mult
                                          ).then_inc(cand_steps, 1)
                        dve.wait_ge(cand_steps, 2 * c + 1)
                        dve.tensor_tensor(cand[:, h], p_max[:, h, :, 0:H], miss[:, h], ALU.add).then_inc(cand_steps, 1)
                        dve.wait_ge(cand_steps, 2 * c + 2)
                        for i in range(C):
                            if over0(C * c + i):
                                dve.wait_ge(maxed, C * c + i)
                            dst = peak[:, bass.ds(blocks[i], 1), :]
                            dve.tensor_tensor(dst, dst, cand[:, h, i:i + 1, :], ALU.max).then_inc(maxed, 1)

            chunk_loop(dve, body)


def edge_pass1b(nc, K, own, agg):
    ctx = ExitStack()
    with ctx:
        sb, ps = ctx_tools(nc, ctx)
        ed = Edges(nc, K, "d")
        M = D + H + 1
        far = sb("a1_far", [P, LANES, C, D + H])
        S = sb("a1_S", [P, 4, C, P])
        rows = sb("a1_rows", [P, LANES, C * P], BF16)
        ST = sb("a1_ST", [P, 2, C * P], BF16)
        score = sb("a1_score", [P, 2, C, H])
        shifted = sb("a1_shifted", [P, 2, C, H])
        msg = sb("a1_msg", [P, 2, C, M])
        p_own = ps("a1_p_own", [P, 2, C, P])
        sums = sb("a1_sums", [P, 2, C, M])
        p_agg = ps("a1_p_agg", [P, 2, C, 2 * P])
        new = Sems(nc, K.used_sems, "a1")
        far_in = new("far_in0", "far_in1", "far_in2", "far_in3")
        rows_in = new("row_in0", "row_in1", "row_in2", "row_in3")
        hot, turned_hot, owned, steps, exped, msg_done, summed, added, cleared = new(
            "hot", "turned_hot", "owned", "steps", "exped", "msg_done", "summed", "added", "cleared")
        [agg_clear] = new("agg_clear")
        [sums_out] = new("sums_out")
        block = ctx.enter_context(nc.Block())

        @block.sync
        def _(sp):
            chunks = K.spill1.rearrange("(c e t) w -> e c t w", t=C, e=P)

            def body(it):
                for lane in range(LANES):
                    if (at := at_stage(it, lane, 0)) is not None:
                        c, l = at
                        if over0(c - LANES + 1):
                            sp.wait_ge(msg_done, c - LANES + 1)
                            sp.wait_ge(turned_hot, c - LANES + 1)
                        ed.load_rows(sp, rows[:, l, :], c).then_inc(rows_in[l], 16)
                        sp.dma_start(far[:, l:l + 1, :, :].rearrange("p o t w -> p o (t w)"),
                                     chunks[:, bass.ds(c, 1), :, :].rearrange("e c t w -> e c (t w)")
                                     ).then_inc(far_in[l], 16)

            chunk_loop(sp, body)

        @block.scalar
        def _(act):
            def body(it):
                for lane in range(LANES):
                    if (at := at_stage(it, lane, 3)) is not None:
                        c, l = at
                        act.wait_ge(steps, 4 * (c + 1))
                        if over0(c - 1):
                            act.wait_ge(summed, c - 1)
                        nc.scalar.activation(msg[:, l % 2, :, D:D + H], shifted[:, l % 2], ACT.Exp).then_inc(exped, 1)
                    if (at := at_stage(it, lane, 5)) is not None:
                        c, l = at
                        act.wait_ge(summed, c + 1)
                        if over0(C * (c - 1)):
                            act.wait_ge(added, C * (c - 1))
                        nc.scalar.activation(sums[:, l % 2], p_agg[:, l % 2, :, 0:M], ACT.Copy).then_inc(sums_out, 1)

            chunk_loop(act, body)

        @block.tensor
        def _(pe):
            regs = [pe.alloc_register(f"a1_pe{i}") for i in range(C)]

            def body(it):
                for lane in range(LANES):
                    if (at := at_stage(it, lane, 3)) is not None:
                        c, l = at
                        blocks = ed.block_values(pe, regs, c)
                        pe.wait_ge(turned_hot, c + 1)
                        if over0(c - 1):
                            pe.wait_ge(steps, 4 * (c - 1))
                        for i in range(C):
                            for part in range(3):
                                mm = pe.matmul(p_own[:, l % 2, i, 0:2 * H], ST[:, l % 2, i * P:(i + 1) * P],
                                               own[:, bass.ds(blocks[i], 1), part, :],
                                               start=(part == 0), stop=(part == 2))
                        mm.then_inc(owned, 1)
                    if (at := at_stage(it, lane, 5)) is not None:
                        c, l = at
                        pe.wait_ge(hot, c + 1)
                        pe.wait_ge(msg_done, c + 1)
                        if over0(c - 1):
                            pe.wait_ge(sums_out, c - 1)
                        for i in range(C):
                            mm = pe.matmul(p_agg[:, l % 2, i, 0:M], S[:, l, i, :], msg[:, l % 2, i, :],
                                           start=True, stop=True)
                        mm.then_inc(summed, 1)

            chunk_loop(pe, body)

        @block.vector
        def _(dve):
            dve.memset(msg[:], 1.0).then_inc(cleared, 1)
            dve.wait_ge(cleared, 1)

            def body(it):
                for lane in range(LANES):
                    if (at := at_stage(it, lane, 2)) is not None:
                        c, l = at
                        if over0(c - LANES + 1):
                            dve.wait_ge(summed, c - LANES + 1)
                        ed.one_hot(dve, S[:, l], c).then_inc(hot, 1)
                        dve.wait_ge(rows_in[l], 16 * lane_turn(it, lane, 2))
                        if over0(c - 1):
                            dve.wait_ge(owned, c - 1)
                        ed.hot_nodes(dve, ST[:, l % 2, :], rows[:, l, :]).then_inc(turned_hot, 1)
                    if (at := at_stage(it, lane, 3)) is not None:
                        c, l = at
                        h = l % 2
                        dve.wait_ge(owned, c + 1)
                        dve.wait_ge(far_in[l], 16 * lane_turn(it, lane, 3))
                        if over0(c - 1):
                            dve.wait_ge(exped, c - 1)
                        dve.tensor_tensor(score[:, h], p_own[:, h, :, 0:H], far[:, l, :, D:D + H], ALU.add
                                          ).then_inc(steps, 1)
                        dve.wait_ge(steps, 4 * c + 1)
                        dve.scalar_tensor_tensor(out=shifted[:, h], in0=score[:, h], scalar=0.2, in1=score[:, h],
                                                 op0=ALU.mult, op1=ALU.max).then_inc(steps, 1)
                        dve.wait_ge(steps, 4 * c + 2)
                        dve.tensor_tensor(score[:, h], shifted[:, h], p_own[:, h, :, H:2 * H], ALU.subtract
                                          ).then_inc(steps, 1)
                        dve.wait_ge(steps, 4 * c + 3)
                        dve.tensor_scalar(shifted[:, h], score[:, h], 0.0, None, ALU.min).then_inc(steps, 1)
                    if (at := at_stage(it, lane, 4)) is not None:
                        c, l = at
                        h = l % 2
                        dve.wait_ge(exped, c + 1)
                        ex = msg[:, h, :, D:D + H].unsqueeze(2).to_broadcast([P, C, HD, H])
                        dve.tensor_tensor(msg[:, h, :, 0:D].rearrange("p t (d h) -> p t d h", h=H),
                                          far[:, l, :, 0:D].rearrange("p t (d h) -> p t d h", h=H), ex, ALU.mult
                                          ).then_inc(msg_done, 1)

            chunk_loop(dve, body)

        @block.gpsimd
        def _(pool):
            regs = [pool.alloc_register(f"a1_pool{i}") for i in range(C)]
            pool.memset(agg[:], 0.0).then_inc(agg_clear, 1)
            pool.wait_ge(agg_clear, 1)

            def body(it):
                for lane in range(LANES):
                    if (at := at_stage(it, lane, 5)) is not None:
                        c, l = at
                        add_to_blocks(pool, ed, regs, c, agg, sums[:, l % 2], M, sums_out, added)

            chunk_loop(pool, body)


def layer1(nc, K, x, root):
    with ExitStack() as ctx:
        sb, _ = ctx_tools(nc, ctx)
        peak, own = sb("peak1", [P, B, H]), sb("own1", [P, B, 2 * H])
        with ExitStack() as inner:
            h = inner.enter_context(nc.sbuf_tensor("h1", [P, B, D], F32))
            node_pass(nc, K, "n1h", x, [(K.w("in1"), D, K.v("b_in1"), h)])
            node_pass(nc, K, "n1a", h, [(K.w("a1"), 2 * H, K.v("b_a1"), own),
                                             (K.w("a1"), 2 * H, K.v("b_a1"), (K.table1, D, H))])
            [out] = Sems(nc, K.used_sems, "h1")("out")
            with nc.Block() as block:
                @block.sync
                def _(sp):
                    rows = K.table1.rearrange("(b n) f -> n b f", n=P)
                    sp.dma_start(rows[:, :, 0:D], h[:]).then_inc(out, 16)
                    sp.wait_ge(out, 16)
        edge_pass1a(nc, K, peak)
        agg = sb("agg1", [P, B, D + H + 1])
        y, tmp = sb("y1", [P, B, D]), sb("tmp1", [P, B, D])

        def largest(dve, link, scalar_step):
            link(dve.tensor_copy(own[:, :, 0:H], own[:, :, H:2 * H]))
            link(dve.tensor_tensor(peak[:], peak[:], own[:, :, 0:H], ALU.add))
            link(dve.scalar_tensor_tensor(out=own[:, :, H:2 * H], in0=peak[:], scalar=0.2, in1=peak[:],
                                          op0=ALU.mult, op1=ALU.max))

        on_vector(nc, K, "f1a", largest)
        own_parts = sb("own1_parts", [P, B, 3, 2 * H], BF16)

        def split(dve, link, scalar_step):
            for part in range(3):
                link(dve.tensor_copy(own_parts[:, :, part, :], own[:]))
                if part < 2:
                    link(dve.tensor_tensor(own[:], own[:], own_parts[:, :, part, :], ALU.subtract))

        on_vector(nc, K, "f1s", split)
        edge_pass1b(nc, K, own_parts, agg)

        def divide(dve, link, scalar_step):
            link(dve.tensor_scalar(peak[:], agg[:, :, D:D + H], 1e-30, None, ALU.max))
            link(dve.reciprocal(peak[:], peak[:]))
            for b in range(HD):
                link(dve.tensor_tensor(y[:, :, b * H:(b + 1) * H], agg[:, :, b * H:(b + 1) * H], peak[:], ALU.mult))
            link(dve.tensor_scalar(root[:], agg[:, :, D + H], 1.0, None, ALU.add))
            scalar_step(K.stat[:, 0, :], root[:], ACT.Sqrt)
            link(dve.reciprocal(root[:], K.stat[:, 0, :]))

        on_vector(nc, K, "f1b", divide)
        node_pass(nc, K, "n1m", y, [(K.w("mlp1"), D, K.v("b_mlp1"), tmp)])

        def gelu(dve, link, scalar_step):
            scalar_step(y[:], tmp[:], ACT.Gelu_apprx_tanh)

        on_vector(nc, K, "f1c", gelu)
        node_pass(nc, K, "n1n", y, [(K.w("mlp2"), D, K.v("b_mlp2"), tmp)])

        def finish(dve, link, scalar_step):
            link(dve.tensor_tensor(x[:], x[:], tmp[:], ALU.add))
            layer_norm(dve, link, scalar_step, K, x[:], y[:])

        on_vector(nc, K, "f1d", finish)



def edge_pass2(nc, K, i_layer, agg):
    ctx = ExitStack()
    with ctx:
        sb, ps = ctx_tools(nc, ctx)
        ed = Edges(nc, K, "d")
        s = f"g{i_layer}"
        idx = sb(f"{s}_idx", [P, LANES, C], I32)
        far = sb(f"{s}_far", [P, LANES, C, D])
        S = sb(f"{s}_S", [P, 2, C, P])
        p_agg = ps(f"{s}_p_agg", [P, 2, C, D])
        new = Sems(nc, K.used_sems, s)
        picked, gate = new("picked", "gate")
        far_in = new("far_in0", "far_in1", "far_in2", "far_in3")
        hot, summed, added = new("hot", "summed", "added")
        block = ctx.enter_context(nc.Block())

        @block.gpsimd
        def _(pool):
            def body(it):
                for lane in range(LANES):
                    if (at := at_stage(it, lane, 0)) is not None:
                        c, l = at
                        pool.wait_ge(picked, c + 1)
                        if over0(c - LANES + 1):
                            pool.wait_ge(summed, c - LANES + 1)
                        pool.sem_inc(gate, 1)
                        for i in range(C):
                            pool.indirect_dma_start(far[:, l, i, :], None, K.table2[i_layer],
                                                    bass.IndirectOffsetOnAxis(ap=idx[:, l, i:i + 1], axis=0)
                                                    ).then_inc(far_in[l], 16)

            chunk_loop(pool, body)

        @block.scalar
        def _(act):
            def body(it):
                for lane in range(LANES):
                    if (at := at_stage(it, lane, 0)) is not None:
                        c, l = at
                        if over0(c - LANES + 1):
                            act.wait_ge(far_in[l], 64 * (lane_turn(it, lane, 0) - 1))
                        ed.pick_others(act, idx[:, l, :], c).then_inc(picked, 1)

            chunk_loop(act, body)

        @block.tensor
        def _(pe):
            def body(it):
                for lane in range(LANES):
                    if (at := at_stage(it, lane, 2)) is not None:
                        c, l = at
                        pe.wait_ge(hot, c + 1)
                        pe.wait_ge(far_in[l], 64 * lane_turn(it, lane, 2))
                        if over0(C * (c - 1)):
                            pe.wait_ge(added, C * (c - 1))
                        for i in range(C):
                            mm = pe.matmul(p_agg[:, l % 2, i, :], S[:, l % 2, i, :], far[:, l, i, :],
                                           start=True, stop=True)
                        mm.then_inc(summed, 1)

            chunk_loop(pe, body)

        @block.vector
        def _(dve):
            regs = [dve.alloc_register(f"{s}_dve{i}") for i in range(C)]

            def body(it):
                for lane in range(LANES):
                    if (at := at_stage(it, lane, 1)) is not None:
                        c, l = at
                        if over0(c - 1):
                            dve.wait_ge(summed, c - 1)
                        ed.one_hot(dve, S[:, l % 2], c).then_inc(hot, 1)
                    if (at := at_stage(it, lane, 2)) is not None:
                        c, l = at
                        add_to_blocks(dve, ed, regs, c, agg, p_agg[:, l % 2], D, summed, added)

            chunk_loop(dve, body)


def layer2(nc, K, x, root):
    with ExitStack() as ctx:
        sb, _ = ctx_tools(nc, ctx)
        h, agg = sb("h2", [P, B, D]), sb("agg2", [P, B, D])
        nodes = x
        for i in range(3):
            node_pass(nc, K, f"n2{i}", nodes, [(K.w(f"g{i}"), D, None, agg)])
            [out] = Sems(nc, K.used_sems, f"t2{i}")("out")

            def scale(dve, link, scalar_step):
                link(dve.tensor_tensor(agg[:], agg[:], bc_last(root[:], D), ALU.mult))

            on_vector(nc, K, f"f2{i}a", scale)
            with nc.Block() as block:
                @block.sync
                def _(sp, i=i, out=out):
                    sp.dma_start(K.table2[i].rearrange("(b n) f -> n b f", n=P), agg[:]).then_inc(out, 16)
                    sp.wait_ge(out, 16)
            edge_pass2(nc, K, i, agg)

            def finish(dve, link, scalar_step, i=i):
                link(dve.tensor_tensor(h[:], agg[:], bc_last(root[:], D), ALU.mult))
                link(dve.tensor_tensor(h[:], h[:], bc_mid(K.v(f"b_g{i}"), B), ALU.add))
                if i < 2:
                    link(dve.tensor_scalar(h[:], h[:], 0.0, None, ALU.max))
                else:
                    link(dve.tensor_tensor(x[:], x[:], h[:], ALU.add))
                    layer_norm(dve, link, scalar_step, K, x[:], h[:])

            on_vector(nc, K, f"f2{i}b", finish)
            nodes = h



def edge_pass3a(nc, K, q, logit):
    ctx = ExitStack()
    with ctx:
        sb, ps = ctx_tools(nc, ctx)
        ed = Edges(nc, K, "s")
        idx = sb("l3_idx", [P, LANES, C], I32)
        lens = sb("l3_lens", [P, LANES, C])
        far = sb("l3_far", [P, LANES, C, 2 * D])
        S = sb("l3_S", [P, 2, C, P])
        ST = sb("l3_ST", [P, 2, C * P])
        LT = sb("l3_LT", [C, 2, P])
        hid = sb("l3_hid", [P, 2, C * P])
        prod = sb("l3_prod", [P, 2, C, D])
        dot = sb("l3_dot", [P, 2, C, H])
        bias = sb("l3_bias", [P, 2, C, H])
        p_turn = ps("l3_p_turn", [P, C * P])
        p_len = ps("l3_p_len", [C, P])
        p_hid = ps("l3_p_hid", [P, C * P])
        p_q = ps("l3_p_q", [P, 2, C, D])
        p_bias = ps("l3_p_bias", [P, 2, C, P])
        new = Sems(nc, K.used_sems, "l3")
        picked, gate = new("picked", "gate")
        far_in = new("far_in0", "far_in1", "far_in2", "far_in3")
        spilled = new("spilled0", "spilled1", "spilled2", "spilled3")
        hot, turned, kept, q_done, hid_in, hid_out, biased, multiplied, steps = new(
            "hot", "turned", "kept", "q_done", "hid_in", "hid_out", "biased", "multiplied", "steps")
        block = ctx.enter_context(nc.Block())

        @block.gpsimd
        def _(pool):
            def body(it):
                for lane in range(LANES):
                    if (at := at_stage(it, lane, 0)) is not None:
                        c, l = at
                        pool.wait_ge(picked, c + 1)
                        if over0(c - LANES + 1):
                            pool.wait_ge(multiplied, c - LANES + 1)
                            pool.wait_ge(spilled[l], 16 * (lane_turn(it, lane, 0) - 1))
                        pool.sem_inc(gate, 1)
                        for i in range(C):
                            pool.indirect_dma_start(far[:, l, i, :], None, K.table3,
                                                    bass.IndirectOffsetOnAxis(ap=idx[:, l, i:i + 1], axis=0)
                                                    ).then_inc(far_in[l], 16)

            chunk_loop(pool, body)

        @block.sync
        def _(sp):
            chunks = K.spill3.rearrange("(c e t) w -> e c t w", t=C, e=P)

            def body(it):
                for lane in range(LANES):
                    if (at := at_stage(it, lane, 2)) is not None:
                        c, l = at
                        sp.wait_ge(far_in[l], 64 * lane_turn(it, lane, 2))
                        sp.dma_start(chunks[:, bass.ds(c, 1), :, :], far[:, l:l + 1, :, D:2 * D]).then_inc(spilled[l], 16)

            chunk_loop(sp, body)
            for l in range(LANES):
                sp.wait_ge(spilled[l], 16 * ITERS)

        @block.scalar
        def _(act):
            def body(it):
                for lane in range(LANES):
                    if (at := at_stage(it, lane, 0)) is not None:
                        c, l = at
                        if over0(c - LANES + 1):
                            act.wait_ge(far_in[l], 64 * (lane_turn(it, lane, 0) - 1))
                            act.wait_ge(turned, c - LANES + 1)
                        nc.scalar.activation(lens[:, l, :], K.length[:, bass.ds(c * C, C)], ACT.Copy)
                        ed.pick_others(act, idx[:, l, :], c).then_inc(picked, 1)
                    if (at := at_stage(it, lane, 2)) is not None:
                        c, l = at
                        act.wait_ge(turned, c + 1)
                        if over0(c - 1):
                            act.wait_ge(q_done, c - 1)
                            act.wait_ge(hid_in, c - 1)
                        nc.scalar.activation(LT[:, l % 2, :], p_len[:], ACT.Copy)
                        nc.scalar.activation(ST[:, l % 2, :], p_turn[:], ACT.Copy).then_inc(kept, 1)
                    if (at := at_stage(it, lane, 3)) is not None:
                        c, l = at
                        act.wait_ge(hid_in, c + 1)
                        if over0(c - 1):
                            act.wait_ge(biased, c - 1)
                        nc.scalar.activation(hid[:, l % 2, :], p_hid[:], ACT.Silu, bias=K.w("hid_b")).then_inc(hid_out, 1)

            chunk_loop(act, body)

        @block.tensor
        def _(pe):
            regs = [pe.alloc_register(f"l3_pe{i}") for i in range(C)]

            def body(it):
                for lane in range(LANES):
                    if (at := at_stage(it, lane, 2)) is not None:
                        c, l = at
                        pe.wait_ge(hot, c + 1)
                        pe.wait_ge(picked, c + 1)
                        if over0(c):
                            pe.wait_ge(kept, c)
                        for i in range(C):
                            pe.transpose(p_turn[:, i * P:(i + 1) * P], S[:, l % 2, i, :], K.ident[:])
                        pe.transpose(p_len[:], lens[:, l, :], K.ident[:]).then_inc(turned, 1)
                    if (at := at_stage(it, lane, 3)) is not None:
                        c, l = at
                        blocks = ed.block_values(pe, regs, c)
                        pe.wait_ge(kept, c + 1)
                        if over0(c):
                            pe.wait_ge(hid_out, c)
                        for i in range(C):
                            mm = pe.matmul(p_hid[:, i * P:(i + 1) * P], K.w_len[:, i, :], LT[:, l % 2, :],
                                           start=True, stop=True)
                        mm.then_inc(hid_in, 1)
                        if over0(c - 1):
                            pe.wait_ge(multiplied, c - 1)
                        for i in range(C):
                            mm = pe.matmul(p_q[:, l % 2, i, :], ST[:, l % 2, i * P:(i + 1) * P],
                                           q[:, bass.ds(blocks[i], 1), :], start=True, stop=True)
                        mm.then_inc(q_done, 1)
                    if (at := at_stage(it, lane, 4)) is not None:
                        c, l = at
                        pe.wait_ge(hid_out, c + 1)
                        if over0(c - 1):
                            pe.wait_ge(steps, 3 * (c - 1))
                        for i in range(C):
                            mm = pe.matmul(p_bias[:, l % 2, i, 0:H], hid[:, l % 2, i * P:(i + 1) * P], K.w("bias3"),
                                           start=True, stop=True)
                        mm.then_inc(biased, 1)

            chunk_loop(pe, body)

        @block.vector
        def _(dve):
            def body(it):
                for lane in range(LANES):
                    if (at := at_stage(it, lane, 2)) is not None:
                        c, l = at
                        if over0(c - 1):
                            dve.wait_ge(turned, c - 1)
                        ed.one_hot(dve, S[:, l % 2], c).then_inc(hot, 1)
                    if (at := at_stage(it, lane, 4)) is not None:
                        c, l = at
                        h = l % 2
                        dve.wait_ge(q_done, c + 1)
                        dve.wait_ge(far_in[l], 64 * lane_turn(it, lane, 4))
                        dve.tensor_tensor(prod[:, h], p_q[:, h], far[:, l, :, 0:D], ALU.mult).then_inc(multiplied, 1)
                        dve.wait_ge(multiplied, c + 1)
                        dve.tensor_reduce(dot[:, h], prod[:, h].rearrange("p t (h d) -> p t h d", h=H), AX.X, ALU.add
                                          ).then_inc(steps, 1)
                        dve.wait_ge(biased, c + 1)
                        dve.tensor_tensor(bias[:, h], p_bias[:, h, :, 0:H], bc_mid(K.v("b_bias3"), C), ALU.add
                                          ).then_inc(steps, 1)
                        dve.wait_ge(steps, 3 * c + 2)
                        dve.scalar_tensor_tensor(out=logit[:, bass.ds(c * C, C), :], in0=dot[:, h], scalar=HD ** -0.5,
                                                 in1=bias[:, h], op0=ALU.mult, op1=ALU.add).then_inc(steps, 1)

            chunk_loop(dve, body)


def cut_and_exp(nc, K, logit):
    with ExitStack() as ctx:
        sb, ps = ctx_tools(nc, ctx)
        cut, turn, real = sb("cut", [P, T]), sb("turn", [P, T]), sb("real", [P, T])
        most, row, diag = sb("most", [P, H]), sb("row", [H, 1]), sb("diag", [H, H])
        every = sb("every", [P, H])
        p_row, p_all = ps("p_row", [H, P]), ps("p_all", [P, H])
        new = Sems(nc, K.used_sems, "cut")
        chain, turned, asked, answered, ready, crossed = new("chain", "turned", "asked", "answered", "ready", "crossed")
        block = ctx.enter_context(nc.Block())

        @block.vector
        def _(dve):
            count = [0]

            def link(ins):
                count[0] += 1
                ins.then_inc(chain, 1)
                dve.wait_ge(chain, count[0])

            link(dve.tensor_scalar(turn[:], K.length[:], 0.5 / CUTOFF, None, ALU.mult))
            link(dve.tensor_scalar(turn[:], turn[:], 12582912.0, 12582912.0, ALU.add, ALU.subtract))
            link(dve.scalar_tensor_tensor(out=turn[:], in0=turn[:], scalar=-2.0 * CUTOFF, in1=K.length[:],
                                          op0=ALU.mult, op1=ALU.add))
            link(dve.tensor_scalar(cut[:], turn[:], -1.0, None, ALU.mult))
            link(dve.tensor_tensor(turn[:], turn[:], cut[:], ALU.max))
            link(dve.tensor_scalar(turn[:], turn[:], -np.pi / CUTOFF, np.pi / 2, ALU.mult, ALU.add))
            link(dve.tensor_scalar(turn[:], turn[:], -np.pi / 2, np.pi / 2, ALU.max, ALU.min))
            dve.sem_inc(asked, 1)
            dve.wait_ge(answered, 1)
            link(dve.tensor_scalar(cut[:], cut[:], 1.0, 0.5, ALU.add, ALU.mult))
            link(dve.tensor_scalar(turn[:], K.length[:], CUTOFF, None, ALU.is_lt))
            link(dve.tensor_tensor(cut[:], cut[:], turn[:], ALU.mult))
            link(dve.tensor_tensor(logit[:], logit[:], bc_last(cut[:], H), ALU.mult))
            link(dve.tensor_scalar(real[:], K.key["s"][:], 0.0, None, ALU.is_ge))
            link(dve.tensor_scalar(turn[:], real[:], -1.0, 3.0e38, ALU.add, ALU.mult))
            link(dve.tensor_tensor(logit[:], logit[:], bc_last(real[:], H), ALU.mult))
            link(dve.tensor_tensor(logit[:], logit[:], bc_last(turn[:], H), ALU.add))
            link(dve.tensor_reduce(most[:], logit[:].rearrange("p t h -> p h t"), AX.X, ALU.max))
            dve.sem_inc(ready, 1)
            dve.wait_ge(crossed, 1)
            link(dve.tensor_reduce(row[:], p_row[:], AX.X, ALU.max))
            link(dve.tensor_scalar(diag[:], K.ident[0:H, 0:H], row[:, 0:1], None, ALU.mult))
            dve.sem_inc(ready, 1)
            dve.wait_ge(crossed, 2)
            link(dve.tensor_copy(every[:], p_all[:]))
            link(dve.tensor_tensor(logit[:], logit[:], bc_mid(every[:], T), ALU.subtract))
            dve.sem_inc(asked, 1)
            dve.wait_ge(answered, 2)

        @block.tensor
        def _(pe):
            pe.wait_ge(ready, 1)
            pe.transpose(p_row[:], most[:], K.ident[:]).then_inc(crossed, 1)
            pe.wait_ge(ready, 2)
            pe.matmul(p_all[:], K.ones[0:H, :], diag[:], start=True, stop=True).then_inc(crossed, 1)

        @block.scalar
        def _(act):
            act.wait_ge(asked, 1)
            nc.scalar.activation(cut[:], turn[:], ACT.Sin).then_inc(answered, 1)
            act.wait_ge(asked, 2)
            nc.scalar.activation(logit[:], logit[:], ACT.Exp).then_inc(answered, 1)


def edge_pass3b(nc, K, weight, agg):
    ctx = ExitStack()
    with ctx:
        sb, ps = ctx_tools(nc, ctx)
        ed = Edges(nc, K, "s")
        M = D + H
        far = sb("v3_far", [P, LANES, C, D])
        S = sb("v3_S", [P, 2, C, P])
        msg = sb("v3_msg", [P, 2, C, M])
        sums = sb("v3_sums", [P, 2, C, M])
        p_agg = ps("v3_p_agg", [P, 2, C, 2 * P])
        new = Sems(nc, K.used_sems, "v3")
        far_in = new("far_in0", "far_in1", "far_in2", "far_in3")
        hot, weights_in, msg_done, summed, added, agg_clear = new(
            "hot", "weights_in", "msg_done", "summed", "added", "agg_clear")
        [sums_out] = new("sums_out")
        block = ctx.enter_context(nc.Block())

        @block.sync
        def _(sp):
            chunks = K.spill3.rearrange("(c e t) w -> e c t w", t=C, e=P)

            def body(it):
                for lane in range(LANES):
                    if (at := at_stage(it, lane, 0)) is not None:
                        c, l = at
                        if over0(c - LANES + 1):
                            sp.wait_ge(msg_done, c - LANES + 1)
                        sp.dma_start(far[:, l:l + 1, :, :], chunks[:, bass.ds(c, 1), :, :]).then_inc(far_in[l], 16)

            chunk_loop(sp, body)

        @block.scalar
        def _(act):
            def body(it):
                for lane in range(LANES):
                    if (at := at_stage(it, lane, 2)) is not None:
                        c, l = at
                        if over0(c - 1):
                            act.wait_ge(summed, c - 1)
                        nc.scalar.activation(msg[:, l % 2, :, D:M], weight[:, bass.ds(c * C, C), :], ACT.Copy
                                             ).then_inc(weights_in, 1)
                    if (at := at_stage(it, lane, 3)) is not None:
                        c, l = at
                        act.wait_ge(summed, c + 1)
                        if over0(C * (c - 1)):
                            act.wait_ge(added, C * (c - 1))
                        nc.scalar.activation(sums[:, l % 2], p_agg[:, l % 2, :, 0:M], ACT.Copy).then_inc(sums_out, 1)

            chunk_loop(act, body)

        @block.tensor
        def _(pe):
            def body(it):
                for lane in range(LANES):
                    if (at := at_stage(it, lane, 2)) is not None:
                        c, l = at
                        pe.wait_ge(hot, c + 1)
                        pe.wait_ge(msg_done, c + 1)
                        if over0(c - 1):
                            pe.wait_ge(sums_out, c - 1)
                        for i in range(C):
                            mm = pe.matmul(p_agg[:, l % 2, i, 0:M], S[:, l % 2, i, :], msg[:, l % 2, i, :],
                                           start=True, stop=True)
                        mm.then_inc(summed, 1)

            chunk_loop(pe, body)

        @block.vector
        def _(dve):
            def body(it):
                for lane in range(LANES):
                    if (at := at_stage(it, lane, 2)) is not None:
                        c, l = at
                        h = l % 2
                        if over0(c - 1):
                            dve.wait_ge(summed, c - 1)
                        ed.one_hot(dve, S[:, h], c).then_inc(hot, 1)
                        dve.wait_ge(weights_in, c + 1)
                        dve.wait_ge(far_in[l], 16 * lane_turn(it, lane, 2))
                        dve.tensor_tensor(msg[:, h, :, 0:D].rearrange("p t (h d) -> p t h d", h=H),
                                          far[:, l, :, :].rearrange("p t (h d) -> p t h d", h=H),
                                          bc_last(msg[:, h, :, D:M], HD), ALU.mult).then_inc(msg_done, 1)

            chunk_loop(dve, body)

        @block.gpsimd
        def _(pool):
            regs = [pool.alloc_register(f"v3_pool{i}") for i in range(C)]
            pool.memset(agg[:], 0.0).then_inc(agg_clear, 1)
            pool.wait_ge(agg_clear, 1)

            def body(it):
                for lane in range(LANES):
                    if (at := at_stage(it, lane, 3)) is not None:
                        c, l = at
                        add_to_blocks(pool, ed, regs, c, agg, sums[:, l % 2], M, sums_out, added)

            chunk_loop(pool, body)


def layer3(nc, K, x):
    with ExitStack() as ctx:
        sb, _ = ctx_tools(nc, ctx)
        logit = sb("logit3", [P, T, H])
        with ExitStack() as inner:
            q = inner.enter_context(nc.sbuf_tensor("q3", [P, B, D], F32))
            node_pass(nc, K, "n3", x, [(K.w("q3"), D, K.v("b_q3"), q),
                                            (K.w("kv3"), 2 * D, K.v("b_kv3"), (K.table3, 0, 2 * D))])
            edge_pass3a(nc, K, q, logit)
        cut_and_exp(nc, K, logit)
        agg = sb("agg3", [P, B, D + H])
        y, tmp = sb("y3", [P, B, D]), sb("tmp3", [P, B, D])
        edge_pass3b(nc, K, logit, agg)

        def divide(dve, link, scalar_step):
            link(dve.tensor_scalar(tmp[:, :, 0:H], agg[:, :, D:D + H], 1e-8, None, ALU.add))
            link(dve.reciprocal(tmp[:, :, 0:H], tmp[:, :, 0:H]))
            for h in range(H):
                link(dve.tensor_tensor(y[:, :, h * HD:(h + 1) * HD], agg[:, :, h * HD:(h + 1) * HD],
                                       bc_last(tmp[:, :, h], HD), ALU.mult))

        on_vector(nc, K, "f3a", divide)
        node_pass(nc, K, "n3o", y, [(K.w("o3"), D, K.v("b_o3"), tmp)])

        def finish(dve, link, scalar_step):
            link(dve.tensor_tensor(tmp[:], tmp[:], x[:], ALU.add))
            layer_norm(dve, link, scalar_step, K, tmp[:], y[:], K.v("ln_g"), K.v("ln_b"))
            link(dve.tensor_tensor(x[:], x[:], tmp[:], ALU.add))
            layer_norm(dve, link, scalar_step, K, x[:], y[:])

        on_vector(nc, K, "f3b", finish)


def layers(nc, top, K, io):
    x = top.enter_context(nc.sbuf_tensor("x", [P, B, D], F32))
    root = top.enter_context(nc.sbuf_tensor("root", [P, B], F32))
    with ExitStack() as inner:
        late = Late(nc, inner)
        load_and_sort(nc, K, io, late, x)
        load_order(nc, K, "s")
        layer0(nc, K, x, late)
    load_order(nc, K, "d")
    layer1(nc, K, x, root)
    layer2(nc, K, x, root)
    layer3(nc, K, x)
    [stored] = Sems(nc, K.used_sems, "end")("stored")
    with nc.Block() as block:
        @block.sync
        def _(sp):
            sp.dma_start(io["out"], x[:].rearrange("p b d -> p (b d)")).then_inc(stored, 16)
            sp.wait_ge(stored, 16)



class Late:

    def __init__(self, nc, ctx):
        self.pos = ctx.enter_context(nc.sbuf_tensor("late_pos", [P, T], I32))
        self.rec = ctx.enter_context(nc.sbuf_tensor("late_rec", [P, T, REC_D], F32))


class Kept:

    def __init__(self, nc, ctx):
        def sb(name, shape, dt=F32):
            return ctx.enter_context(nc.sbuf_tensor(name, shape, dt))

        self.used_sems = []
        self.W, self.V = sb("weights", [P, NW]), sb("vectors", [P, NV])
        self.w_ef_parts = sb("w_ef_parts", [P, 2, 2 * D], BF16)
        self.ident_bf = sb("ident_bf", [P, P], BF16)
        self.col = sb("col", [P, 1])
        self.w_len = sb("w_len", [C, C, D])
        self.lane = sb("lane", [P, P])
        self.ident, self.ones = sb("ident", [P, P]), sb("ones", [P, P])
        self.key = {k: sb(f"key_{k}", [P, T]) for k in "sd"}
        self.other = {k: sb(f"other_{k}", [P, T], I32) for k in "sd"}
        self.blocks = {k: sb(f"blocks_{k}", [1, T], I32) for k in "sd"}
        self.length = sb("len_sorted", [P, T])
        self.stat = sb("stat", [P, 2, B])
        self.rec_s = nc.dram_tensor("rec_s", [T * P, REC_S], F32).ap()
        self.rec_d = nc.dram_tensor("rec_d", [T * P, REC_D], F32).ap()
        self.key_rows = {k: nc.dram_tensor(f"dram_key_rows_{k}", [T, P], BF16).ap() for k in "sd"}
        self.len_rows = nc.dram_tensor("dram_len_rows", [T, P], F32).ap()
        self.map_dram = {k: nc.dram_tensor(f"map_{k}", [P * G], I32).ap() for k in "sd"}
        self.table0 = nc.dram_tensor("table0", [NP, 2 * D], F32).ap()
        self.table1 = nc.dram_tensor("table1", [NP, D + H], F32).ap()
        self.table2 = [nc.dram_tensor(f"table2_{i}", [NP, D], F32).ap() for i in range(3)]
        self.table3 = nc.dram_tensor("table3", [NP, 2 * D], F32).ap()
        self.spill1 = nc.dram_tensor("spill1", [T * P, D + H], F32).ap()
        self.spill3 = nc.dram_tensor("spill3", [T * P, D], F32).ap()

    def w(self, name):
        a, b = W_COLS[name]
        return self.W[:, a:b]

    def v(self, name):
        a, b = V_COLS[name]
        return self.V[:, a:b]


IO = {"x": ([P, B * D], F32), "src": ([P, COLS], I32), "dst": ([P, COLS], I32), "ef": ([P, COLS * EF], F32),
      "length": ([P, COLS], F32), "weights": ([P, NW], F32), "vectors": ([P, NV], F32),
      "w_ef": ([P, 2 * D], F32), "part": ([P, 5], F32), "w_len": ([C, C, D], F32)}


def build(nc, io):
    ctx = ExitStack()
    with ctx:
        K = Kept(nc, ctx)
        layers(nc, ctx, K, io)


def lay_out(a):
    a = {k: np.asarray(v) for k, v in a.items()}

    def padded(v, rows, fill=0):
        out = np.full((rows, *v.shape[1:]), fill, v.dtype)
        out[:len(v)] = v
        return out

    out = {"x": padded(a["x"], NP).reshape(B, P, D).transpose(1, 0, 2).reshape(P, B * D)}
    for k in ("src", "dst"):
        out[k] = padded(a[k], P * COLS, NP).reshape(P, COLS)
    out["ef"] = padded(a["edge_attr_10"], P * COLS).reshape(P, COLS * EF)
    out["length"] = padded(a["edge_weight1"], P * COLS).reshape(P, COLS)
    gate, cand = a["L0_gnn_gate_w"], a["L0_gnn_cand_w"]
    both = np.concatenate([gate, cand], 1)
    W = np.zeros((P, NW), np.float32)
    for name, w in (("own0", both[0:D]), ("other0", both[D:2 * D]), ("in1", a["L1_gnn_w_in"]),
                    ("a1", np.concatenate([a["L1_gnn_w_au"], a["L1_gnn_w_av"]], 1)),
                    ("mlp1", a["L1_gnn_w1"]), ("mlp2", a["L1_gnn_w2"]),
                    ("g0", a["L2_gnn_W0"]), ("g1", a["L2_gnn_W1"]), ("g2", a["L2_gnn_W2"]),
                    ("q3", a["L3_gnn_Wq"].T), ("kv3", np.concatenate([a["L3_gnn_Wk"].T, a["L3_gnn_Wv"].T], 1)),
                    ("bias3", a["L3_gnn_We2"].T), ("o3", a["L3_gnn_Wo"].T), ("hid_b", a["L3_gnn_be1"][:, None])):
        lo, hi = W_COLS[name]
        W[:, lo:hi] = w
    V = np.zeros((P, NV), np.float32)
    zeros = np.zeros(H, np.float32)
    for name, v in (("b0", np.concatenate([a["L0_gnn_gate_b"], a["L0_gnn_cand_b"]])), ("b_in1", a["L1_gnn_b_in"]),
                    ("b_a1", np.concatenate([a["L1_gnn_b_au"], zeros])), ("b_mlp1", a["L1_gnn_b1"]),
                    ("b_mlp2", a["L1_gnn_b2"]), ("b_g0", a["L2_gnn_b0"]), ("b_g1", a["L2_gnn_b1"]),
                    ("b_g2", a["L2_gnn_b2"]), ("b_q3", a["L3_gnn_bq"]),
                    ("b_kv3", np.concatenate([a["L3_gnn_bk"], a["L3_gnn_bv"]])), ("b_bias3", a["L3_gnn_be2"]),
                    ("b_o3", a["L3_gnn_bo"]), ("bn_g", a["L0_gnn_bn_gamma"]), ("bn_b", a["L0_gnn_bn_beta"]),
                    ("ln_g", a["L3_gnn_ln_g"]), ("ln_b", a["L3_gnn_ln_b"])):
        lo, hi = V_COLS[name]
        V[:, lo:hi] = v[None, :]
    out["weights"], out["vectors"] = W, V
    w_ef, part = np.zeros((P, 2 * D), np.float32), np.zeros((P, 5), np.float32)
    for half in range(P // PARTS):
        part[half * PARTS:(half + 1) * PARTS, 3 + half] = 1
        for j, which in enumerate(WEIGHT_PARTS):
            at = half * PARTS + j * EF
            w_ef[at:at + EF] = both[2 * D:]
            part[at:at + EF, which] = 1
    w_len = np.zeros((C, C, D), np.float32)
    for i in range(C):
        w_len[i, i] = a["L3_gnn_We1"][:, 0]
    out["w_ef"], out["part"], out["w_len"] = w_ef, part, w_len
    return {k: np.ascontiguousarray(v) for k, v in out.items()}


def kernel(**inputs):
    import concourse.bacc as bacc
    from concourse.bass_utils import run_bass_kernel_spmd

    nc = bacc.Bacc("TRN2", target_bir_lowering=False, num_devices=1)
    arrays = {f"in_{k}": v for k, v in lay_out(inputs).items()}
    io = {k: nc.dram_tensor(f"in_{k}", shape, dt, kind="ExternalInput").ap() for k, (shape, dt) in IO.items()}
    io["out"] = nc.dram_tensor("out", [P, B * D], F32, kind="ExternalOutput").ap()
    build(nc, io)
    got = run_bass_kernel_spmd(nc, [arrays], core_ids=[0]).results[0]["out"]
    return np.ascontiguousarray(got.reshape(P, B, D).transpose(1, 0, 2).reshape(NP, D)[:N])
```

```python
from contextlib import ExitStack

import numpy as np

import concourse.bass as bass
from concourse import mybir

F32 = mybir.dt.float32
I32 = mybir.dt.int32
BF16 = mybir.dt.bfloat16
ALU = mybir.AluOpType
ACT = mybir.ActivationFunctionType
AX = mybir.AxisListType

P = 128
N = 6250
E = 100000
D = 128
H = 8
HD = D // H
EF = 10
B = -(-N // P)
NP = B * P
LAST = N - (B - 1) * P
COLS = -(-E // P)
C = 4
LANES = 4
T = COLS + B
T = -(-T // (C * LANES)) * C * LANES
NCH = T // C
ITERS = NCH // LANES
REC_S = 2 + EF + 1
PARTS = 64
FEAT_PARTS = (0, 0, 0, 1, 1, 2)
WEIGHT_PARTS = (0, 1, 2, 0, 1, 0)
REC_D = 2
G = 7
NG = B // G
SG = 17
NSG = COLS // SG
BIG = 1.0e30
CUTOFF = 5.0
EXP_LN_SET = "natural_log_exp_and_others"
assert NG % 2 == 1 and B % G == 0 and COLS % SG == 0 and NSG % 2 == 0 and NCH % LANES == 0

W_COLS, V_COLS = {}, {}


assert len(FEAT_PARTS) == len(WEIGHT_PARTS) and len(FEAT_PARTS) * EF <= PARTS


def _place(table, items):
    at = 0
    for name, n in items:
        table[name] = (at, at + n)
        at += n
    return at


NW = _place(W_COLS, [("own0", 256), ("other0", 256), ("in1", D), ("a1", 2 * H), ("mlp1", D), ("mlp2", D),
                     ("g0", D), ("g1", D), ("g2", D), ("q3", D), ("kv3", 2 * D), ("bias3", H), ("o3", D),
                     ("hid_w", 1), ("hid_b", 1)])
NV = _place(V_COLS, [("b0", 256), ("b_in1", D), ("b_a1", 2 * H), ("b_mlp1", D), ("b_mlp2", D), ("b_g0", D),
                     ("b_g1", D), ("b_g2", D), ("b_q3", D), ("b_kv3", 2 * D), ("b_bias3", H), ("b_o3", D),
                     ("bn_g", D), ("bn_b", D), ("ln_g", D), ("ln_b", D)])


def over0(v):
    return not isinstance(v, int) or v > 0


def ctx_tools(nc, ctx):
    def sb(name, shape, dt=F32):
        return ctx.enter_context(nc.sbuf_tensor(name, shape, dt))

    def ps(name, shape, dt=F32):
        return ctx.enter_context(nc.psum_tensor(name, shape, dt))

    return sb, ps


def bc_mid(ap, n):
    return ap.unsqueeze(1).to_broadcast([ap.shape[0], n, ap.shape[1]])


def bc_last(ap, n):
    return ap.unsqueeze(len(ap.shape)).to_broadcast([*ap.shape, n])


def chunk_loop(eng, body, peel=2):
    for it in range(peel):
        body(it)
    with eng.Fori(peel, ITERS) as it:
        body(it)
    for it in range(ITERS, ITERS + 2):
        body(it)


def at_stage(it, lane, lag):
    if isinstance(it, int):
        c = LANES * it + lane - lag
        return (c, c % LANES) if 0 <= c < NCH else None
    return it * LANES + (lane - lag), (lane - lag) % LANES


class Sems:

    MOST = 110

    def __init__(self, nc, used, stage):
        if len(used) > self.MOST:
            nc.clear_and_free_semaphores(used)
            nc.all_engine_barrier()
            used.clear()
        self.nc, self.used, self.stage = nc, used, stage

    def __call__(self, *names):
        sems = [self.nc.alloc_semaphore(f"{self.stage}_{n}") for n in names]
        self.used.extend(sems)
        return sems



def load_and_sort(nc, K, io, late, x):
    ctx = ExitStack()
    with ctx:
        sb, ps = ctx_tools(nc, ctx)
        key = {"s": sb("src_i", [P, COLS], I32), "d": sb("dst_i", [P, COLS], I32)}
        whole = {"s": sb("src_f", [P, COLS]), "d": sb("dst_f", [P, COLS])}
        local = sb("src_local", [P, COLS])
        pos = {"s": sb("src_pos", [P, COLS]), "d": sb("dst_pos", [P, T])}
        pos_i = {"s": sb("src_pos_i", [P, COLS], I32), "d": late.pos}
        blk = sb("blk", [P, COLS])
        mask = sb("mask", [P, COLS])
        rank = sb("rank", [P, COLS])
        feats = sb("feats", [P, COLS, EF])
        length = sb("length", [P, COLS])
        w_ef, part = sb("w_ef", [P, 2 * D]), sb("part", [P, 5])
        lane_i, tile_i, col_i = sb("lane_i", [P, P], I32), sb("tile_i", [P, G], I32), sb("col_i", [P, 1], I32)
        before = sb("before", [P, P])
        ef_parts = sb("ef_parts", [P, 3, 2 * D])
        cnt = sb("cnt", [P, B])
        few = sb("few", [P, 6, B])
        few_i = sb("few_i", [P, B], I32)
        tile_no = sb("tile_no", [P, G])
        past = sb("past", [P, G, B - 1])
        tb_f = sb("tb_f", [P, G])
        tb_i = {"s": sb("tb_s", [P, G], I32), "d": sb("tb_d", [P, G], I32)}
        pad = sb("pad", [P, 104, REC_S])
        after = sb("after", [P, COLS], I32)
        downs = sb("downs", [P, 1])
        start_f, start_i = sb("start_f", [P, G]), sb("start_i", [P, G], I32)
        starts = sb("starts", [1, T], I32)
        p_downs = ps("p_downs", [P, 1])
        stage_s = sb("stage_s", [P, 2, SG, REC_S])
        stage_i = sb("stage_i", [P, 2, SG], I32)
        p_cnt = {"s": ps("p_cnt_s", [P, 2, 64]), "d": ps("p_cnt_d", [P, 2, 64])}
        new = Sems(nc, K.used_sems, "sort")
        loaded, consts, chain, counted, summed = new("loaded", "consts", "chain", "counted", "summed")
        pads_set, pads_out, map_ready, map_out = new("pads_set", "pads_out", "map_ready", "map_out")
        pos_ready, gate, maps_in = new("pos_ready", "gate", "maps_in")
        staged, sent = new("staged0", "staged1"), new("sent0", "sent1")
        starts_ready, starts_out, starts_in, searched, judged, flagged = new(
            "starts_ready", "starts_out", "starts_in", "searched", "judged", "flagged")
        [tiles_out] = new("tiles_out")
        [src_in] = new("src_in")
        n_loads = 9
        block = ctx.enter_context(nc.Block())

        @block.sync
        def _(sp):
            sp.dma_start(key["s"][:], io["src"]).then_inc(src_in, 16)
            for ints, first in ((key["d"], 0), (after, 1)):
                sp.dma_start(ints[:], io["dst"][first:first + P * COLS].rearrange("(p n) -> p n", p=P)
                             ).then_inc(loaded, 16)
            sp.dma_start(x[:].rearrange("p b d -> p (b d)"), io["x"]).then_inc(loaded, 16)
            sp.dma_start(feats[:].rearrange("p a b -> p (a b)"), io["ef"]).then_inc(loaded, 16)
            sp.dma_start(length[:], io["length"]).then_inc(loaded, 16)
            sp.dma_start(K.W[:], io["weights"]).then_inc(loaded, 16)
            sp.dma_start(K.V[:], io["vectors"]).then_inc(loaded, 16)
            sp.dma_start(w_ef[:], io["w_ef"]).then_inc(loaded, 16)
            sp.dma_start(part[:], io["part"]).then_inc(loaded, 16)
            sp.wait_ge(pads_set, 2)
            rows = K.rec_s.rearrange("(a p n) w -> a p (n w)", p=P, n=104)
            for a in range(T // 104):
                sp.dma_start(rows[a], pad[:].rearrange("p n w -> p (n w)")).then_inc(pads_out, 16)
            for n, k in enumerate("sd"):
                sp.wait_ge(map_ready, n + 1)
                sp.dma_start(K.map_dram[k].rearrange("(n p) -> p n", p=P), tb_i[k][:],
                             allow_slow_non_contiguous=True).then_inc(map_out, 16)
                sp.wait_ge(map_out, 16 * (n + 1))
                sp.dma_start(K.blocks[k][0:1, :], K.map_dram[k][0:T].unsqueeze(0)).then_inc(maps_in, 16)
            sp.wait_ge(maps_in, 32)
            sp.wait_ge(starts_ready, 1)
            sp.dma_start(K.starts_dram.rearrange("(n p) -> p n", p=P), start_i[:],
                         allow_slow_non_contiguous=True).then_inc(starts_out, 16)
            sp.wait_ge(starts_out, 16)
            sp.dma_start(starts[:], K.starts_dram[0:T].unsqueeze(0)).then_inc(starts_in, 16)
            sp.wait_ge(starts_in, 16)
            sp.wait_ge(flagged, 1)
            some = C * LANES
            regs = [sp.alloc_register(f"sort_sp{i}") for i in range(some)]
            tiles = K.rec_d.rearrange("(t e) w -> t (e w)", e=P)
            with sp.If_eq(disordered(sp, K, "sort_sp_flag"), 0):
                with sp.Fori(0, T // some) as it:
                    sp.load(regs, starts[0:1, bass.ds(it * some, some)])
                    for i in range(some):
                        start = sp.snap(regs[i], min_val=0, max_val=REC_D * P * COLS)
                        sp.dma_start(tiles[bass.ds(it * some + i, 1), :],
                                     io["ends"][bass.ds(start, REC_D * P)].unsqueeze(0)).then_inc(tiles_out, 16)
                sp.wait_ge(tiles_out, 16 * T)

        @block.gpsimd
        def _(pool):
            pool.iota(lane_i[:], pattern=[[1, P]], base=0, channel_multiplier=0).then_inc(consts, 1)
            pool.iota(tile_i[:], pattern=[[P, G]], base=0, channel_multiplier=1).then_inc(consts, 1)
            pool.iota(col_i[:], pattern=[[0, 1]], base=0, channel_multiplier=1).then_inc(consts, 1)
            pool.memset(K.ident[:], 0.0).then_inc(consts, 1)
            pool.memset(K.ones[:], 1.0).then_inc(consts, 1)
            pool.memset(pad[:].rearrange("p n w -> p (n w)"), 0.0).then_inc(pads_set, 1)
            pool.wait_ge(consts, 5)
            pool.affine_select(out=K.ident[:], in_=K.ident[:], compare_op=ALU.not_equal, fill=1.0, base=0,
                               pattern=[[-1, P]], channel_multiplier=1).then_inc(consts, 1)
            pool.affine_select(out=before[:], in_=K.ones[:], compare_op=ALU.is_gt, fill=0.0, base=0,
                               pattern=[[1, P]], channel_multiplier=-1).then_inc(consts, 1)
            pool.wait_ge(pads_out, 16 * (T // 104))

            def scatter(it):
                for half in range(2):
                    pool.wait_ge(staged[half], 1 * (it + 1))
                    pool.sem_inc(gate, 1)
                    for j in range(SG):
                        pool.indirect_dma_start(
                            K.rec_s, bass.IndirectOffsetOnAxis(ap=stage_i[:, half, j:j + 1], axis=0),
                            stage_s[:, half, j, :], None,
                            bounds_check=T * P - 1, oob_is_err=False).then_inc(sent[half], 16)

            scatter(0)
            with pool.Fori(1, NSG // 2) as it:
                scatter(it)
            for half in range(2):
                pool.wait_ge(sent[half], 16 * SG * (NSG // 2))

        @block.scalar
        def _(act):
            act.wait_ge(loaded, 16 * n_loads)
            act.wait_ge(pos_ready, 1)

            def fill(it):
                for half in range(2):
                    cols = bass.ds((it * 2 + half) * SG, SG)
                    if over0(it):
                        act.wait_ge(sent[half], 16 * SG * it)
                    dst = stage_s[:, half]
                    nc.scalar.activation(stage_i[:, half, :], pos_i["s"][:, cols], ACT.Copy)
                    nc.scalar.activation(dst[:, :, 0], local[:, cols], ACT.Copy)
                    nc.scalar.activation(dst[:, :, 1], whole["d"][:, cols], ACT.Copy)
                    nc.scalar.activation(dst[:, :, 2:2 + EF], feats[:, cols, :], ACT.Copy)
                    nc.scalar.activation(dst[:, :, 2 + EF], length[:, cols], ACT.Copy).then_inc(staged[half], 1)

            fill(0)
            with act.Fori(1, NSG // 2) as it:
                fill(it)

        @block.tensor
        def _(pe):
            pe.wait_ge(consts, 7)
            for n, k in enumerate("sd"):
                if k == "d":
                    pe.wait_ge(searched, 1)
                    pe.matmul(p_downs[:], K.ones[:], downs[:], start=True, stop=True).then_inc(judged, 1)
                pe.wait_ge(counted, n + 1)
                pe.matmul(p_cnt[k][:, 0, 0:B], K.ones[:], cnt[:], start=True, stop=True)
                pe.matmul(p_cnt[k][:, 1, 0:B], before[:], cnt[:], start=True, stop=True).then_inc(summed, 1)

        @block.vector
        def _(dve):
            count = [0]

            def link(ins):
                count[0] += 1
                ins.then_inc(chain, 1)
                dve.wait_ge(chain, count[0])

            dve.wait_ge(pads_set, 1)
            dve.memset(pad[:, :, 0], -1.0).then_inc(pads_set, 1)
            dve.wait_ge(consts, 3)
            dve.tensor_copy(K.col[:], col_i[:])
            dve.tensor_copy(K.lane[:], lane_i[:])
            link(dve.tensor_copy(tile_no[:], tile_i[:]))
            total, nt_end, nt, base, tend, slack = (few[:, i, :] for i in range(6))
            dve.wait_ge(src_in, 16)
            for n, k in enumerate("sd"):
                if n == 1:
                    dve.wait_ge(summed, 1)
                    link(dve.tensor_tensor(mask[:], key["d"][:], after[:], ALU.is_gt))
                    link(dve.tensor_reduce(downs[:], mask[:], AX.X, ALU.add))
                    dve.sem_inc(searched, 1)
                    dve.wait_ge(judged, 1)
                    link(dve.tensor_scalar(K.disorder[:], p_downs[:], 1.0, None, ALU.min))
                    dve.sem_inc(flagged, 1)
                else:
                    link(dve.tensor_copy(whole[k][:], key[k][:]))
                link(dve.tensor_scalar(key[k][:], key[k][:], 7, None, ALU.arith_shift_right))
                link(dve.tensor_copy(blk[:], key[k][:]))
                if k == "s":
                    link(dve.scalar_tensor_tensor(out=local[:], in0=blk[:], scalar=-float(P), in1=whole[k][:],
                                                  op0=ALU.mult, op1=ALU.add))
                with dve.Fori(0, NG) as g:
                    for j in range(G):
                        one = bass.ds(g * G + j, 1)
                        dve.tensor_scalar(mask[:], blk[:], K.lane[:, one], None, ALU.is_equal, ALU.add,
                                          accum_out=cnt[:, one])
                        dve.drain()
                dve.drain().then_inc(counted, 1)
                dve.wait_ge(summed, n + 1)
                link(dve.tensor_copy(total, p_cnt[k][:, 0, 0:B]))
                link(dve.tensor_scalar(few_i[:], total, float(P - 1), None, ALU.add))
                link(dve.tensor_scalar(few_i[:], few_i[:], 7, None, ALU.arith_shift_right))
                link(dve.tensor_copy(nt, few_i[:]))
                link(dve.tensor_tensor_scan(tend, nt, nt, 0.0, ALU.add, ALU.max))
                link(dve.tensor_tensor(nt_end, tend, nt, ALU.subtract))
                link(dve.scalar_tensor_tensor(out=base, in0=nt_end, scalar=float(P), in1=p_cnt[k][:, 1, 0:B],
                                              op0=ALU.mult, op1=ALU.add))
                link(dve.tensor_tensor(past[:], bc_last(tile_no[:], B - 1), bc_mid(tend[:, 0:B - 1], G), ALU.is_ge))
                link(dve.tensor_reduce(tb_f[:], past[:], AX.X, ALU.add))
                link(dve.tensor_copy(tb_i[k][:], tb_f[:]))
                dve.sem_inc(map_ready, 1)
                if k == "d":
                    link(dve.tensor_scalar(K.block_start[:], tb_f[:], float(P), None, ALU.mult))
                    link(dve.scalar_tensor_tensor(out=slack, in0=nt, scalar=-float(P), in1=total,
                                                  op0=ALU.mult, op1=ALU.add))
                    link(dve.tensor_tensor(past[:], past[:], bc_mid(slack[:, 0:B - 1], G), ALU.mult))
                    link(dve.tensor_reduce(start_f[:], past[:], AX.X, ALU.add))
                    link(dve.scalar_tensor_tensor(out=start_f[:], in0=tile_no[:], scalar=float(P), in1=start_f[:],
                                                  op0=ALU.mult, op1=ALU.add))
                    link(dve.tensor_scalar(start_i[:], start_f[:], float(P * COLS), float(REC_D), ALU.min, ALU.mult))
                    dve.sem_inc(starts_ready, 1)
                link(dve.memset(pos[k][:], float(1 << 22)))
                with dve.Fori(0, NG) as g:
                    for j in range(G):
                        one = bass.ds(g * G + j, 1)
                        dve.tensor_scalar(mask[:], blk[:], K.lane[:, one], None, ALU.is_equal)
                        dve.drain()
                        dve.tensor_tensor_scan(rank[:], mask[:], mask[:], base[:, one], ALU.add, ALU.max)
                        dve.drain()
                        dve.copy_predicated(pos[k][:, 0:COLS], mask[:].bitcast(I32), rank[:])
                        dve.drain()
                link(dve.tensor_scalar(pos_i[k][:], pos[k][:], -1.0, None, ALU.add))
                if k == "s":
                    dve.wait_ge(loaded, 16 * n_loads)
                    link(dve.tensor_copy(whole["d"][:], key["d"][:]))
                dve.sem_inc(pos_ready, 1)
            high, rest, mid = (ef_parts[:, i, :] for i in range(3))
            dve.wait_ge(consts, 7)
            link(dve.tensor_copy(K.ident_bf[:], K.ident[:]))
            link(dve.tensor_copy(K.w_ef_parts[:, 0], w_ef[:]))
            link(dve.tensor_copy(high, K.w_ef_parts[:, 0]))
            link(dve.tensor_tensor(rest, w_ef[:], high, ALU.subtract))
            link(dve.tensor_copy(K.w_ef_parts[:, 0], rest))
            link(dve.tensor_copy(mid, K.w_ef_parts[:, 0]))
            link(dve.tensor_tensor(rest, rest, mid, ALU.subtract))
            link(dve.tensor_scalar(high, high, part[:, 0:1], None, ALU.mult))
            link(dve.scalar_tensor_tensor(out=high, in0=mid, scalar=part[:, 1:2], in1=high,
                                          op0=ALU.mult, op1=ALU.add))
            link(dve.scalar_tensor_tensor(out=high, in0=rest, scalar=part[:, 2:3], in1=high,
                                          op0=ALU.mult, op1=ALU.add))
            for tile in range(2):
                link(dve.tensor_scalar(K.w_ef_parts[:, tile], high, part[:, 3 + tile:4 + tile], None, ALU.mult))
            link(dve.memset(late.rec[:], 0.0))
            link(dve.tensor_copy(late.rec[:, 0:COLS, 0], whole["d"][:]))
            link(dve.tensor_copy(late.rec[:, 0:COLS, 1], whole["s"][:]))


def disordered(eng, K, name):
    reg = eng.alloc_register(name)
    eng.load(reg, K.disorder[0:1, 0:1])
    return reg


def scatter_by_destination(nc, K, late):
    with ExitStack() as ctx:
        sb, _ = ctx_tools(nc, ctx)
        pad = sb("pad_d", [P, 104, REC_D], I32)
        late_i = sb("late_i", [P, 2, C], I32)
        late_rec = sb("late_rec_now", [P, 2, C, REC_D], I32)
        new = Sems(nc, K.used_sems, "by_dst")
        pads_set, pads_out, late_set, gate = new("pads_set", "pads_out", "late_set", "gate")
        late_out = new("late_out0", "late_out1")
        block = ctx.enter_context(nc.Block())

        @block.sync
        def _(sp):
            with sp.If_ne(disordered(sp, K, "by_dst_sp"), 0):
                sp.wait_ge(pads_set, 2)
                rows = K.rec_d.rearrange("(a p n) w -> a p (n w)", p=P, n=104)
                for a in range(T // 104):
                    sp.dma_start(rows[a], pad[:].rearrange("p n w -> p (n w)")).then_inc(pads_out, 16)

        @block.vector
        def _(dve):
            with dve.If_ne(disordered(dve, K, "by_dst_dve"), 0):
                dve.memset(pad[:], 0.0).then_inc(pads_set, 1)
                dve.wait_ge(pads_set, 1)
                dve.memset(pad[:, :, 0], -1.0).then_inc(pads_set, 1)

        @block.scalar
        def _(act):
            with act.If_ne(disordered(act, K, "by_dst_act"), 0):
                def body(it):
                    for half in range(2):
                        if over0(it):
                            act.wait_ge(late_out[half], 16 * C * it)
                        cols = bass.ds((2 * it + half) * C, C)
                        nc.scalar.activation(late_i[:, half, :], late.pos[:, cols], ACT.Copy)
                        nc.scalar.activation(late_rec[:, half], late.rec[:, cols, :], ACT.Copy).then_inc(late_set, 1)

                body(0)
                with act.Fori(1, NCH // 2) as it:
                    body(it)

        @block.gpsimd
        def _(pool):
            with pool.If_ne(disordered(pool, K, "by_dst_pool"), 0):
                pool.wait_ge(pads_out, 16 * (T // 104))
                with pool.Fori(0, NCH // 2) as it:
                    for half in range(2):
                        pool.wait_ge(late_set, 2 * it + half + 1)
                        pool.sem_inc(gate, 1)
                        for i in range(C):
                            pool.indirect_dma_start(
                                K.rec_d, bass.IndirectOffsetOnAxis(ap=late_i[:, half, i:i + 1], axis=0),
                                late_rec[:, half, i, :], None,
                                bounds_check=T * P - 1, oob_is_err=False).then_inc(late_out[half], 16)
                for half in range(2):
                    pool.wait_ge(late_out[half], 16 * C * NCH // 2)


def load_order(nc, K, k):
    ctx = ExitStack()
    with ctx:
        sb, ps = ctx_tools(nc, ctx)
        groups = [(g * P, min(P, T - g * P)) for g in range(-(-T // P))]
        words = REC_S if k == "s" else REC_D
        rec = K.rec_s if k == "s" else K.rec_d
        rows = sb(f"rows_{k}", [P, 2, P * words], F32 if k == "s" else I32)
        own, other = sb(f"own_rows_{k}", [P, 2, P]), sb(f"other_rows_{k}", [P, 2, P])
        key_rows, len_rows = sb(f"key_rows_{k}", [P, 2, P], BF16), sb(f"len_rows_{k}", [P, 2, P])
        turned = ps(f"turned_{k}", [P, 2, 4, P])
        new = Sems(nc, K.used_sems, f"order_{k}")
        row_in = new("row_in0", "row_in1")
        [local] = new("local")
        turned_in, copied, rows_set = new("turned", "copied", "rows_set")
        key_out, len_out = new("key_out0", "key_out1"), new("len_out0", "len_out1")
        block = ctx.enter_context(nc.Block())

        @block.sync
        def _(sp):
            for n, (t0, nt) in enumerate(groups):
                if n >= 2:
                    sp.wait_ge(turned_in, n - 1)
                    sp.wait_ge(rows_set, n - 1)
                sp.dma_start(rows[0:nt, n % 2, 0:P * words],
                             rec[t0 * P:(t0 + nt) * P, :].rearrange("(t e) w -> t (e w)", e=P)).then_inc(row_in[n % 2], 16)

        @block.tensor
        def _(pe):
            for n, (t0, nt) in enumerate(groups):
                pe.wait_ge(row_in[n % 2], 16 * (n // 2 + 1))
                if n >= 2:
                    pe.wait_ge(copied, n - 1)
                v = rows[0:nt, n % 2, 0:P * words].rearrange("t (e w) -> t w e", w=words)
                if k == "s":
                    sources = [v[:, w, :] for w in (0, 1, REC_S - 1)]
                else:
                    pe.wait_ge(local, n + 1)
                    sources = [own[0:nt, n % 2, :], other[0:nt, n % 2, :]]
                for i, src in enumerate(sources):
                    mm = pe.transpose(turned[:, n % 2, i, 0:nt], src, K.ident[0:nt, 0:nt])
                mm.then_inc(turned_in, 1)

        @block.vector
        def _(dve):
            def localize(n):
                t0, nt = groups[n]
                dve.wait_ge(row_in[n % 2], 16 * (n // 2 + 1))
                if n >= 2:
                    dve.wait_ge(turned_in, n - 1)
                    dve.wait_ge(rows_set, n - 1)
                v = rows[0:nt, n % 2, :].rearrange("t (e w) -> t w e", w=words)
                dve.tensor_scalar(own[0:nt, n % 2, :], v[:, 0, :], K.block_start[0:nt, n:n + 1], None, ALU.subtract)
                dve.tensor_scalar(other[0:nt, n % 2, :], v[:, 1, :], float(N - 1), None, ALU.min).then_inc(local, 1)

            if k == "d":
                localize(0)
            for n, (t0, nt) in enumerate(groups):
                if k == "d" and n + 1 < len(groups):
                    localize(n + 1)
                dve.wait_ge(turned_in, n + 1)
                dve.tensor_copy(K.key[k][:, t0:t0 + nt], turned[:, n % 2, 0, 0:nt])
                last = dve.tensor_copy(K.other[k][:, t0:t0 + nt], turned[:, n % 2, 1, 0:nt])
                if k == "s":
                    last = dve.tensor_copy(K.length[:, t0:t0 + nt], turned[:, n % 2, 2, 0:nt])
                last.then_inc(copied, 1)

        @block.scalar
        def _(act):
            for n, (t0, nt) in enumerate(groups):
                act.wait_ge(row_in[n % 2], 16 * (n // 2 + 1))
                if n >= 2:
                    act.wait_ge(key_out[n % 2], 16 * (n // 2))
                    if k == "s":
                        act.wait_ge(len_out[n % 2], 16 * (n // 2))
                v = rows[0:nt, n % 2, 0:P * words].rearrange("t (e w) -> t w e", w=words)
                if k == "d":
                    act.wait_ge(local, n + 1)
                keys = v[:, 0, :] if k == "s" else own[0:nt, n % 2, :]
                last = nc.scalar.activation(key_rows[0:nt, n % 2, :], keys, ACT.Copy)
                if k == "s":
                    last = nc.scalar.activation(len_rows[0:nt, n % 2, :], v[:, REC_S - 1, :], ACT.Copy)
                last.then_inc(rows_set, 1)

        @block.gpsimd
        def _(pool):
            for n, (t0, nt) in enumerate(groups):
                pool.wait_ge(rows_set, n + 1)
                pool.dma_start(K.key_rows[k][t0:t0 + nt, :], key_rows[0:nt, n % 2, :]).then_inc(key_out[n % 2], 16)
                if k == "s":
                    pool.dma_start(K.len_rows[t0:t0 + nt, :], len_rows[0:nt, n % 2, :]).then_inc(len_out[n % 2], 16)
            for half in range(2):
                times = (len(groups) + 1 - half) // 2
                pool.wait_ge(key_out[half], 16 * times)
                if k == "s":
                    pool.wait_ge(len_out[half], 16 * times)


def sort_in_tiles(nc, K):
    k = "d"
    with ExitStack() as ctx:
        sb, ps = ctx_tools(nc, ctx)
        comp, comp_t = sb("comp", [P, T]), sb("comp_t", [P, 1])
        wide, less, rank, perm = sb("wide", [P, P]), sb("less", [P, P]), sb("rank_in_tile", [P, 1]), sb("perm", [P, P])
        pair, out_rows = sb("pair", [P, 2]), sb("out_rows", [P, P], BF16)
        p_row, p_pair, p_back = ps("p_comp_row", [P, P]), ps("p_pair", [P, 2]), ps("p_key_rows", [P, P])
        groups = [(g * P, min(P, T - g * P)) for g in range(-(-T // P))]
        new = Sems(nc, K.used_sems, "tiles")
        widened, laid_out, ranked, sorted_t, taken, stored, turned, rows_ready, pe_gate, dve_gate = new(
            "widened", "laid_out", "ranked", "sorted_t", "taken", "stored", "turned", "rows_ready", "pe_gate", "dve_gate")
        block = ctx.enter_context(nc.Block())

        @block.vector
        def _(dve):
            with dve.If_ne(disordered(dve, K, "tiles_dve"), 0):
                dve.tensor_scalar(comp[:], K.key[k][:], float(P), K.col[:, 0:1], ALU.mult, ALU.add)
                dve.drain()
                with dve.Fori(0, T) as t:
                    one = bass.ds(t, 1)
                    dve.tensor_copy(comp_t[:], comp[:, one])
                    dve.tensor_copy(pair[:, 0:1], K.key[k][:, one])
                    dve.tensor_copy(pair[:, 1:2], K.other[k][:, one])
                    dve.drain()
                    dve.tensor_scalar(wide[:], K.ones[:], comp_t[:, 0:1], None, ALU.mult).then_inc(widened, 1)
                    dve.wait_ge(laid_out, t + 1)
                    dve.tensor_scalar(less[:], p_row[:], comp_t[:, 0:1], None, ALU.is_lt, ALU.add, accum_out=rank[:])
                    dve.drain()
                    dve.tensor_scalar(perm[:], K.lane[:], rank[:, 0:1], None, ALU.is_equal).then_inc(ranked, 1)
                    dve.wait_ge(sorted_t, t + 1)
                    dve.sem_inc(dve_gate, 1)
                    dve.tensor_copy(K.key[k][:, one], p_pair[:, 0:1])
                    dve.tensor_copy(K.other[k][:, one], p_pair[:, 1:2])
                    dve.drain()
                dve.sem_inc(taken, 1)
                for g, (t0, nt) in enumerate(groups):
                    dve.wait_ge(turned, g + 1)
                    if g:
                        dve.wait_ge(stored, 16 * g)
                    dve.tensor_copy(out_rows[0:nt, :], p_back[0:nt, :]).then_inc(rows_ready, 1)

        @block.tensor
        def _(pe):
            with pe.If_ne(disordered(pe, K, "tiles_pe"), 0):
                with pe.Fori(0, T) as t:
                    pe.wait_ge(widened, t + 1)
                    pe.sem_inc(pe_gate, 1)
                    pe.transpose(p_row[:], wide[:], K.ident[:]).then_inc(laid_out, 1)
                    pe.wait_ge(ranked, t + 1)
                    pe.sem_inc(pe_gate, 1)
                    pe.matmul(p_pair[:], perm[:], pair[:], start=True, stop=True).then_inc(sorted_t, 1)
                pe.wait_ge(taken, 1)
                for g, (t0, nt) in enumerate(groups):
                    if g:
                        pe.wait_ge(rows_ready, g)
                    pe.transpose(p_back[0:nt, :], K.key[k][:, t0:t0 + nt], K.ident[:]).then_inc(turned, 1)

        @block.sync
        def _(sp):
            with sp.If_ne(disordered(sp, K, "tiles_sp"), 0):
                for g, (t0, nt) in enumerate(groups):
                    sp.wait_ge(rows_ready, g + 1)
                    sp.dma_start(K.key_rows[k][t0:t0 + nt, :], out_rows[0:nt, :]).then_inc(stored, 16)
                sp.wait_ge(stored, 16 * len(groups))



def two_by_two(eng, step):
    for s in range(3):
        step(s, s % 2)
    with eng.Fori(1, (NG - 1) // 2) as pair:
        for s in (1, 2):
            step(pair * 2 + s, s % 2)
    step(NG, NG % 2)


def node_pass(nc, K, stage, nodes, outs, clear=None):
    ctx = ExitStack()
    with ctx:
        sb, ps = ctx_tools(nc, ctx)
        group = sb(f"{stage}_group", [P, 2, G, D])
        turned = sb(f"{stage}_turned", [P, 2, G, P])
        result = sb(f"{stage}_result", [P, G, max(o[1] for o in outs)])
        p_turn = ps(f"{stage}_p_turn", [P, 2, 8, P])
        p_out = ps(f"{stage}_p_out", [P, 4, 512])
        new = Sems(nc, K.used_sems, stage)
        picked, turns, turned_in, product, taken, stored = new(
            "picked", "turns", "turned_in", "product", "taken", "stored")
        n_out = len(outs)
        buffered = [i for i, o in enumerate(outs) if isinstance(o[3], tuple) and len(o[3]) == 3]
        drams = [i for i, o in enumerate(outs) if isinstance(o[3], tuple)]
        block = ctx.enter_context(nc.Block())

        apart = all(o[1] <= P for o in outs)

        def bank_of(half, o):
            return 2 * ((half * n_out + o) % 2) if apart else 0

        def product_of(n, i, bank):
            per = 512 // n if n >= 128 else 4
            return p_out[:, bank + i // per, (i % per) * n:(i % per) * n + n]

        @block.scalar
        def _(act):
            def step(s, half):
                if not isinstance(s, int) or s < NG:
                    if over0(s - 1):
                        act.wait_ge(turns, s - 1)
                    nc.scalar.activation(group[:, half], nodes[:, bass.ds(s * G, G), :], ACT.Copy).then_inc(picked, 1)
                if over0(s):
                    act.wait_ge(turns, s)
                    if over0(s - 2):
                        act.wait_ge(product, (s - 2) * n_out)
                    nc.scalar.activation(turned[:, 1 - half], p_turn[:, 1 - half, 0:G, :], ACT.Copy
                                         ).then_inc(turned_in, 1)

            two_by_two(act, step)

        @block.tensor
        def _(pe):
            def step(s, half):
                if not isinstance(s, int) or s < NG:
                    pe.wait_ge(picked, s + 1)
                    if over0(s - 1):
                        pe.wait_ge(turned_in, s - 1)
                    for i in range(G):
                        mm = pe.transpose(p_turn[:, half, i, :], group[:, half, i, :], K.ident[:])
                    mm.then_inc(turns, 1)
                if over0(s):
                    pe.wait_ge(turned_in, s)
                    for o, (w, n, _, _) in enumerate(outs):
                        before = (s - 1) * n_out + o - (1 if apart else 0)
                        if over0(before):
                            pe.wait_ge(taken, before)
                        for i in range(G):
                            mm = pe.matmul(product_of(n, i, bank_of(1 - half, o)), turned[:, 1 - half, i, :], w,
                                           start=True, stop=True)
                        mm.then_inc(product, 1)

            two_by_two(pe, step)

        @block.gpsimd
        def _(pool):
            if clear is not None:
                pool.memset(clear[:], 0.0)

        @block.vector
        def _(dve):
            def body(it, half):
                for o, (_, n, bias, target) in enumerate(outs):
                    dve.wait_ge(product, it * n_out + o + 1)
                    if o in buffered:
                        before = it * len(drams) + drams.index(o)
                        if over0(before):
                            dve.wait_ge(stored, before * 16)
                    per = 512 // n if n >= 128 else 4
                    for a in range(0, G, per):
                        m = min(per, G - a)
                        p = p_out[:, bank_of(half, o) + a // per, 0:m * n].rearrange("p (m n) -> p m n", n=n)
                        whole = target[0] if o in drams and o not in buffered else target
                        dst = result[:, a:a + m, 0:n] if o in buffered else whole[:, bass.ds(it * G + a, m), 0:n]
                        if bias is None:
                            last = dve.tensor_copy(dst, p)
                        elif bias.shape[1] == B:
                            last = dve.tensor_tensor(dst, p, bc_last(bias[:, bass.ds(it * G + a, m)], n), ALU.mult)
                        else:
                            last = dve.tensor_tensor(dst, p, bc_mid(bias, m), ALU.add)
                    last.then_inc(taken, 1)

            two_by_two(dve, lambda s, half: body(s - 1, 1 - half) if over0(s) else None)

        @block.sync
        def _(sp):
            def body(it):
                for o in drams:
                    sp.wait_ge(taken, it * n_out + o + 1)
                    if o in buffered:
                        table, col, width = outs[o][3]
                        src = result[:, :, 0:width]
                    else:
                        (kept, table), col, width = outs[o][3], 0, outs[o][1]
                        src = kept[:, bass.ds(it * G, G), :]
                    rows = table.rearrange("(b n) f -> n b f", n=P)
                    sp.dma_start(rows[:, bass.ds(it * G, G), col:col + width], src).then_inc(stored, 16)

            if drams:
                body(0)
                with sp.Fori(1, NG) as it:
                    body(it)
                sp.wait_ge(stored, 16 * NG * len(drams))


def on_vector(nc, K, stage, program):
    with ExitStack() as ctx:
        new = Sems(nc, K.used_sems, stage)
        chain, asked, answered = new("chain", "asked", "answered")
        block = ctx.enter_context(nc.Block())
        todo = []

        @block.vector
        def _(dve):
            count = [0]

            def link(ins):
                count[0] += 1
                ins.then_inc(chain, 1)
                dve.wait_ge(chain, count[0])

            def scalar_step(out, in_, func, **kw):
                todo.append((out, in_, func, kw))
                dve.sem_inc(asked, 1)
                dve.wait_ge(answered, len(todo))

            program(dve, link, scalar_step)

        @block.scalar
        def _(act):
            for n, (out, in_, func, kw) in enumerate(todo):
                act.wait_ge(asked, n + 1)
                nc.scalar.activation(out, in_, func, **kw).then_inc(answered, 1)


def layer_norm(dve, link, scalar_step, K, t, tmp, scale=None, shift=None):
    mean, var = K.stat[:, 0, :], K.stat[:, 1, :]
    link(dve.tensor_reduce(mean, t, AX.X, ALU.add))
    link(dve.tensor_scalar(mean, mean, 1.0 / D, None, ALU.mult))
    link(dve.tensor_tensor(t, t, bc_last(mean, D), ALU.subtract))
    link(dve.tensor_tensor(tmp, t, t, ALU.mult))
    link(dve.tensor_reduce(var, tmp, AX.X, ALU.add))
    link(dve.tensor_scalar(var, var, 1.0 / D, 1e-5, ALU.mult, ALU.add))
    scalar_step(mean, var, ACT.Sqrt)
    link(dve.reciprocal(var, mean))
    link(dve.tensor_tensor(t, t, bc_last(var, D), ALU.mult))
    if scale is not None:
        link(dve.tensor_tensor(t, t, bc_mid(scale, B), ALU.mult))
        link(dve.tensor_tensor(t, t, bc_mid(shift, B), ALU.add))



class Edges:

    def __init__(self, nc, K, k):
        self.nc, self.K, self.k = nc, K, k

    def pick_others(self, act, out, c):
        return self.nc.scalar.activation(out, self.K.other[self.k][:, bass.ds(c * C, C)], ACT.Copy)

    def one_hot(self, dve, out, c):
        keys = self.K.key[self.k][:, bass.ds(c * C, C)]
        return dve.tensor_tensor(out, bc_mid(self.K.lane[:], C), bc_last(keys, P), ALU.is_equal)

    def load_rows(self, sp, out, c):
        rows = self.K.key_rows[self.k].rearrange("t e -> (t e)")[bass.ds(c * (C * P), C * P)]
        return sp.dma_start(out, rows.unsqueeze(0).to_broadcast([P, C * P]))

    def hot_nodes(self, dve, out, rows):
        return dve.tensor_scalar(out, rows, self.K.col[:, 0:1], None, ALU.is_equal)

    def block_values(self, eng, regs, c):
        eng.load(regs, self.K.blocks[self.k][0:1, bass.ds(c * C, C)])
        return [eng.snap(r, min_val=0, max_val=B - 1) for r in regs]


def edge_pass0(nc, K, own, agg):
    ctx = ExitStack()
    with ctx:
        sb, ps = ctx_tools(nc, ctx)
        ed = Edges(nc, K, "s")
        idx = sb("e0_idx", [P, LANES, C], I32)
        far = sb("e0_far", [P, LANES, C, 2 * D])
        rec = sb("e0_rec", [P, LANES, C * REC_S])
        S = sb("e0_S", [P, 4, C, P])
        rows = sb("e0_rows", [P, LANES, C * P], BF16)
        ST = sb("e0_ST", [P, 2, C * P])
        parts = sb("e0_parts", [P, 2, C, PARTS], BF16)
        rest = sb("e0_rest", [P, 2, C, EF])
        FT = sb("e0_FT", [P, 2, C // 2, P], BF16)
        z = sb("e0_z", [P, 2, C, 2 * D])
        soft = sb("e0_soft", [P, 2, C, 2 * D])
        low = sb("e0_low", [P, 2, C, D])
        p_feat = ps("e0_p_feat", [P, 2, C // 2, 4 * P], BF16)
        p_z = ps("e0_p_z", [P, 2, C, 2 * D])
        p_agg = ps("e0_p_agg", [P, 2, C, D])
        new = Sems(nc, K.used_sems, "e0")
        picked, gate = new("picked", "gate")
        rows_in = new("row_in0", "row_in1", "row_in2", "row_in3")
        recs_in = new("rec_in0", "rec_in1", "rec_in2", "rec_in3")
        far_in = new("far_in0", "far_in1", "far_in2", "far_in3")
        hot, turned, kept, z_done, z_read, abs_done, exp_done, ln_done = new(
            "hot", "turned", "kept", "z_done", "z_read", "abs_done", "exp_done", "ln_done")
        turned_hot, split, split_steps, cleared = new("turned_hot", "split", "split_steps", "cleared")
        halves, sig_done, msg_done, summed, added = new("halves", "sig_done", "msg_done", "summed", "added")
        block = ctx.enter_context(nc.Block())

        @block.gpsimd
        def _(pool):
            def body(it):
                for lane in range(LANES):
                    if (at := at_stage(it, lane, 0)) is not None:
                        c, l = at
                        pool.wait_ge(picked, c + 1)
                        if over0(c - LANES + 1):
                            pool.wait_ge(z_read, c - LANES + 1)
                        pool.sem_inc(gate, 1)
                        for i in range(C):
                            pool.indirect_dma_start(far[:, l, i, :], None, K.table0,
                                                    bass.IndirectOffsetOnAxis(ap=idx[:, l, i:i + 1], axis=0)
                                                    ).then_inc(far_in[l], 16)

            chunk_loop(pool, body)

        @block.sync
        def _(sp):
            chunks = K.rec_s.rearrange("(c t e) w -> e c t w", t=C, e=P)

            def body(it):
                for lane in range(LANES):
                    if (at := at_stage(it, lane, 0)) is not None:
                        c, l = at
                        if over0(c - LANES + 1):
                            sp.wait_ge(split, c - LANES + 1)
                            sp.wait_ge(turned_hot, c - LANES + 1)
                        ed.load_rows(sp, rows[:, l, :], c).then_inc(rows_in[l], 16)
                        sp.dma_start(rec[:, l, :].rearrange("p (o t w) -> p o t w", o=1, t=C),
                                     chunks[:, bass.ds(c, 1), :, :]).then_inc(recs_in[l], 16)

            chunk_loop(sp, body)

        @block.scalar
        def _(act):
            act.preload_act_table_set(EXP_LN_SET)

            def body(it):
                for lane in range(LANES):
                    if (at := at_stage(it, lane, 0)) is not None:
                        c, l = at
                        if over0(c - LANES + 1):
                            act.wait_ge(far_in[l], 64 * (lane_turn(it, lane, 0) - 1))
                        ed.pick_others(act, idx[:, l, :], c).then_inc(picked, 1)
                    if (at := at_stage(it, lane, 2)) is not None:
                        c, l = at
                        act.wait_ge(turned, c + 1)
                        if over0(c - 1):
                            act.wait_ge(z_done, c - 1)
                        nc.scalar.activation(FT[:, l % 2], p_feat[:, l % 2, :, 0:P], ACT.Copy).then_inc(kept, 1)
                    if (at := at_stage(it, lane, 4)) is not None:
                        c, l = at
                        act.wait_ge(halves, 2 * c + 1)
                        nc.scalar.activation(low[:, l % 2], low[:, l % 2], ACT.Exp).then_inc(sig_done, 1)
                    if (at := at_stage(it, lane, 3)) is not None:
                        c, l = at
                        act.wait_ge(z_read, c + 1)
                        nc.scalar.activation(soft[:, l % 2], z[:, l % 2], ACT.Abs).then_inc(abs_done, 1)
                        act.wait_ge(abs_done, c + 1)
                        nc.scalar.activation(soft[:, l % 2], soft[:, l % 2], ACT.Exp, scale=-1.0).then_inc(exp_done, 1)
                        act.wait_ge(exp_done, c + 1)
                        nc.scalar.activation(soft[:, l % 2], soft[:, l % 2], ACT.Ln, bias=1.0).then_inc(ln_done, 1)

            chunk_loop(act, body)

        @block.tensor
        def _(pe):
            regs = [pe.alloc_register(f"e0_pe{i}") for i in range(C)]

            def body(it):
                for lane in range(LANES):
                    if (at := at_stage(it, lane, 2)) is not None:
                        c, l = at
                        pe.wait_ge(split, c + 1)
                        if over0(c - 1):
                            pe.wait_ge(kept, c - 1)
                        for j in range(C // 2):
                            mm = pe.transpose(p_feat[:, l % 2, j, 0:P],
                                              parts[:, l % 2, 2 * j:2 * j + 2, :].rearrange("p t w -> p (t w)"),
                                              K.ident_bf[:])
                        mm.then_inc(turned, 1)
                    if (at := at_stage(it, lane, 3)) is not None:
                        c, l = at
                        blocks = ed.block_values(pe, regs, c)
                        pe.wait_ge(kept, c + 1)
                        pe.wait_ge(turned_hot, c + 1)
                        if over0(c - 1):
                            pe.wait_ge(z_read, c - 1)
                        for i in range(C):
                            pe.matmul(p_z[:, l % 2, i, :], ST[:, l % 2, i * P:(i + 1) * P],
                                      own[:, bass.ds(blocks[i], 1), :], start=True, stop=False)
                            mm = pe.matmul(p_z[:, l % 2, i, :], FT[:, l % 2, i // 2, :],
                                           K.w_ef_parts[:, i % 2], start=False, stop=True)
                        mm.then_inc(z_done, 1)
                    if (at := at_stage(it, lane, 5)) is not None:
                        c, l = at
                        pe.wait_ge(hot, c + 1)
                        pe.wait_ge(msg_done, c + 1)
                        if over0(C * (c - 1)):
                            pe.wait_ge(added, C * (c - 1))
                        for i in range(C):
                            mm = pe.matmul(p_agg[:, l % 2, i, :], S[:, l, i, :], low[:, l % 2, i, :],
                                           start=True, stop=True)
                        mm.then_inc(summed, 1)

            chunk_loop(pe, body)

        @block.vector
        def _(dve):
            regs = [dve.alloc_register(f"e0_dve{i}") for i in range(C)]

            dve.memset(parts[:], 0.0).then_inc(cleared, 1)
            dve.wait_ge(cleared, 1)

            def split_step(step, c, l, turn):
                h = l % 2
                feats = rec[:, l, :].rearrange("p (t w) -> p t w", w=REC_S)[:, :, 2:2 + EF]
                high, mid, low_part = (parts[:, h, :, a * EF:b * EF] for a, b in ((0, 3), (3, 5), (5, 6)))
                if step == 0:
                    dve.wait_ge(recs_in[l], turn)
                    if over0(c - 1):
                        dve.wait_ge(turned, c - 1)
                    dve.tensor_copy(high.rearrange("p t (r f) -> p t r f", f=EF),
                                    feats.unsqueeze(2).to_broadcast([P, C, 3, EF])).then_inc(split_steps, 1)
                    return
                dve.wait_ge(split_steps, 3 * c + step)
                if step == 1:
                    dve.tensor_tensor(rest[:, h], feats, high[:, :, 0:EF], ALU.subtract).then_inc(split_steps, 1)
                elif step == 2:
                    dve.tensor_copy(mid.rearrange("p t (r f) -> p t r f", f=EF),
                                    rest[:, h].unsqueeze(2).to_broadcast([P, C, 2, EF])).then_inc(split_steps, 1)
                else:
                    dve.tensor_tensor(low_part, rest[:, h], mid[:, :, 0:EF], ALU.subtract).then_inc(split, 1)

            def body(it):
                for lane in range(LANES):
                    to_split, to_mark, to_read, to_gate, to_add = (at_stage(it, lane, lag) for lag in (1, 2, 3, 4, 6))
                    turn = 16 * lane_turn(it, lane, 1)
                    if to_add is not None:
                        c, l = to_add
                        blocks = ed.block_values(dve, regs, c)
                        dve.wait_ge(summed, c + 1)
                        add_block(dve, blocks, 0, c, agg, p_agg[:, l % 2], D, added)
                    if to_split is not None:
                        split_step(0, *to_split, turn)
                    if to_mark is not None:
                        c, l = to_mark
                        if over0(c - LANES + 1):
                            dve.wait_ge(summed, c - LANES + 1)
                        ed.one_hot(dve, S[:, l], c).then_inc(hot, 1)
                    if to_add is not None:
                        add_block(dve, blocks, 1, to_add[0], agg, p_agg[:, to_add[1] % 2], D, added)
                    if to_split is not None:
                        split_step(1, *to_split, turn)
                    if to_mark is not None:
                        c, l = to_mark
                        dve.wait_ge(rows_in[l], 16 * lane_turn(it, lane, 2))
                        if over0(c - 1):
                            dve.wait_ge(z_done, c - 1)
                        ed.hot_nodes(dve, ST[:, l % 2, :], rows[:, l, :]).then_inc(turned_hot, 1)
                    if to_add is not None:
                        add_block(dve, blocks, 2, to_add[0], agg, p_agg[:, to_add[1] % 2], D, added)
                    if to_split is not None:
                        split_step(2, *to_split, turn)
                    if to_gate is not None:
                        c, l = to_gate
                        dve.wait_ge(ln_done, c + 1)
                        if over0(c - 1):
                            dve.wait_ge(summed, c - 1)
                        dve.scalar_tensor_tensor(out=low[:, l % 2], in0=z[:, l % 2, :, 0:D], scalar=0.0,
                                                 in1=soft[:, l % 2, :, 0:D], op0=ALU.min, op1=ALU.subtract
                                                 ).then_inc(halves, 1)
                    if to_add is not None:
                        add_block(dve, blocks, 3, to_add[0], agg, p_agg[:, to_add[1] % 2], D, added)
                    if to_split is not None:
                        split_step(3, *to_split, turn)
                    if to_gate is not None:
                        c, l = to_gate
                        dve.scalar_tensor_tensor(out=z[:, l % 2, :, D:2 * D], in0=z[:, l % 2, :, D:2 * D], scalar=0.0,
                                                 in1=soft[:, l % 2, :, D:2 * D], op0=ALU.max, op1=ALU.add
                                                 ).then_inc(halves, 1)
                    if to_read is not None:
                        c, l = to_read
                        dve.wait_ge(z_done, c + 1)
                        dve.wait_ge(far_in[l], 64 * lane_turn(it, lane, 3))
                        dve.tensor_tensor(z[:, l % 2], p_z[:, l % 2], far[:, l], ALU.add).then_inc(z_read, 1)
                    if to_gate is not None:
                        c, l = to_gate
                        dve.wait_ge(sig_done, c + 1)
                        dve.wait_ge(halves, 2 * c + 2)
                        dve.tensor_tensor(low[:, l % 2], low[:, l % 2], z[:, l % 2, :, D:2 * D], ALU.mult).then_inc(msg_done, 1)

            chunk_loop(dve, body)


def lane_turn(it, lane, lag):
    return (LANES * it + lane - lag) // LANES + 1 if isinstance(it, int) else it + (lane - lag) // LANES + 1


def add_block(dve, blocks, i, c, agg, p, n, added):
    if over0(C * c + i):
        dve.wait_ge(added, C * c + i)
    dst = agg[:, bass.ds(blocks[i], 1), 0:n]
    dve.tensor_tensor(dst, dst, p[:, i:i + 1, 0:n], ALU.add).then_inc(added, 1)


def add_to_blocks(dve, ed, regs, c, agg, p, n, summed, added):
    blocks = ed.block_values(dve, regs, c)
    dve.wait_ge(summed, c + 1)
    for i in range(C):
        add_block(dve, blocks, i, c, agg, p, n, added)


def add_to_pair(pool, ed, regs, c, pair, sums, summed, added):
    blocks = ed.block_values(pool, regs, c)
    pool.wait_ge(summed, c + 1)
    for i in range(C):
        if over0(C * c + i - 1):
            pool.wait_ge(added, C * c + i - 1)
        dst = pair[i % 2][:, bass.ds(blocks[i], 1), :]
        pool.tensor_tensor(dst, dst, sums[:, i:i + 1, :], ALU.add).then_inc(added, 1)


def layer0(nc, K, x):
    with ExitStack() as ctx:
        agg = ctx.enter_context(nc.sbuf_tensor("agg0", [P, B, D], F32))
        with ExitStack() as inner:
            own = inner.enter_context(nc.sbuf_tensor("own0", [P, B, 2 * D], F32))
            node_pass(nc, K, "n0", x, [(K.w("own0"), 2 * D, K.v("b0"), own),
                                            (K.w("other0"), 2 * D, None, (K.table0, 0, 2 * D))], clear=agg)
            edge_pass0(nc, K, own, agg)
        tmp = ctx.enter_context(nc.sbuf_tensor("tmp0", [P, B, D], F32))
        batch_norm(nc, K, agg, tmp)

        def program(dve, link, scalar_step):
            link(dve.tensor_tensor(agg[:], agg[:], bc_mid(K.v("bn_b"), B), ALU.add))
            link(dve.tensor_tensor(agg[:], agg[:], x[:], ALU.add))
            scalar_step(tmp[:], agg[:], ACT.Abs)
            scalar_step(tmp[:], tmp[:], ACT.Exp, scale=-1.0)
            scalar_step(tmp[:], tmp[:], ACT.Ln, bias=1.0)
            link(dve.scalar_tensor_tensor(out=agg[:], in0=agg[:], scalar=0.0, in1=tmp[:], op0=ALU.max, op1=ALU.add))
            link(dve.tensor_tensor(x[:], x[:], agg[:], ALU.add))
            layer_norm(dve, link, scalar_step, K, x[:], tmp[:])

        on_vector(nc, K, "f0", program)


def batch_norm(nc, K, agg, tmp):
    with ExitStack() as ctx:
        sb, ps = ctx_tools(nc, ctx)
        p_sum = ps("bn_p_sum", [P, 2, 512])
        mean, rstd, by_row = sb("bn_mean", [P, D]), sb("bn_rstd", [P, D]), sb("bn_by_row", [P, D])
        new = Sems(nc, K.used_sems, "bn")
        chain, mean_sum, summed_rows, var_sum, asked, rooted = new("chain", "mean_sum", "summed_rows", "var_sum", "asked", "rooted")
        block = ctx.enter_context(nc.Block())

        @block.tensor
        def _(pe):
            for n, done in enumerate((mean_sum, var_sum)):
                pe.wait_ge(summed_rows, n + 1)
                pe.matmul(p_sum[:, n, 0:D], K.ones[:], by_row[:], start=True, stop=True).then_inc(done, 1)

        @block.scalar
        def _(act):
            act.wait_ge(asked, 1)
            nc.scalar.activation(mean[:], rstd[:], ACT.Sqrt).then_inc(rooted, 1)

        @block.vector
        def _(dve):
            count = [0]

            def link(ins):
                count[0] += 1
                ins.then_inc(chain, 1)
                dve.wait_ge(chain, count[0])

            def sum_rows(src):
                link(dve.tensor_reduce(by_row[:], src[:, 0:B - 1, :].rearrange("p b d -> p d b"), AX.X, ALU.add))
                link(dve.tensor_tensor(by_row[0:LAST, :], by_row[0:LAST, :], src[0:LAST, B - 1, :], ALU.add))
                dve.sem_inc(summed_rows, 1)

            sum_rows(agg)
            dve.wait_ge(mean_sum, 1)
            link(dve.tensor_scalar(mean[:], p_sum[:, 0, 0:D], 1.0 / N, None, ALU.mult))
            link(dve.tensor_tensor(agg[:], agg[:], bc_mid(mean[:], B), ALU.subtract))
            link(dve.tensor_tensor(tmp[:], agg[:], agg[:], ALU.mult))
            sum_rows(tmp)
            dve.wait_ge(var_sum, 1)
            dve.tensor_scalar(rstd[:], p_sum[:, 1, 0:D], 1.0 / N, 1e-5, ALU.mult, ALU.add).then_inc(asked, 1)
            dve.wait_ge(rooted, 1)
            link(dve.reciprocal(rstd[:], mean[:]))
            link(dve.tensor_tensor(rstd[:], rstd[:], K.v("bn_g"), ALU.mult))
            link(dve.tensor_tensor(agg[:], agg[:], bc_mid(rstd[:], B), ALU.mult))



def edge_pass1a(nc, K, peak):
    ctx = ExitStack()
    with ctx:
        sb, ps = ctx_tools(nc, ctx)
        ed = Edges(nc, K, "d")
        R = C * H
        idx = sb("m1_idx", [P, LANES, C], I32)
        far = sb("m1_far", [P, LANES, C, D + H])
        S = sb("m1_S", [P, 2, C, P])
        a_u = sb("m1_au", [P, 2, C, H])
        keys = sb("m1_keys", [P, 2, C, H])
        same = sb("m1_same", [R, 2, P + 1])
        reset = sb("m1_reset", [R, 2, P])
        run = sb("m1_run", [R, 2, P])
        kt = sb("m1_kt", [R, 2, P])
        ends = sb("m1_ends", [R, 2, 2, P])
        back = sb("m1_back", [P, 2, 2, R])
        miss = sb("m1_miss", [P, 2, C, H])
        cand = sb("m1_cand", [P, 2, C, H])
        p_turn = ps("m1_p_turn", [R, 2, 2, 2 * P])
        p_back = ps("m1_p_back", [P, 2, 2, 4 * R * 2])
        p_max = ps("m1_p_max", [P, 2, C, 2 * P])
        new = Sems(nc, K.used_sems, "m1")
        picked, gate = new("picked", "gate")
        far_in = new("far_in0", "far_in1", "far_in2", "far_in3")
        spilled = new("spilled0", "spilled1", "spilled2", "spilled3")
        hot, laid, turned, scanned, scan_steps, returned, copied, spread, maxed = new(
            "hot", "laid", "turned", "scanned", "scan_steps", "returned", "copied", "spread", "maxed")
        cleared, cand_steps, pe_gate = new("cleared", "cand_steps", "pe_gate")
        block = ctx.enter_context(nc.Block())

        @block.gpsimd
        def _(pool):
            def body(it):
                for lane in range(LANES):
                    if (at := at_stage(it, lane, 0)) is not None:
                        c, l = at
                        pool.wait_ge(picked, c + 1)
                        if over0(c - LANES + 1):
                            pool.wait_ge(laid, c - LANES + 1)
                            pool.wait_ge(spilled[l], 16 * (lane_turn(it, lane, 0) - 1))
                        pool.sem_inc(gate, 1)
                        for i in range(C):
                            pool.indirect_dma_start(far[:, l, i, :], None, K.table1,
                                                    bass.IndirectOffsetOnAxis(ap=idx[:, l, i:i + 1], axis=0)
                                                    ).then_inc(far_in[l], 16)

            chunk_loop(pool, body)

        @block.sync
        def _(sp):
            chunks = K.spill1.rearrange("(c e t) w -> e c t w", t=C, e=P)

            def body(it):
                for lane in range(LANES):
                    if (at := at_stage(it, lane, 2)) is not None:
                        c, l = at
                        sp.wait_ge(far_in[l], 64 * lane_turn(it, lane, 2))
                        sp.dma_start(chunks[:, bass.ds(c, 1), :, :].rearrange("e c t w -> e c (t w)"),
                                     far[:, l:l + 1, :, :].rearrange("p o t w -> p o (t w)")).then_inc(spilled[l], 16)

            chunk_loop(sp, body)
            for l in range(LANES):
                sp.wait_ge(spilled[l], 16 * ITERS)

        @block.scalar
        def _(act):
            def body(it):
                for lane in range(LANES):
                    if (at := at_stage(it, lane, 0)) is not None:
                        c, l = at
                        if over0(c - LANES + 1):
                            act.wait_ge(far_in[l], 64 * (lane_turn(it, lane, 0) - 1))
                        ed.pick_others(act, idx[:, l, :], c).then_inc(picked, 1)
                    if (at := at_stage(it, lane, 2)) is not None:
                        c, l = at
                        act.wait_ge(far_in[l], 64 * lane_turn(it, lane, 2))
                        if over0(c - 1):
                            act.wait_ge(turned, c - 1)
                        nc.scalar.activation(keys[:, l % 2], bc_last(K.key["d"][:, bass.ds(c * C, C)], H), ACT.Copy)
                        nc.scalar.activation(a_u[:, l % 2], far[:, l, :, D:D + H], ACT.Copy).then_inc(laid, 1)
                    if (at := at_stage(it, lane, 3)) is not None:
                        c, l = at
                        act.wait_ge(returned, c + 1)
                        if over0(c - 1):
                            act.wait_ge(spread, c - 1)
                        nc.scalar.activation(back[:, l % 2], p_back[:, l % 2, :, 0:R], ACT.Copy).then_inc(copied, 1)

            chunk_loop(act, body)

        @block.tensor
        def _(pe):
            def body(it):
                for lane in range(LANES):
                    if (at := at_stage(it, lane, 2)) is not None:
                        c, l = at
                        pe.wait_ge(laid, c + 1)
                        if over0(c - 1):
                            pe.wait_ge(scanned, c - 1)
                        pe.transpose(p_turn[:, l % 2, 0, 0:P], a_u[:, l % 2].rearrange("p t h -> p (t h)"), K.ident[:])
                        pe.transpose(p_turn[:, l % 2, 1, 0:P], keys[:, l % 2].rearrange("p t h -> p (t h)"), K.ident[:]
                                     ).then_inc(turned, 1)
                    if (at := at_stage(it, lane, 3)) is not None:
                        c, l = at
                        pe.wait_ge(scanned, c + 1)
                        if over0(c - 1):
                            pe.wait_ge(copied, c - 1)
                        pe.sem_inc(pe_gate, 1)
                        pe.transpose(p_back[:, l % 2, 0, 0:R], ends[:, l % 2, 0, :], K.ident[0:R, 0:R])
                        pe.transpose(p_back[:, l % 2, 1, 0:R], ends[:, l % 2, 1, :], K.ident[0:R, 0:R]).then_inc(returned, 1)
                    if (at := at_stage(it, lane, 4)) is not None:
                        c, l = at
                        pe.wait_ge(hot, c + 1)
                        pe.wait_ge(copied, c + 1)
                        if over0(c - 1):
                            pe.wait_ge(cand_steps, 2 * (c - 1))
                        for i in range(C):
                            mm = pe.matmul(p_max[:, l % 2, i, 0:2 * H],
                                           S[:, l % 2, i, :], back[:, l % 2, :, i * H:(i + 1) * H], start=True, stop=True)
                        mm.then_inc(spread, 1)

            chunk_loop(pe, body)

        @block.vector
        def _(dve):
            regs = [dve.alloc_register(f"m1_dve{i}") for i in range(C)]
            dve.memset(peak[:], -BIG).then_inc(cleared, 1)
            dve.memset(same[:], 0.0).then_inc(cleared, 1)
            dve.wait_ge(cleared, 2)

            def body(it):
                for lane in range(LANES):
                    if (at := at_stage(it, lane, 3)) is not None:
                        c, l = at
                        h = l % 2
                        dve.wait_ge(turned, c + 1)
                        if over0(c - 1):
                            dve.wait_ge(returned, c - 1)
                        dve.tensor_copy(kt[:, h, :], p_turn[:, h, 1, 0:P]).then_inc(scan_steps, 1)
                        dve.wait_ge(scan_steps, 4 * c + 1)
                        dve.tensor_tensor(same[:, h, 1:P], kt[:, h, 1:P], kt[:, h, 0:P - 1], ALU.is_equal
                                          ).then_inc(scan_steps, 1)
                        dve.wait_ge(scan_steps, 4 * c + 2)
                        dve.tensor_scalar(ends[:, h, 1, :], same[:, h, 1:P + 1], -1.0, 1.0, ALU.mult, ALU.add)
                        dve.tensor_scalar(reset[:, h, :], same[:, h, 0:P], -1.0, BIG, ALU.add, ALU.mult
                                          ).then_inc(scan_steps, 1)
                        dve.wait_ge(scan_steps, 4 * c + 3)
                        dve.tensor_tensor_scan(run[:, h, :], reset[:, h, :], p_turn[:, h, 0, 0:P], -BIG, ALU.add, ALU.max
                                               ).then_inc(scan_steps, 1)
                        dve.wait_ge(scan_steps, 4 * c + 4)
                        dve.tensor_tensor(ends[:, h, 0, :], run[:, h, :], ends[:, h, 1, :], ALU.mult).then_inc(scanned, 1)
                    if (at := at_stage(it, lane, 3)) is not None:
                        c, l = at
                        if over0(c - 1):
                            dve.wait_ge(spread, c - 1)
                        ed.one_hot(dve, S[:, l % 2], c).then_inc(hot, 1)
                    if (at := at_stage(it, lane, 5)) is not None:
                        c, l = at
                        h = l % 2
                        blocks = ed.block_values(dve, regs, c)
                        dve.wait_ge(spread, c + 1)
                        dve.tensor_scalar(miss[:, h], p_max[:, h, :, H:2 * H], -1.0, BIG, ALU.add, ALU.mult
                                          ).then_inc(cand_steps, 1)
                        dve.wait_ge(cand_steps, 2 * c + 1)
                        dve.tensor_tensor(cand[:, h], p_max[:, h, :, 0:H], miss[:, h], ALU.add).then_inc(cand_steps, 1)
                        dve.wait_ge(cand_steps, 2 * c + 2)
                        for i in range(C):
                            if over0(C * c + i):
                                dve.wait_ge(maxed, C * c + i)
                            dst = peak[:, bass.ds(blocks[i], 1), :]
                            dve.tensor_tensor(dst, dst, cand[:, h, i:i + 1, :], ALU.max).then_inc(maxed, 1)

            chunk_loop(dve, body)


def edge_pass1b(nc, K, own, agg):
    ctx = ExitStack()
    with ctx:
        sb, ps = ctx_tools(nc, ctx)
        ed = Edges(nc, K, "d")
        M = D + H + 1
        far = sb("a1_far", [P, LANES, C, D + H])
        S = sb("a1_S", [P, 4, C, P])
        rows = sb("a1_rows", [P, LANES, C * P], BF16)
        ST = sb("a1_ST", [P, 2, C * P], BF16)
        score = sb("a1_score", [P, 2, C, H])
        shifted = sb("a1_shifted", [P, 2, C, H])
        msg = sb("a1_msg", [P, 2, C, M])
        p_own = ps("a1_p_own", [P, 2, C, P])
        sums = sb("a1_sums", [P, 2, C, M])
        p_agg = ps("a1_p_agg", [P, 2, C, 2 * P])
        new = Sems(nc, K.used_sems, "a1")
        far_in = new("far_in0", "far_in1", "far_in2", "far_in3")
        rows_in = new("row_in0", "row_in1", "row_in2", "row_in3")
        hot, turned_hot, owned, steps, exped, msg_done, summed, added, cleared = new(
            "hot", "turned_hot", "owned", "steps", "exped", "msg_done", "summed", "added", "cleared")
        [agg_clear] = new("agg_clear")
        [sums_out] = new("sums_out")
        block = ctx.enter_context(nc.Block())

        @block.sync
        def _(sp):
            chunks = K.spill1.rearrange("(c e t) w -> e c t w", t=C, e=P)

            def body(it):
                for lane in range(LANES):
                    if (at := at_stage(it, lane, 0)) is not None:
                        c, l = at
                        if over0(c - LANES + 1):
                            sp.wait_ge(turned_hot, c - LANES + 1)
                        ed.load_rows(sp, rows[:, l, :], c).then_inc(rows_in[l], 16)
                        if over0(c - LANES + 1):
                            sp.wait_ge(msg_done, c - LANES + 1)
                        sp.dma_start(far[:, l:l + 1, :, :].rearrange("p o t w -> p o (t w)"),
                                     chunks[:, bass.ds(c, 1), :, :].rearrange("e c t w -> e c (t w)")
                                     ).then_inc(far_in[l], 16)

            chunk_loop(sp, body)

        @block.scalar
        def _(act):
            def body(it):
                for lane in range(LANES):
                    if (at := at_stage(it, lane, 3)) is not None:
                        c, l = at
                        act.wait_ge(steps, 4 * (c + 1))
                        if over0(c - 1):
                            act.wait_ge(summed, c - 1)
                        nc.scalar.activation(msg[:, l % 2, :, D:D + H], shifted[:, l % 2], ACT.Exp).then_inc(exped, 1)
                    if (at := at_stage(it, lane, 5)) is not None:
                        c, l = at
                        act.wait_ge(summed, c + 1)
                        if over0(C * (c - 1)):
                            act.wait_ge(added, C * (c - 1))
                        nc.scalar.activation(sums[:, l % 2], p_agg[:, l % 2, :, 0:M], ACT.Copy).then_inc(sums_out, 1)

            chunk_loop(act, body)

        @block.tensor
        def _(pe):
            regs = [pe.alloc_register(f"a1_pe{i}") for i in range(C)]

            def body(it):
                for lane in range(LANES):
                    if (at := at_stage(it, lane, 3)) is not None:
                        c, l = at
                        blocks = ed.block_values(pe, regs, c)
                        pe.wait_ge(turned_hot, c + 1)
                        if over0(c - 1):
                            pe.wait_ge(steps, 4 * (c - 1))
                        for i in range(C):
                            for part in range(3):
                                mm = pe.matmul(p_own[:, l % 2, i, 0:2 * H], ST[:, l % 2, i * P:(i + 1) * P],
                                               own[:, bass.ds(blocks[i], 1), part, :],
                                               start=(part == 0), stop=(part == 2))
                        mm.then_inc(owned, 1)
                    if (at := at_stage(it, lane, 5)) is not None:
                        c, l = at
                        pe.wait_ge(hot, c + 1)
                        pe.wait_ge(msg_done, c + 1)
                        if over0(c - 1):
                            pe.wait_ge(sums_out, c - 1)
                        for i in range(C):
                            mm = pe.matmul(p_agg[:, l % 2, i, 0:M], S[:, l, i, :], msg[:, l % 2, i, :],
                                           start=True, stop=True)
                        mm.then_inc(summed, 1)

            chunk_loop(pe, body)

        @block.vector
        def _(dve):
            dve.memset(msg[:], 1.0).then_inc(cleared, 1)
            dve.wait_ge(cleared, 1)

            def body(it):
                for lane in range(LANES):
                    to_mark, to_score, to_weigh = (at_stage(it, lane, lag) for lag in (2, 3, 4))
                    if to_mark is not None:
                        c, l = to_mark
                        if over0(c - LANES + 1):
                            dve.wait_ge(summed, c - LANES + 1)
                        ed.one_hot(dve, S[:, l], c).then_inc(hot, 1)
                    if to_mark is not None:
                        c, l = to_mark
                        dve.wait_ge(rows_in[l], 16 * lane_turn(it, lane, 2))
                        if over0(c - 1):
                            dve.wait_ge(owned, c - 1)
                        ed.hot_nodes(dve, ST[:, l % 2, :], rows[:, l, :]).then_inc(turned_hot, 1)
                    if to_score is not None:
                        c, l = to_score
                        h = l % 2
                        dve.wait_ge(owned, c + 1)
                        dve.wait_ge(far_in[l], 16 * lane_turn(it, lane, 3))
                        if over0(c - 1):
                            dve.wait_ge(exped, c - 1)
                        dve.tensor_tensor(score[:, h], p_own[:, h, :, 0:H], far[:, l, :, D:D + H], ALU.add
                                          ).then_inc(steps, 1)
                    if to_weigh is not None:
                        c, l = to_weigh
                        h = l % 2
                        dve.wait_ge(exped, c + 1)
                        ex = msg[:, h, :, D:D + H].unsqueeze(2).to_broadcast([P, C, HD, H])
                        dve.tensor_tensor(msg[:, h, :, 0:D].rearrange("p t (d h) -> p t d h", h=H),
                                          far[:, l, :, 0:D].rearrange("p t (d h) -> p t d h", h=H), ex, ALU.mult
                                          ).then_inc(msg_done, 1)
                    if to_score is not None:
                        c, l = to_score
                        h = l % 2
                        dve.wait_ge(steps, 4 * c + 1)
                        dve.scalar_tensor_tensor(out=shifted[:, h], in0=score[:, h], scalar=0.2, in1=score[:, h],
                                                 op0=ALU.mult, op1=ALU.max).then_inc(steps, 1)
                    if to_score is not None:
                        c, l = to_score
                        h = l % 2
                        dve.wait_ge(steps, 4 * c + 2)
                        dve.tensor_tensor(score[:, h], shifted[:, h], p_own[:, h, :, H:2 * H], ALU.subtract
                                          ).then_inc(steps, 1)
                    if to_score is not None:
                        c, l = to_score
                        h = l % 2
                        dve.wait_ge(steps, 4 * c + 3)
                        dve.tensor_scalar(shifted[:, h], score[:, h], 0.0, None, ALU.min).then_inc(steps, 1)

            chunk_loop(dve, body)

        @block.gpsimd
        def _(pool):
            regs = [pool.alloc_register(f"a1_pool{i}") for i in range(C)]
            for sums_of in agg:
                pool.memset(sums_of[:], 0.0).then_inc(agg_clear, 1)
            pool.wait_ge(agg_clear, 2)

            def body(it):
                for lane in range(LANES):
                    if (at := at_stage(it, lane, 5)) is not None:
                        c, l = at
                        add_to_pair(pool, ed, regs, c, agg, sums[:, l % 2], sums_out, added)

            chunk_loop(pool, body)


def layer1(nc, K, x, root):
    with ExitStack() as ctx:
        sb, _ = ctx_tools(nc, ctx)
        peak, own = sb("peak1", [P, B, H]), sb("own1", [P, B, 2 * H])
        with ExitStack() as inner:
            h = inner.enter_context(nc.sbuf_tensor("h1", [P, B, D], F32))
            node_pass(nc, K, "n1h", x, [(K.w("in1"), D, K.v("b_in1"), (h, K.table1))])
            node_pass(nc, K, "n1a", h, [(K.w("a1"), 2 * H, K.v("b_a1"), own),
                                             (K.w("a1"), 2 * H, K.v("b_a1"), (K.table1, D, H))])
        edge_pass1a(nc, K, peak)
        agg = sb("agg1", [P, B, D + H + 1])

        def largest(dve, link, scalar_step):
            link(dve.tensor_copy(own[:, :, 0:H], own[:, :, H:2 * H]))
            link(dve.tensor_tensor(peak[:], peak[:], own[:, :, 0:H], ALU.add))
            link(dve.scalar_tensor_tensor(out=own[:, :, H:2 * H], in0=peak[:], scalar=0.2, in1=peak[:],
                                          op0=ALU.mult, op1=ALU.max))

        on_vector(nc, K, "f1a", largest)
        with ExitStack() as inner:
            own_parts = inner.enter_context(nc.sbuf_tensor("own1_parts", [P, B, 3, 2 * H], BF16))
            odd = inner.enter_context(nc.sbuf_tensor("agg1_odd", [P, B, D + H + 1], F32))

            def split(dve, link, scalar_step):
                for part in range(3):
                    link(dve.tensor_copy(own_parts[:, :, part, :], own[:]))
                    if part < 2:
                        link(dve.tensor_tensor(own[:], own[:], own_parts[:, :, part, :], ALU.subtract))

            on_vector(nc, K, "f1s", split)
            edge_pass1b(nc, K, own_parts, (agg, odd))
            on_vector(nc, K, "f1o", lambda dve, link, scalar_step:
                      link(dve.tensor_tensor(agg[:], agg[:], odd[:], ALU.add)))
        y, tmp = sb("y1", [P, B, D]), sb("tmp1", [P, B, D])

        def divide(dve, link, scalar_step):
            link(dve.tensor_scalar(peak[:], agg[:, :, D:D + H], 1e-30, None, ALU.max))
            link(dve.reciprocal(peak[:], peak[:]))
            for b in range(HD):
                link(dve.tensor_tensor(y[:, :, b * H:(b + 1) * H], agg[:, :, b * H:(b + 1) * H], peak[:], ALU.mult))
            link(dve.tensor_scalar(root[:], agg[:, :, D + H], 1.0, None, ALU.add))
            scalar_step(K.stat[:, 0, :], root[:], ACT.Sqrt)
            link(dve.reciprocal(root[:], K.stat[:, 0, :]))

        on_vector(nc, K, "f1b", divide)
        node_pass(nc, K, "n1m", y, [(K.w("mlp1"), D, K.v("b_mlp1"), tmp)])

        def gelu(dve, link, scalar_step):
            scalar_step(y[:], tmp[:], ACT.Gelu_apprx_tanh)

        on_vector(nc, K, "f1c", gelu)
        node_pass(nc, K, "n1n", y, [(K.w("mlp2"), D, K.v("b_mlp2"), tmp)])

        def finish(dve, link, scalar_step):
            link(dve.tensor_tensor(x[:], x[:], tmp[:], ALU.add))
            layer_norm(dve, link, scalar_step, K, x[:], y[:])

        on_vector(nc, K, "f1d", finish)



def edge_pass2(nc, K, i_layer, agg):
    ctx = ExitStack()
    with ctx:
        sb, ps = ctx_tools(nc, ctx)
        ed = Edges(nc, K, "d")
        s = f"g{i_layer}"
        idx = sb(f"{s}_idx", [P, LANES, C], I32)
        far = sb(f"{s}_far", [P, LANES, C, D])
        S = sb(f"{s}_S", [P, 2, C, P])
        p_agg = ps(f"{s}_p_agg", [P, 2, C, D])
        new = Sems(nc, K.used_sems, s)
        picked, gate = new("picked", "gate")
        far_in = new("far_in0", "far_in1", "far_in2", "far_in3")
        hot, summed, added = new("hot", "summed", "added")
        block = ctx.enter_context(nc.Block())

        @block.gpsimd
        def _(pool):
            def body(it):
                for lane in range(LANES):
                    if (at := at_stage(it, lane, 0)) is not None:
                        c, l = at
                        pool.wait_ge(picked, c + 1)
                        if over0(c - LANES + 1):
                            pool.wait_ge(summed, c - LANES + 1)
                        pool.sem_inc(gate, 1)
                        for i in range(C):
                            pool.indirect_dma_start(far[:, l, i, :], None, K.table2[i_layer],
                                                    bass.IndirectOffsetOnAxis(ap=idx[:, l, i:i + 1], axis=0)
                                                    ).then_inc(far_in[l], 16)

            chunk_loop(pool, body)

        @block.scalar
        def _(act):
            def body(it):
                for lane in range(LANES):
                    if (at := at_stage(it, lane, 0)) is not None:
                        c, l = at
                        if over0(c - LANES + 1):
                            act.wait_ge(far_in[l], 64 * (lane_turn(it, lane, 0) - 1))
                        ed.pick_others(act, idx[:, l, :], c).then_inc(picked, 1)

            chunk_loop(act, body)

        @block.tensor
        def _(pe):
            def body(it):
                for lane in range(LANES):
                    if (at := at_stage(it, lane, 2)) is not None:
                        c, l = at
                        pe.wait_ge(hot, c + 1)
                        pe.wait_ge(far_in[l], 64 * lane_turn(it, lane, 2))
                        if over0(C * (c - 1)):
                            pe.wait_ge(added, C * (c - 1))
                        for i in range(C):
                            mm = pe.matmul(p_agg[:, l % 2, i, :], S[:, l % 2, i, :], far[:, l, i, :],
                                           start=True, stop=True)
                        mm.then_inc(summed, 1)

            chunk_loop(pe, body)

        @block.vector
        def _(dve):
            regs = [dve.alloc_register(f"{s}_dve{i}") for i in range(C)]

            def body(it):
                for lane in range(LANES):
                    if (at := at_stage(it, lane, 1)) is not None:
                        c, l = at
                        if over0(c - 1):
                            dve.wait_ge(summed, c - 1)
                        ed.one_hot(dve, S[:, l % 2], c).then_inc(hot, 1)
                    if (at := at_stage(it, lane, 2)) is not None:
                        c, l = at
                        add_to_blocks(dve, ed, regs, c, agg, p_agg[:, l % 2], D, summed, added)

            chunk_loop(dve, body)


def layer2(nc, K, x, root):
    with ExitStack() as ctx:
        sb, _ = ctx_tools(nc, ctx)
        h, agg = sb("h2", [P, B, D]), sb("agg2", [P, B, D])
        nodes = x
        for i in range(3):
            node_pass(nc, K, f"n2{i}", nodes, [(K.w(f"g{i}"), D, root, (agg, K.table2[i]))])
            edge_pass2(nc, K, i, agg)

            def finish(dve, link, scalar_step, i=i):
                link(dve.tensor_tensor(h[:], agg[:], bc_last(root[:], D), ALU.mult))
                link(dve.tensor_tensor(h[:], h[:], bc_mid(K.v(f"b_g{i}"), B), ALU.add))
                if i < 2:
                    link(dve.tensor_scalar(h[:], h[:], 0.0, None, ALU.max))
                else:
                    link(dve.tensor_tensor(x[:], x[:], h[:], ALU.add))
                    layer_norm(dve, link, scalar_step, K, x[:], h[:])

            on_vector(nc, K, f"f2{i}b", finish)
            nodes = h



def edge_pass3a(nc, K, q, logit):
    ctx = ExitStack()
    with ctx:
        sb, ps = ctx_tools(nc, ctx)
        ed = Edges(nc, K, "s")
        idx = sb("l3_idx", [P, LANES, C], I32)
        rows = sb("l3_rows", [P, LANES, C * P], BF16)
        lens = sb("l3_lens", [P, LANES, C * P])
        far = sb("l3_far", [P, LANES, C, 2 * D])
        ST = sb("l3_ST", [P, 2, C * P])
        hid = sb("l3_hid", [P, 2, C * P])
        prod = sb("l3_prod", [P, 2, C, D])
        dot = sb("l3_dot", [P, 2, C, H])
        bias = sb("l3_bias", [P, 2, C, H])
        p_q = ps("l3_p_q", [P, 2, C, D])
        p_bias = ps("l3_p_bias", [P, 2, C, P])
        new = Sems(nc, K.used_sems, "l3")
        picked, gate = new("picked", "gate")
        far_in = new("far_in0", "far_in1", "far_in2", "far_in3")
        spilled = new("spilled0", "spilled1", "spilled2", "spilled3")
        rows_in = new("row_in0", "row_in1", "row_in2", "row_in3")
        turned_hot, q_done, hid_out, biased, multiplied, steps = new(
            "turned_hot", "q_done", "hid_out", "biased", "multiplied", "steps")
        block = ctx.enter_context(nc.Block())

        @block.gpsimd
        def _(pool):
            def body(it):
                for lane in range(LANES):
                    if (at := at_stage(it, lane, 0)) is not None:
                        c, l = at
                        pool.wait_ge(picked, c + 1)
                        if over0(c - LANES + 1):
                            pool.wait_ge(multiplied, c - LANES + 1)
                            pool.wait_ge(spilled[l], 16 * (lane_turn(it, lane, 0) - 1))
                        pool.sem_inc(gate, 1)
                        for i in range(C):
                            pool.indirect_dma_start(far[:, l, i, :], None, K.table3,
                                                    bass.IndirectOffsetOnAxis(ap=idx[:, l, i:i + 1], axis=0)
                                                    ).then_inc(far_in[l], 16)

            chunk_loop(pool, body)

        @block.sync
        def _(sp):
            chunks = K.spill3.rearrange("(c e t) w -> e c t w", t=C, e=P)

            def body(it):
                for lane in range(LANES):
                    if (at := at_stage(it, lane, 0)) is not None:
                        c, l = at
                        if over0(c - LANES + 1):
                            sp.wait_ge(turned_hot, c - LANES + 1)
                            sp.wait_ge(hid_out, c - LANES + 1)
                        ed.load_rows(sp, rows[:, l, :], c).then_inc(rows_in[l], 16)
                        lengths = K.len_rows.rearrange("t e -> (t e)")[bass.ds(c * (C * P), C * P)]
                        sp.dma_start(lens[:, l, :], lengths.unsqueeze(0).to_broadcast([P, C * P])
                                     ).then_inc(rows_in[l], 16)
                    if (at := at_stage(it, lane, 2)) is not None:
                        c, l = at
                        sp.wait_ge(far_in[l], 64 * lane_turn(it, lane, 2))
                        sp.dma_start(chunks[:, bass.ds(c, 1), :, :], far[:, l:l + 1, :, D:2 * D]).then_inc(spilled[l], 16)

            chunk_loop(sp, body)
            for l in range(LANES):
                sp.wait_ge(spilled[l], 16 * ITERS)

        @block.scalar
        def _(act):
            def body(it):
                for lane in range(LANES):
                    if (at := at_stage(it, lane, 0)) is not None:
                        c, l = at
                        if over0(c - LANES + 1):
                            act.wait_ge(far_in[l], 64 * (lane_turn(it, lane, 0) - 1))
                        ed.pick_others(act, idx[:, l, :], c).then_inc(picked, 1)
                    if (at := at_stage(it, lane, 2)) is not None:
                        c, l = at
                        act.wait_ge(rows_in[l], 32 * lane_turn(it, lane, 2))
                        if over0(c - 1):
                            act.wait_ge(biased, c - 1)
                        nc.scalar.activation(hid[:, l % 2, :], lens[:, l, :], ACT.Silu, scale=K.w("hid_w"),
                                             bias=K.w("hid_b")).then_inc(hid_out, 1)

            chunk_loop(act, body)

        @block.tensor
        def _(pe):
            regs = [pe.alloc_register(f"l3_pe{i}") for i in range(C)]

            def body(it):
                for lane in range(LANES):
                    if (at := at_stage(it, lane, 3)) is not None:
                        c, l = at
                        blocks = ed.block_values(pe, regs, c)
                        pe.wait_ge(turned_hot, c + 1)
                        if over0(c - 1):
                            pe.wait_ge(multiplied, c - 1)
                        for i in range(C):
                            mm = pe.matmul(p_q[:, l % 2, i, :], ST[:, l % 2, i * P:(i + 1) * P],
                                           q[:, bass.ds(blocks[i], 1), :], start=True, stop=True)
                        mm.then_inc(q_done, 1)
                    if (at := at_stage(it, lane, 4)) is not None:
                        c, l = at
                        pe.wait_ge(hid_out, c + 1)
                        if over0(c - 1):
                            pe.wait_ge(steps, 3 * (c - 1))
                        for i in range(C):
                            mm = pe.matmul(p_bias[:, l % 2, i, 0:H], hid[:, l % 2, i * P:(i + 1) * P], K.w("bias3"),
                                           start=True, stop=True)
                        mm.then_inc(biased, 1)

            chunk_loop(pe, body)

        @block.vector
        def _(dve):
            def body(it):
                for lane in range(LANES):
                    if (at := at_stage(it, lane, 2)) is not None:
                        c, l = at
                        dve.wait_ge(rows_in[l], 32 * lane_turn(it, lane, 2))
                        if over0(c - 1):
                            dve.wait_ge(q_done, c - 1)
                        ed.hot_nodes(dve, ST[:, l % 2, :], rows[:, l, :]).then_inc(turned_hot, 1)
                    if (at := at_stage(it, lane, 4)) is not None:
                        c, l = at
                        h = l % 2
                        dve.wait_ge(q_done, c + 1)
                        dve.wait_ge(far_in[l], 64 * lane_turn(it, lane, 4))
                        dve.tensor_tensor(prod[:, h], p_q[:, h], far[:, l, :, 0:D], ALU.mult).then_inc(multiplied, 1)
                        dve.wait_ge(multiplied, c + 1)
                        dve.tensor_reduce(dot[:, h], prod[:, h].rearrange("p t (h d) -> p t h d", h=H), AX.X, ALU.add
                                          ).then_inc(steps, 1)
                        dve.wait_ge(biased, c + 1)
                        dve.tensor_tensor(bias[:, h], p_bias[:, h, :, 0:H], bc_mid(K.v("b_bias3"), C), ALU.add
                                          ).then_inc(steps, 1)
                        dve.wait_ge(steps, 3 * c + 2)
                        dve.scalar_tensor_tensor(out=logit[:, bass.ds(c * C, C), :], in0=dot[:, h], scalar=HD ** -0.5,
                                                 in1=bias[:, h], op0=ALU.mult, op1=ALU.add).then_inc(steps, 1)

            chunk_loop(dve, body)


def cut_and_exp(nc, K, logit):
    with ExitStack() as ctx:
        sb, ps = ctx_tools(nc, ctx)
        cut, turn, real = sb("cut", [P, T]), sb("turn", [P, T]), sb("real", [P, T])
        most, row, diag = sb("most", [P, H]), sb("row", [H, 1]), sb("diag", [H, H])
        every = sb("every", [P, H])
        p_row, p_all = ps("p_row", [H, P]), ps("p_all", [P, H])
        new = Sems(nc, K.used_sems, "cut")
        chain, turned, asked, answered, ready, crossed = new("chain", "turned", "asked", "answered", "ready", "crossed")
        block = ctx.enter_context(nc.Block())

        @block.vector
        def _(dve):
            count = [0]

            def link(ins):
                count[0] += 1
                ins.then_inc(chain, 1)
                dve.wait_ge(chain, count[0])

            link(dve.tensor_scalar(turn[:], K.length[:], 0.5 / CUTOFF, None, ALU.mult))
            link(dve.tensor_scalar(turn[:], turn[:], 12582912.0, 12582912.0, ALU.add, ALU.subtract))
            link(dve.scalar_tensor_tensor(out=turn[:], in0=turn[:], scalar=-2.0 * CUTOFF, in1=K.length[:],
                                          op0=ALU.mult, op1=ALU.add))
            link(dve.tensor_scalar(cut[:], turn[:], -1.0, None, ALU.mult))
            link(dve.tensor_tensor(turn[:], turn[:], cut[:], ALU.max))
            link(dve.tensor_scalar(turn[:], turn[:], -np.pi / CUTOFF, np.pi / 2, ALU.mult, ALU.add))
            link(dve.tensor_scalar(turn[:], turn[:], -np.pi / 2, np.pi / 2, ALU.max, ALU.min))
            dve.sem_inc(asked, 1)
            dve.wait_ge(answered, 1)
            link(dve.tensor_scalar(cut[:], cut[:], 1.0, 0.5, ALU.add, ALU.mult))
            link(dve.tensor_scalar(turn[:], K.length[:], CUTOFF, None, ALU.is_lt))
            link(dve.tensor_tensor(cut[:], cut[:], turn[:], ALU.mult))
            link(dve.tensor_tensor(logit[:], logit[:], bc_last(cut[:], H), ALU.mult))
            link(dve.tensor_scalar(real[:], K.key["s"][:], 0.0, None, ALU.is_ge))
            link(dve.tensor_scalar(turn[:], real[:], -1.0, 3.0e38, ALU.add, ALU.mult))
            link(dve.tensor_tensor(logit[:], logit[:], bc_last(real[:], H), ALU.mult))
            link(dve.tensor_tensor(logit[:], logit[:], bc_last(turn[:], H), ALU.add))
            link(dve.tensor_reduce(most[:], logit[:].rearrange("p t h -> p h t"), AX.X, ALU.max))
            dve.sem_inc(ready, 1)
            dve.wait_ge(crossed, 1)
            link(dve.tensor_reduce(row[:], p_row[:], AX.X, ALU.max))
            link(dve.tensor_scalar(diag[:], K.ident[0:H, 0:H], row[:, 0:1], None, ALU.mult))
            dve.sem_inc(ready, 1)
            dve.wait_ge(crossed, 2)
            link(dve.tensor_copy(every[:], p_all[:]))
            link(dve.tensor_tensor(logit[:], logit[:], bc_mid(every[:], T), ALU.subtract))
            dve.sem_inc(asked, 1)
            dve.wait_ge(answered, 2)

        @block.tensor
        def _(pe):
            pe.wait_ge(ready, 1)
            pe.transpose(p_row[:], most[:], K.ident[:]).then_inc(crossed, 1)
            pe.wait_ge(ready, 2)
            pe.matmul(p_all[:], K.ones[0:H, :], diag[:], start=True, stop=True).then_inc(crossed, 1)

        @block.scalar
        def _(act):
            act.wait_ge(asked, 1)
            nc.scalar.activation(cut[:], turn[:], ACT.Sin).then_inc(answered, 1)
            act.wait_ge(asked, 2)
            nc.scalar.activation(logit[:], logit[:], ACT.Exp).then_inc(answered, 1)


def edge_pass3b(nc, K, weight, agg):
    ctx = ExitStack()
    with ctx:
        sb, ps = ctx_tools(nc, ctx)
        ed = Edges(nc, K, "s")
        M = D + H
        far = sb("v3_far", [P, LANES, C, D])
        S = sb("v3_S", [P, 2, C, P])
        msg = sb("v3_msg", [P, 2, C, M])
        sums = sb("v3_sums", [P, 2, C, M])
        p_agg = ps("v3_p_agg", [P, 2, C, 2 * P])
        new = Sems(nc, K.used_sems, "v3")
        far_in = new("far_in0", "far_in1", "far_in2", "far_in3")
        hot, weights_in, msg_done, summed, added, agg_clear = new(
            "hot", "weights_in", "msg_done", "summed", "added", "agg_clear")
        [sums_out] = new("sums_out")
        block = ctx.enter_context(nc.Block())

        @block.sync
        def _(sp):
            chunks = K.spill3.rearrange("(c e t) w -> e c t w", t=C, e=P)

            def body(it):
                for lane in range(LANES):
                    if (at := at_stage(it, lane, 0)) is not None:
                        c, l = at
                        if over0(c - LANES + 1):
                            sp.wait_ge(msg_done, c - LANES + 1)
                        sp.dma_start(far[:, l:l + 1, :, :], chunks[:, bass.ds(c, 1), :, :]).then_inc(far_in[l], 16)

            chunk_loop(sp, body)

        @block.scalar
        def _(act):
            def body(it):
                for lane in range(LANES):
                    if (at := at_stage(it, lane, 2)) is not None:
                        c, l = at
                        if over0(c - 1):
                            act.wait_ge(summed, c - 1)
                        nc.scalar.activation(msg[:, l % 2, :, D:M], weight[:, bass.ds(c * C, C), :], ACT.Copy
                                             ).then_inc(weights_in, 1)
                    if (at := at_stage(it, lane, 3)) is not None:
                        c, l = at
                        act.wait_ge(summed, c + 1)
                        if over0(C * (c - 1)):
                            act.wait_ge(added, C * (c - 1))
                        nc.scalar.activation(sums[:, l % 2], p_agg[:, l % 2, :, 0:M], ACT.Copy).then_inc(sums_out, 1)

            chunk_loop(act, body)

        @block.tensor
        def _(pe):
            def body(it):
                for lane in range(LANES):
                    if (at := at_stage(it, lane, 2)) is not None:
                        c, l = at
                        pe.wait_ge(hot, c + 1)
                        pe.wait_ge(msg_done, c + 1)
                        if over0(c - 1):
                            pe.wait_ge(sums_out, c - 1)
                        for i in range(C):
                            mm = pe.matmul(p_agg[:, l % 2, i, 0:M], S[:, l % 2, i, :], msg[:, l % 2, i, :],
                                           start=True, stop=True)
                        mm.then_inc(summed, 1)

            chunk_loop(pe, body)

        @block.vector
        def _(dve):
            def body(it):
                for lane in range(LANES):
                    if (at := at_stage(it, lane, 2)) is not None:
                        c, l = at
                        h = l % 2
                        if over0(c - 1):
                            dve.wait_ge(summed, c - 1)
                        ed.one_hot(dve, S[:, h], c).then_inc(hot, 1)
                        dve.wait_ge(weights_in, c + 1)
                        dve.wait_ge(far_in[l], 16 * lane_turn(it, lane, 2))
                        dve.tensor_tensor(msg[:, h, :, 0:D].rearrange("p t (h d) -> p t h d", h=H),
                                          far[:, l, :, :].rearrange("p t (h d) -> p t h d", h=H),
                                          bc_last(msg[:, h, :, D:M], HD), ALU.mult).then_inc(msg_done, 1)

            chunk_loop(dve, body)

        @block.gpsimd
        def _(pool):
            regs = [pool.alloc_register(f"v3_pool{i}") for i in range(C)]
            for sums_of in agg:
                pool.memset(sums_of[:], 0.0).then_inc(agg_clear, 1)
            pool.wait_ge(agg_clear, 2)

            def body(it):
                for lane in range(LANES):
                    if (at := at_stage(it, lane, 3)) is not None:
                        c, l = at
                        add_to_pair(pool, ed, regs, c, agg, sums[:, l % 2], sums_out, added)

            chunk_loop(pool, body)


def layer3(nc, K, x):
    with ExitStack() as ctx:
        sb, _ = ctx_tools(nc, ctx)
        logit = sb("logit3", [P, T, H])
        with ExitStack() as inner:
            q = inner.enter_context(nc.sbuf_tensor("q3", [P, B, D], F32))
            node_pass(nc, K, "n3", x, [(K.w("q3"), D, K.v("b_q3"), q),
                                            (K.w("kv3"), 2 * D, K.v("b_kv3"), (K.table3, 0, 2 * D))])
            edge_pass3a(nc, K, q, logit)
        cut_and_exp(nc, K, logit)
        agg = sb("agg3", [P, B, D + H])
        with ExitStack() as inner:
            odd = inner.enter_context(nc.sbuf_tensor("agg3_odd", [P, B, D + H], F32))
            edge_pass3b(nc, K, logit, (agg, odd))
            on_vector(nc, K, "f3o", lambda dve, link, scalar_step:
                      link(dve.tensor_tensor(agg[:], agg[:], odd[:], ALU.add)))
        y, tmp = sb("y3", [P, B, D]), sb("tmp3", [P, B, D])

        def divide(dve, link, scalar_step):
            link(dve.tensor_scalar(tmp[:, :, 0:H], agg[:, :, D:D + H], 1e-8, None, ALU.add))
            link(dve.reciprocal(tmp[:, :, 0:H], tmp[:, :, 0:H]))
            for h in range(H):
                link(dve.tensor_tensor(y[:, :, h * HD:(h + 1) * HD], agg[:, :, h * HD:(h + 1) * HD],
                                       bc_last(tmp[:, :, h], HD), ALU.mult))

        on_vector(nc, K, "f3a", divide)
        node_pass(nc, K, "n3o", y, [(K.w("o3"), D, K.v("b_o3"), tmp)])

        def finish(dve, link, scalar_step):
            link(dve.tensor_tensor(tmp[:], tmp[:], x[:], ALU.add))
            layer_norm(dve, link, scalar_step, K, tmp[:], y[:], K.v("ln_g"), K.v("ln_b"))
            link(dve.tensor_tensor(x[:], x[:], tmp[:], ALU.add))
            layer_norm(dve, link, scalar_step, K, x[:], y[:])

        on_vector(nc, K, "f3b", finish)


def layers(nc, top, K, io):
    x = top.enter_context(nc.sbuf_tensor("x", [P, B, D], F32))
    root = top.enter_context(nc.sbuf_tensor("root", [P, B], F32))
    with ExitStack() as inner:
        late = Late(nc, inner)
        load_and_sort(nc, K, io, late, x)
        scatter_by_destination(nc, K, late)
    load_order(nc, K, "s")
    load_order(nc, K, "d")
    sort_in_tiles(nc, K)
    layer0(nc, K, x)
    layer1(nc, K, x, root)
    layer2(nc, K, x, root)
    layer3(nc, K, x)
    [stored] = Sems(nc, K.used_sems, "end")("stored")
    with nc.Block() as block:
        @block.sync
        def _(sp):
            sp.dma_start(io["out"], x[:].rearrange("p b d -> p (b d)")).then_inc(stored, 16)
            sp.wait_ge(stored, 16)




class Late:

    def __init__(self, nc, ctx):
        self.pos = ctx.enter_context(nc.sbuf_tensor("late_pos", [P, T], I32))
        self.rec = ctx.enter_context(nc.sbuf_tensor("late_rec", [P, T, REC_D], I32))


class Kept:

    def __init__(self, nc, ctx):
        def sb(name, shape, dt=F32):
            return ctx.enter_context(nc.sbuf_tensor(name, shape, dt))

        self.used_sems = []
        self.W, self.V = sb("weights", [P, NW]), sb("vectors", [P, NV])
        self.w_ef_parts = sb("w_ef_parts", [P, 2, 2 * D], BF16)
        self.ident_bf = sb("ident_bf", [P, P], BF16)
        self.col = sb("col", [P, 1])
        self.block_start = sb("block_start", [P, G])
        self.disorder = sb("disorder", [P, 1], I32)
        self.lane = sb("lane", [P, P])
        self.ident, self.ones = sb("ident", [P, P]), sb("ones", [P, P])
        self.key = {k: sb(f"key_{k}", [P, T]) for k in "sd"}
        self.other = {k: sb(f"other_{k}", [P, T], I32) for k in "sd"}
        self.blocks = {k: sb(f"blocks_{k}", [1, T], I32) for k in "sd"}
        self.length = sb("len_sorted", [P, T])
        self.stat = sb("stat", [P, 2, B])
        self.rec_s = nc.dram_tensor("rec_s", [T * P, REC_S], F32).ap()
        self.rec_d = nc.dram_tensor("rec_d", [T * P, REC_D], I32).ap()
        self.starts_dram = nc.dram_tensor("dram_starts", [P * G], I32).ap()
        self.key_rows = {k: nc.dram_tensor(f"dram_key_rows_{k}", [T, P], BF16).ap() for k in "sd"}
        self.len_rows = nc.dram_tensor("dram_len_rows", [T, P], F32).ap()
        self.map_dram = {k: nc.dram_tensor(f"map_{k}", [P * G], I32).ap() for k in "sd"}
        self.table0 = nc.dram_tensor("table0", [NP, 2 * D], F32).ap()
        self.table1 = nc.dram_tensor("table1", [NP, D + H], F32).ap()
        self.table2 = [nc.dram_tensor(f"table2_{i}", [NP, D], F32).ap() for i in range(3)]
        self.table3 = nc.dram_tensor("table3", [NP, 2 * D], F32).ap()
        self.spill1 = nc.dram_tensor("spill1", [T * P, D + H], F32).ap()
        self.spill3 = nc.dram_tensor("spill3", [T * P, D], F32).ap()

    def w(self, name):
        a, b = W_COLS[name]
        return self.W[:, a:b]

    def v(self, name):
        a, b = V_COLS[name]
        return self.V[:, a:b]


IO = {"x": ([P, B * D], F32), "src": ([P, COLS], I32), "dst": ([P * COLS + P], I32),
      "ends": ([REC_D * (P * COLS + P)], I32), "ef": ([P, COLS * EF], F32),
      "length": ([P, COLS], F32), "weights": ([P, NW], F32), "vectors": ([P, NV], F32),
      "w_ef": ([P, 2 * D], F32), "part": ([P, 5], F32)}


def build(nc, io):
    ctx = ExitStack()
    with ctx:
        K = Kept(nc, ctx)
        layers(nc, ctx, K, io)


def lay_out(a):
    a = {k: np.asarray(v) for k, v in a.items()}

    def padded(v, rows, fill=0):
        out = np.full((rows, *v.shape[1:]), fill, v.dtype)
        out[:len(v)] = v
        return out

    out = {"x": padded(a["x"], NP).reshape(B, P, D).transpose(1, 0, 2).reshape(P, B * D)}
    out["src"] = padded(a["src"], P * COLS, NP).reshape(P, COLS)
    out["dst"] = padded(a["dst"], P * COLS + P, NP)
    out["ends"] = padded(np.stack([a["dst"], a["src"]], 1), P * COLS + P, NP).reshape(-1)
    out["ef"] = padded(a["edge_attr_10"], P * COLS).reshape(P, COLS * EF)
    out["length"] = padded(a["edge_weight1"], P * COLS).reshape(P, COLS)
    gate, cand = a["L0_gnn_gate_w"], a["L0_gnn_cand_w"]
    both = np.concatenate([gate, cand], 1)
    W = np.zeros((P, NW), np.float32)
    for name, w in (("own0", both[0:D]), ("other0", both[D:2 * D]), ("in1", a["L1_gnn_w_in"]),
                    ("a1", np.concatenate([a["L1_gnn_w_au"], a["L1_gnn_w_av"]], 1)),
                    ("mlp1", a["L1_gnn_w1"]), ("mlp2", a["L1_gnn_w2"]),
                    ("g0", a["L2_gnn_W0"]), ("g1", a["L2_gnn_W1"]), ("g2", a["L2_gnn_W2"]),
                    ("q3", a["L3_gnn_Wq"].T), ("kv3", np.concatenate([a["L3_gnn_Wk"].T, a["L3_gnn_Wv"].T], 1)),
                    ("bias3", a["L3_gnn_We2"].T), ("o3", a["L3_gnn_Wo"].T), ("hid_w", a["L3_gnn_We1"]), ("hid_b", a["L3_gnn_be1"][:, None])):
        lo, hi = W_COLS[name]
        W[:, lo:hi] = w
    V = np.zeros((P, NV), np.float32)
    zeros = np.zeros(H, np.float32)
    for name, v in (("b0", np.concatenate([a["L0_gnn_gate_b"], a["L0_gnn_cand_b"]])), ("b_in1", a["L1_gnn_b_in"]),
                    ("b_a1", np.concatenate([a["L1_gnn_b_au"], zeros])), ("b_mlp1", a["L1_gnn_b1"]),
                    ("b_mlp2", a["L1_gnn_b2"]), ("b_g0", a["L2_gnn_b0"]), ("b_g1", a["L2_gnn_b1"]),
                    ("b_g2", a["L2_gnn_b2"]), ("b_q3", a["L3_gnn_bq"]),
                    ("b_kv3", np.concatenate([a["L3_gnn_bk"], a["L3_gnn_bv"]])), ("b_bias3", a["L3_gnn_be2"]),
                    ("b_o3", a["L3_gnn_bo"]), ("bn_g", a["L0_gnn_bn_gamma"]), ("bn_b", a["L0_gnn_bn_beta"]),
                    ("ln_g", a["L3_gnn_ln_g"]), ("ln_b", a["L3_gnn_ln_b"])):
        lo, hi = V_COLS[name]
        V[:, lo:hi] = v[None, :]
    out["weights"], out["vectors"] = W, V
    w_ef, part = np.zeros((P, 2 * D), np.float32), np.zeros((P, 5), np.float32)
    for half in range(P // PARTS):
        part[half * PARTS:(half + 1) * PARTS, 3 + half] = 1
        for j, which in enumerate(WEIGHT_PARTS):
            at = half * PARTS + j * EF
            w_ef[at:at + EF] = both[2 * D:]
            part[at:at + EF, which] = 1
    out["w_ef"], out["part"] = w_ef, part
    return {k: np.ascontiguousarray(v) for k, v in out.items()}


def kernel(**inputs):
    import concourse.bacc as bacc
    from concourse.bass_utils import run_bass_kernel_spmd

    nc = bacc.Bacc("TRN2", target_bir_lowering=False, num_devices=1)
    arrays = {f"in_{k}": v for k, v in lay_out(inputs).items()}
    io = {k: nc.dram_tensor(f"in_{k}", shape, dt, kind="ExternalInput").ap() for k, (shape, dt) in IO.items()}
    io["out"] = nc.dram_tensor("out", [P, B * D], F32, kind="ExternalOutput").ap()
    build(nc, io)
    got = run_bass_kernel_spmd(nc, [arrays], core_ids=[0]).results[0]["out"]
    return np.ascontiguousarray(got.reshape(P, B, D).transpose(1, 0, 2).reshape(NP, D)[:N])
```
